# Optimizing a Trainium2 kernel written in Bass

```python
import numpy as np
import jax
import jax.numpy as jnp

def _softmax(x, axis=-1):
    return jax.nn.softmax(x, axis=axis)

def _gelu(x):
    return jax.nn.gelu(x, approximate=True)

def _silu(x):
    return jax.nn.silu(x)

def _sigmoid(x):
    return jax.nn.sigmoid(x)

def _layernorm(x, axis=-1, eps=1e-05):
    m = jnp.mean(x, axis=axis, keepdims=True)
    v = jnp.var(x, axis=axis, keepdims=True)
    return (x - m) / jnp.sqrt(v + eps)

def _scatter_add(tgt, idx, src, axis=0):
    return tgt.at[idx].add(src)

def _segment_sum(src, seg, n):
    return jax.ops.segment_sum(src, seg, n)
kernel_name = 'mk_gnn_resnorm_d4_gnn_r64_81519c'

def setup_inputs(seed: int=0):
    np.random.seed(seed)
    _w = jnp.asarray

    def _rec_inputs():
        import jax
        import jax.numpy as jnp
        _gk = jax.random.key(seed)
        x = -0.0008691 + 1 * jax.random.normal(jax.random.fold_in(_gk, 1), (100000, 128), jnp.float32)
        src = jax.random.randint(jax.random.fold_in(_gk, 2), (25000,), 0, 100000, jnp.int32)
        dst = jax.random.randint(jax.random.fold_in(_gk, 3), (25000,), 0, 100000, jnp.int32)
        _o = jnp.argsort(dst, stable=True)
        src = src[_o]
        dst = dst[_o]
        edge_attr_16 = 0.000254156 + 0.999948 * jax.random.normal(jax.random.fold_in(_gk, 11), (25000, 16), jnp.float32)
        edge_attr_64 = -5.16925e-05 + 1.00005 * jax.random.normal(jax.random.fold_in(_gk, 12), (25000, 64), jnp.float32)
        return (x, src, dst, edge_attr_16, edge_attr_64)
    x, src, dst, edge_attr_16, edge_attr_64 = _rec_inputs()

    def _L0_gnn_setup():
        import jax, jax.numpy as jnp
        import numpy as np
        N_NODES = 10000
        N_EDGES = 10000
        IN_CH = 128
        OUT_CH = 128
        key = jax.random.key(seed)
        k1, k2, k3, k4 = jax.random.split(key, 4)
        x = jax.random.normal(k1, (N_NODES, IN_CH), dtype=jnp.float32)
        edge_index = jax.random.randint(k2, (2, N_EDGES), 0, N_NODES, dtype=jnp.int64)
        bound = 1.0 / np.sqrt(2 * IN_CH)
        W = jax.random.uniform(k3, (OUT_CH, 2 * IN_CH), dtype=jnp.float32, minval=-bound, maxval=bound)
        b = jax.random.uniform(k4, (OUT_CH,), dtype=jnp.float32, minval=-bound, maxval=bound)
        return {'x': x, 'W': W, 'b': b, 'edge_index': edge_index}
    _L0_gnn_all = _L0_gnn_setup()
    _L0_gnn_in = {k: v for k, v in _L0_gnn_all.items() if k in ('W', 'b')}
    del _L0_gnn_all

    def _L1_gnn_setup():
        import jax, jax.numpy as jnp
        import numpy as np
        NEG_SLOPE_ATT = 0.2
        NEG_SLOPE_OUT = 0.01
        key = jax.random.key(seed)
        ks = jax.random.split(key, 6)
        N, E, D_IN, D_OUT, D_EDGE = (50000, 12500, 128, 128, 16)
        s = 1.0 / np.sqrt(D_IN)
        return {'x': jax.random.normal(ks[0], (N, D_IN), jnp.float32), 'edge_index': jax.random.randint(ks[1], (2, E), 0, N, jnp.int64), 'edge_attr': jax.random.normal(ks[2], (E, D_EDGE), jnp.float32), 'Wl': jax.random.normal(ks[3], (D_IN, D_OUT), jnp.float32) * s, 'bl': jnp.zeros((D_OUT,), jnp.float32), 'Wr': jax.random.normal(ks[4], (D_IN, D_OUT), jnp.float32) * s, 'br': jnp.zeros((D_OUT,), jnp.float32), 'att': jax.random.normal(ks[5], (D_OUT,), jnp.float32) * s, 'bias': jnp.zeros((D_OUT,), jnp.float32)}
    _L1_gnn_all = _L1_gnn_setup()
    _L1_gnn_in = {k: v for k, v in _L1_gnn_all.items() if k in ('Wl', 'bl', 'Wr', 'br', 'att', 'bias')}
    del _L1_gnn_all

    def _L2_gnn_setup():
        import jax, jax.numpy as jnp
        import numpy as np
        N_NODES = 100000
        IN_DIM = 128
        HIDDEN = 64
        N_EDGES = 25000
        key = jax.random.key(seed)
        ks = jax.random.split(key, 9)
        x = jax.random.normal(ks[0], (N_NODES, IN_DIM), dtype=jnp.float32)
        edge_index = jax.random.randint(ks[1], (2, N_EDGES), 0, N_NODES, dtype=jnp.int64)
        s = 1.0 / np.sqrt(IN_DIM)
        sh = 1.0 / np.sqrt(HIDDEN)
        W_sim = jax.random.uniform(ks[2], (IN_DIM, HIDDEN), jnp.float32, -s, s)
        b_sim = jax.random.uniform(ks[3], (HIDDEN,), jnp.float32, -s, s)
        w_vec = jax.random.uniform(ks[4], (HIDDEN, 1), jnp.float32, -sh, sh)
        b_vec = jax.random.uniform(ks[5], (1,), jnp.float32, -sh, sh)
        W1 = jax.random.uniform(ks[6], (IN_DIM, HIDDEN), jnp.float32, -s, s)
        b1 = jax.random.uniform(ks[7], (HIDDEN,), jnp.float32, -s, s)
        W2 = jax.random.uniform(ks[8], (HIDDEN, IN_DIM), jnp.float32, -sh, sh)
        b2 = jnp.zeros((IN_DIM,), dtype=jnp.float32)
        return {'x': x, 'edge_index': edge_index, 'W_sim': W_sim, 'b_sim': b_sim, 'w_vec': w_vec, 'b_vec': b_vec, 'W1': W1, 'b1': b1, 'W2': W2, 'b2': b2}
    _L2_gnn_all = _L2_gnn_setup()
    _L2_gnn_in = {k: v for k, v in _L2_gnn_all.items() if k in ('W_sim', 'b_sim', 'w_vec', 'b_vec', 'W1', 'b1', 'W2', 'b2')}
    del _L2_gnn_all

    def _L3_gnn_setup():
        import jax, jax.numpy as jnp
        import numpy as np
        N, E, H, ED, GD = (100000, 25000, 128, 64, 64)
        LN_EPS = 1e-05

        def _mlp(x, w1, b1, w2, b2):
            return jax.nn.relu(x @ w1 + b1) @ w2 + b2
        key = jax.random.key(seed)
        ks = jax.random.split(key, 16)
        s = lambda d: 1.0 / np.sqrt(d)
        return {'node_state': jax.random.normal(ks[0], (N, H), jnp.float32), 'edge_index': jax.random.randint(ks[1], (2, E), 0, N, jnp.int64), 'edge_state': jax.random.normal(ks[2], (E, ED), jnp.float32), 'global_state': jax.random.normal(ks[3], (GD,), jnp.float32), 'msg_w1': jax.random.normal(ks[4], (H + ED + GD, H), jnp.float32) * s(H + ED + GD), 'msg_b1': jnp.zeros((H,), jnp.float32), 'msg_w2': jax.random.normal(ks[5], (H, H), jnp.float32) * s(H), 'msg_b2': jnp.zeros((H,), jnp.float32), 'upd_w1': jax.random.normal(ks[6], (2 * H + GD, H), jnp.float32) * s(2 * H + GD), 'upd_b1': jnp.zeros((H,), jnp.float32), 'upd_w2': jax.random.normal(ks[7], (H, H), jnp.float32) * s(H), 'upd_b2': jnp.zeros((H,), jnp.float32), 'ln_gamma': jnp.ones((H,), jnp.float32), 'ln_beta': jnp.zeros((H,), jnp.float32)}
    _L3_gnn_all = _L3_gnn_setup()
    _L3_gnn_in = {k: v for k, v in _L3_gnn_all.items() if k in ('global_state', 'msg_w1', 'msg_b1', 'msg_w2', 'msg_b2', 'upd_w1', 'upd_b1', 'upd_w2', 'upd_b2', 'ln_gamma', 'ln_beta')}
    del _L3_gnn_all
    return {'x': x, 'src': src, 'dst': dst, 'edge_attr_16': edge_attr_16, 'edge_attr_64': edge_attr_64, 'L0_gnn_W': _L0_gnn_in['W'], 'L0_gnn_b': _L0_gnn_in['b'], 'L1_gnn_Wl': _L1_gnn_in['Wl'], 'L1_gnn_bl': _L1_gnn_in['bl'], 'L1_gnn_Wr': _L1_gnn_in['Wr'], 'L1_gnn_br': _L1_gnn_in['br'], 'L1_gnn_att': _L1_gnn_in['att'], 'L1_gnn_bias': _L1_gnn_in['bias'], 'L2_gnn_W_sim': _L2_gnn_in['W_sim'], 'L2_gnn_b_sim': _L2_gnn_in['b_sim'], 'L2_gnn_w_vec': _L2_gnn_in['w_vec'], 'L2_gnn_b_vec': _L2_gnn_in['b_vec'], 'L2_gnn_W1': _L2_gnn_in['W1'], 'L2_gnn_b1': _L2_gnn_in['b1'], 'L2_gnn_W2': _L2_gnn_in['W2'], 'L2_gnn_b2': _L2_gnn_in['b2'], 'L3_gnn_global_state': _L3_gnn_in['global_state'], 'L3_gnn_msg_w1': _L3_gnn_in['msg_w1'], 'L3_gnn_msg_b1': _L3_gnn_in['msg_b1'], 'L3_gnn_msg_w2': _L3_gnn_in['msg_w2'], 'L3_gnn_msg_b2': _L3_gnn_in['msg_b2'], 'L3_gnn_upd_w1': _L3_gnn_in['upd_w1'], 'L3_gnn_upd_b1': _L3_gnn_in['upd_b1'], 'L3_gnn_upd_w2': _L3_gnn_in['upd_w2'], 'L3_gnn_upd_b2': _L3_gnn_in['upd_b2'], 'L3_gnn_ln_gamma': _L3_gnn_in['ln_gamma'], 'L3_gnn_ln_beta': _L3_gnn_in['ln_beta']}

def reference(x, src, dst, edge_attr_16, edge_attr_64, L0_gnn_W, L0_gnn_b, L1_gnn_Wl, L1_gnn_bl, L1_gnn_Wr, L1_gnn_br, L1_gnn_att, L1_gnn_bias, L2_gnn_W_sim, L2_gnn_b_sim, L2_gnn_w_vec, L2_gnn_b_vec, L2_gnn_W1, L2_gnn_b1, L2_gnn_W2, L2_gnn_b2, L3_gnn_global_state, L3_gnn_msg_w1, L3_gnn_msg_b1, L3_gnn_msg_w2, L3_gnn_msg_b2, L3_gnn_upd_w1, L3_gnn_upd_b1, L3_gnn_upd_w2, L3_gnn_upd_b2, L3_gnn_ln_gamma, L3_gnn_ln_beta):
    import jax
    import jax.numpy as jnp

    def _L0_gnn_ref(x, W, b, edge_index):
        import jax, jax.numpy as jnp
        import numpy as np
        N_NODES = 10000
        N_EDGES = 10000
        IN_CH = 128
        OUT_CH = 128
        src, dst = (edge_index[0], edge_index[1])
        x_i = x[dst]
        x_j = x[src]
        feat = jnp.concatenate([x_i, x_j - x_i], axis=-1)
        msg = feat @ W.T + b
        out = jax.ops.segment_max(msg, dst, num_segments=x.shape[0])
        return jnp.where(jnp.isfinite(out), out, 0.0)

    def _L1_gnn_ref(x, edge_index, edge_attr, Wl, bl, Wr, br, att, bias):
        import jax, jax.numpy as jnp
        import numpy as np
        NEG_SLOPE_ATT = 0.2
        NEG_SLOPE_OUT = 0.01
        N = x.shape[0]
        loop = jnp.arange(N, dtype=edge_index.dtype)
        src = jnp.concatenate([edge_index[0], loop])
        dst = jnp.concatenate([edge_index[1], loop])
        x_l = x @ Wl + bl
        x_r = x @ Wr + br
        e = jax.nn.leaky_relu(x_l[src] + x_r[dst], NEG_SLOPE_ATT) @ att
        m = jax.ops.segment_max(e, dst, num_segments=N)
        p = jnp.exp(e - m[dst])
        z = jax.ops.segment_sum(p, dst, num_segments=N)
        alpha = p / z[dst]
        out = jax.ops.segment_sum(alpha[:, None] * x_l[src], dst, num_segments=N)
        out = out + bias
        return jax.nn.leaky_relu(out, NEG_SLOPE_OUT)

    def _L2_gnn_ref(x, edge_index, W_sim, b_sim, w_vec, b_vec, W1, b1, W2, b2):
        import jax, jax.numpy as jnp
        import numpy as np
        N_NODES = 100000
        IN_DIM = 128
        HIDDEN = 64
        N_EDGES = 25000
        h = jnp.tanh(x @ W_sim + b_sim)
        weights = jax.nn.sigmoid((h @ w_vec + b_vec)[:, 0])
        row, col = (edge_index[0], edge_index[1])
        msg = x[col] * weights[col][:, None]
        readout = jax.ops.segment_sum(msg, row, num_segments=x.shape[0])
        prompts = jax.nn.relu(readout @ W1 + b1) @ W2 + b2
        return x + prompts

    def _L3_gnn_ref(node_state, edge_index, edge_state, global_state, msg_w1, msg_b1, msg_w2, msg_b2, upd_w1, upd_b1, upd_w2, upd_b2, ln_gamma, ln_beta):
        import jax, jax.numpy as jnp
        import numpy as np
        N, E, H, ED, GD = (100000, 25000, 128, 64, 64)
        LN_EPS = 1e-05

        def _mlp(x, w1, b1, w2, b2):
            return jax.nn.relu(x @ w1 + b1) @ w2 + b2
        src, dst = (edge_index[0], edge_index[1])
        num_nodes = node_state.shape[0]
        num_edges = src.shape[0]
        global_edges = jnp.broadcast_to(global_state, (num_edges, global_state.shape[0]))
        message_input = jnp.concatenate([node_state[src], edge_state, global_edges], axis=-1)
        messages = _mlp(message_input, msg_w1, msg_b1, msg_w2, msg_b2)
        aggregated = jax.ops.segment_sum(messages, dst, num_segments=num_nodes)
        degree = jax.ops.segment_sum(jnp.ones((num_edges,), node_state.dtype), dst, num_segments=num_nodes)
        aggregated = aggregated / jnp.maximum(degree, 1.0)[:, None]
        global_nodes = jnp.broadcast_to(global_state, (num_nodes, global_state.shape[0]))
        update_input = jnp.concatenate([node_state, aggregated, global_nodes], axis=-1)
        delta = _mlp(update_input, upd_w1, upd_b1, upd_w2, upd_b2)
        x = node_state + delta
        mu = jnp.mean(x, axis=-1, keepdims=True)
        var = jnp.mean(jnp.square(x - mu), axis=-1, keepdims=True)
        return (x - mu) * jax.lax.rsqrt(var + LN_EPS) * ln_gamma + ln_beta
    edge_index = jnp.stack([src, dst])
    x = _layernorm(x + _L0_gnn_ref(x, L0_gnn_W, L0_gnn_b, edge_index), axis=-1)
    x = _layernorm(x + _L1_gnn_ref(x, edge_index, edge_attr_16, L1_gnn_Wl, L1_gnn_bl, L1_gnn_Wr, L1_gnn_br, L1_gnn_att, L1_gnn_bias), axis=-1)
    x = _layernorm(x + _L2_gnn_ref(x, edge_index, L2_gnn_W_sim, L2_gnn_b_sim, L2_gnn_w_vec, L2_gnn_b_vec, L2_gnn_W1, L2_gnn_b1, L2_gnn_W2, L2_gnn_b2), axis=-1)
    x = _layernorm(x + _L3_gnn_ref(x, edge_index, edge_attr_64, L3_gnn_global_state, L3_gnn_msg_w1, L3_gnn_msg_b1, L3_gnn_msg_w2, L3_gnn_msg_b2, L3_gnn_upd_w1, L3_gnn_upd_b1, L3_gnn_upd_w2, L3_gnn_upd_b2, L3_gnn_ln_gamma, L3_gnn_ln_beta), axis=-1)
    return x

_drawn_inputs = setup_inputs


def setup_inputs(seed=0):
    import zlib

    import numpy as np

    out = dict(_drawn_inputs(seed))
    spreads = {'L1_gnn_bl': (0.0, 0.1),
     'L1_gnn_br': (0.0, 2.0),
     'L1_gnn_bias': (0.0, 0.1),
     'L2_gnn_b2': (0.0, 0.1),
     'L3_gnn_msg_b1': (0.0, 0.8),
     'L3_gnn_msg_b2': (0.0, 0.8),
     'L3_gnn_upd_b1': (0.0, 0.311),
     'L3_gnn_upd_b2': (0.0, 0.1),
     'L3_gnn_ln_gamma': (1.0, 0.2),
     'L3_gnn_ln_beta': (0.0, 0.1)}
    factors = {'L0_gnn_b': 4.179,
     'L2_gnn_W_sim': 8.0,
     'L2_gnn_b_sim': 64.0,
     'L2_gnn_w_vec': 21.405,
     'L2_gnn_b1': 6.281}
    for name, (base, spread) in spreads.items():
        noise = np.random.default_rng([zlib.crc32(name.encode()), seed]).standard_normal(out[name].shape)
        drawn = base * np.exp(spread * noise) if base else spread * noise
        out[name] = jnp.asarray(drawn.astype(out[name].dtype))
    for name, factor in factors.items():
        out[name] = (out[name] * factor).astype(out[name].dtype)
    return out
```

```python
import concourse.bass as bass
from concourse import mybir
from contextlib import ExitStack

F32 = mybir.dt.float32
I32 = mybir.dt.int32
ALU = mybir.AluOpType
ACT = mybir.ActivationFunctionType

P = 128
D = 128
K = 4
G = K * P
H = 64
UNROLL = 4
EPS = 1e-5
BIG = 1e38
NOWHERE = 1 << 20
ATT_SLOPE = 0.2
OUT_SLOPE = 0.01


def round_up(n, m):
    return -(-n // m) * m


class Tally:

    def __init__(self, sems, per_step):
        self.sems, self.per_step, self.count, self.into = sems, per_step, [0, 0], 0

    def add(self, parity):
        self.count[parity] += 1
        return self.sems[parity]

    def enter(self, i, first):
        self.into = (i - first) * (UNROLL // 2 * self.per_step * 16 // UNROLL)

    def leave(self, trips):
        self.into = 0
        for parity in range(2):
            self.count[parity] += (trips - 1) * (UNROLL // 2) * self.per_step

    def wait(self, eng, parity):
        if self.count[parity]:
            eng.wait_ge(self.sems[parity], self.into + 16 * self.count[parity])


def dma_steps(eng, body, tallies, steps, first, last):
    for t in range(first):
        body(t, t % UNROLL)
    with eng.Fori(first, last - UNROLL + 1, UNROLL) as i:
        for tally in tallies:
            tally.enter(i, first)
        for u in range(UNROLL):
            body(i + u, u)
    for tally in tallies:
        tally.leave((last - first) // UNROLL)
    for t in range(last, steps):
        body(t, t % UNROLL)


def steps_of(eng, body, steps):
    with eng.Fori(0, steps - UNROLL + 1, UNROLL) as i:
        for u in range(UNROLL):
            body(i + u, u)


def await_step(eng, t, step_sems):
    for s in step_sems:
        eng.wait_ge(s, t + 1)


def tiles(buf):
    return [buf[:, k * P:(k + 1) * P] for k in range(K)]


def build(nc, v, out):
    N = v["x"].shape[0]
    GROUPS = v["dst_windows"].shape[0]
    NODE_GROUPS = -(-N // G)

    ctx = ExitStack()
    with ctx:
        def sb(name, shape, dt=F32):
            return ctx.enter_context(nc.sbuf_tensor(name, shape, dt))

        def sem(name):
            return ctx.enter_context(nc.semaphore(name))

        def pair(name):
            return [sem(f"{name}_even"), sem(f"{name}_odd")]

        def dram(name, shape):
            return nc.dram_tensor(name, shape, F32, kind="Internal").ap()

        tables = [dram(f"state_{n}", (N, D)) for n in (1, 2, 3)]
        dst1_turned = dram("dst1_turned", (GROUPS, P, G))
        dst1_filled = dram("dst1_filled", (GROUPS, P, G))
        dst3 = dram("dst_state_3", (GROUPS * G, D))
        readout = dram("readout", (N + 2 * G, D))
        MASKS = ("goes_on", "restart", "is_last", "not_last")
        mask_rows = {m: dram(m, (GROUPS, G)) for m in (*MASKS, "source")}

        RING = 74
        arena = sb("arena", [P, RING * G])
        bank = [ctx.enter_context(nc.psum_tensor(f"bank{i}", [P, G], F32)) for i in range(8)]

        class Rings:

            def __init__(self):
                self.used = 0

            def __call__(self, n):
                at = [arena[:, (self.used + i) * G:(self.used + i + 1) * G] for i in range(n)]
                self.used += n
                assert self.used <= RING - 4
                return at

        restart = [arena[:, i * G:(i + 1) * G] for i in range(RING - 4, RING)]
        ident = sb("ident", [P, P])
        ones_row = sb("ones_row", [1, P])
        half_neg = sb("half_neg", [P, 5 * K])
        w = {}
        for name in ("Wl", "Wr", "Wlr", "W_self", "W_nbr", "Wlin", "att_relu", "att_lin", "msg1x", "msg2",
                     "upd1x", "upd1a", "upd2"):
            w[name] = sb("w_" + name, [P, P])
        w["W_sim"] = sb("w_W_sim", [P, H])
        w["W1"] = sb("w_W1", [P, H])
        for name in ("W2", "msg1e", "msg1g", "upd1g"):
            w[name] = sb("w_" + name, [H, P])
        col = {}
        for name in ("L0_b", "bl", "br", "bias", "b_vec", "msg_b1", "msg_b2", "upd_b1", "bl_br", "bl_bias",
                     "msg_c", "upd_c_node", "upd_c_edge", "att"):
            col[name] = sb("c_" + name, [P, 1])
        for name in ("b_sim", "b1", "glob", "w_vec"):
            col[name] = sb("c_" + name, [H, 1])
        row = {}
        for name in ("xl_bias", "xl_bias_lin", "b2", "upd_b2"):
            row[name] = sb("r_" + name, [1, G])
        wide = {}
        for name in ("gamma", "beta"):
            wide[name] = sb("n_" + name, [P, G])
        src_index = sb("src_index", [P, GROUPS * K], I32)
        dst_index = sb("dst_index", [P, GROUPS * K], I32)
        src_value = sb("src_value", [P, GROUPS * K])
        spare_row = sb("spare_row", [P, K])
        earlier = sb("earlier", [P, K, G])
        put_index = sb("put_index", [P, GROUPS * K], I32)
        index_now = [sb(f"index_now{i}", [P, 2 * K], I32) for i in range(2)]
        put_now = [sb(f"put_now{i}", [P, K], I32) for i in range(2)]
        add_now = [sb(f"add_now{i}", [P, K], I32) for i in range(4)]
        src_now = sb("src_now", [P, K])
        repeats = sb("repeats", [P, K])
        detour = sb("detour", [P, K])
        gate = [sb(f"gate{i}", [P, K]) for i in range(2)]
        stats = sb("stats", [P, 5 * K, 6])
        mean2 = sb("mean2", [P, 5 * K])
        gap = sb("gap", [P, 5 * K])
        spread = sb("spread", [P, 5 * K])
        gap2 = sb("gap2", [P, 5 * K])
        var = sb("var", [P, 5 * K])
        rstd = [sb(f"rstd{i}", [P, 5 * K]) for i in range(2)]
        shift = [sb(f"shift{i}", [P, 5 * K]) for i in range(2)]
        max_run = [sb(f"max_run{i}", [P, G + 1]) for i in range(2)]

        def prepare():
            loads = sem("weights_loaded")
            idm = sem("identity_made")
            ready = sem("operands_ready")
            products = sem("products_ready")
            made = sem("prep_made")
            stored = sem("masks_stored")
            W0 = arena[:, 0:2 * P]
            win_i = sb("windows", [GROUPS, G + 2], I32)
            dst_next = sb("dst_next", [P, GROUPS * K], I32)
            differs = sb("differs", [P, GROUPS * K])
            mask = {m: sb("m_" + m, [GROUPS, G]) for m in MASKS}
            r = {n: sb("raw_" + n, [1, P]) for n in ("bl", "bias", "b2", "upd_b2")}
            src_i = sb("src_row_i", [GROUPS, G], I32)
            mask["source"] = sb("m_source", [GROUPS, G])
            ones_wide = sb("ones_wide", [P, P])
            att_s = sb("att_s", [P, 2])
            raw_gamma, raw_beta = sb("raw_gamma", [P, P]), sb("raw_beta", [P, P])

            def as_col(a):
                return a.rearrange("(p a) -> p a", a=1)

            def as_row(a):
                return a.rearrange("(a p) -> a p", a=1)

            pieces = [
                (W0, v["L0_gnn_W"]), (w["Wl"][:], v["L1_gnn_Wl"]), (w["Wr"][:], v["L1_gnn_Wr"]),
                (w["W_sim"][:], v["L2_gnn_W_sim"]), (w["W1"][:], v["L2_gnn_W1"]), (w["W2"][:], v["L2_gnn_W2"]),
                (w["msg1x"][:], v["L3_gnn_msg_w1"][0:D, :]), (w["msg1e"][:], v["L3_gnn_msg_w1"][D:D + H, :]),
                (w["msg1g"][:], v["L3_gnn_msg_w1"][D + H:D + 2 * H, :]), (w["msg2"][:], v["L3_gnn_msg_w2"]),
                (w["upd1x"][:], v["L3_gnn_upd_w1"][0:D, :]), (w["upd1a"][:], v["L3_gnn_upd_w1"][D:2 * D, :]),
                (w["upd1g"][:], v["L3_gnn_upd_w1"][2 * D:2 * D + H, :]), (w["upd2"][:], v["L3_gnn_upd_w2"]),
                (col["L0_b"][:], as_col(v["L0_gnn_b"])), (col["bl"][:], as_col(v["L1_gnn_bl"])),
                (col["br"][:], as_col(v["L1_gnn_br"])), (col["bias"][:], as_col(v["L1_gnn_bias"])),
                (col["att"][:], as_col(v["L1_gnn_att"])), (col["b_sim"][:], as_col(v["L2_gnn_b_sim"])),
                (col["b1"][:], as_col(v["L2_gnn_b1"])), (col["w_vec"][:], v["L2_gnn_w_vec"]),
                (col["b_vec"][:], as_row(v["L2_gnn_b_vec"]).to_broadcast([P, 1])),
                (col["glob"][:], as_col(v["L3_gnn_global_state"])), (col["msg_b1"][:], as_col(v["L3_gnn_msg_b1"])),
                (col["msg_b2"][:], as_col(v["L3_gnn_msg_b2"])), (col["upd_b1"][:], as_col(v["L3_gnn_upd_b1"])),
                (r["bl"][:], as_row(v["L1_gnn_bl"])), (r["bias"][:], as_row(v["L1_gnn_bias"])),
                (r["b2"][:], as_row(v["L2_gnn_b2"])), (r["upd_b2"][:], as_row(v["L3_gnn_upd_b2"])),
                (raw_gamma[:], as_row(v["L3_gnn_ln_gamma"]).to_broadcast([P, P])),
                (raw_beta[:], as_row(v["L3_gnn_ln_beta"]).to_broadcast([P, P])),
                (win_i[:], v["dst_windows"]), (src_index[:], v["src_tiles"]), (dst_index[:], v["dst_tiles"]),
                (dst_next[:], v["dst_next_tiles"]), (src_i[:], v["src_rows"]),
            ]
            with nc.Block() as block:
                @block.sync
                def _(sp):
                    for to, of in pieces:
                        sp.dma_start(to, of).then_inc(loads, 16)
                    sp.wait_ge(made, 2)
                    for m in mask_rows:
                        sp.dma_start(mask_rows[m], mask[m][:]).then_inc(stored, 16)
                    sp.wait_ge(stored, 16 * len(mask_rows))

                @block.gpsimd
                def _(pool):
                    pool.memset(ident[:], 0.0).then_inc(idm, 1)
                    pool.wait_ge(idm, 1)
                    pool.affine_select(out=ident[:], in_=ident[:], compare_op=ALU.not_equal, fill=1.0, base=0,
                                       pattern=[[-1, P]], channel_multiplier=1).then_inc(idm, 1)
                    pool.iota(spare_row[:], pattern=[[P, K]], base=N, channel_multiplier=1,
                              allow_small_or_imprecise_dtypes=True)
                    pool.memset(earlier[:], 1.0).then_inc(idm, 1)
                    pool.wait_ge(idm, 3)
                    pool.affine_select(out=earlier[:], in_=earlier[:], compare_op=ALU.is_gt, fill=0.0, base=0,
                                       pattern=[[P, K], [-1, G]], channel_multiplier=1).then_inc(idm, 1)

                @block.vector
                def _(dve):
                    dve.memset(ones_row[:], 1.0)
                    dve.memset(ones_wide[:], 1.0)
                    dve.memset(half_neg[:], -0.5)
                    for b in bank:
                        dve.memset(b[:], 0.0)
                    for i in range(2):
                        dve.memset(gate[i][:], 0.0)
                        dve.memset(rstd[i][:], 0.0)
                        dve.memset(shift[i][:], 0.0)
                        dve.memset(max_run[i][:], 0.0)
                    dve.wait_ge(loads, 16 * len(pieces))
                    dve.wait_ge(idm, 4)
                    dve.drain()
                    dve.tensor_scalar(att_s[:, 0:1], col["att"][:], 1.0 - ATT_SLOPE, None, ALU.mult)
                    dve.tensor_scalar(att_s[:, 1:2], col["att"][:], ATT_SLOPE, None, ALU.mult).then_inc(ready, 1)
                    dve.drain()
                    dve.tensor_scalar(w["att_relu"][:], ones_wide[:], att_s[:, 0:1], None, ALU.mult)
                    dve.tensor_scalar(w["att_lin"][:], ones_wide[:], att_s[:, 1:2], None, ALU.mult)
                    dve.tensor_tensor(w["Wlr"][:], w["Wl"][:], w["Wr"][:], ALU.add)
                    dve.scalar_tensor_tensor(w["Wlin"][:], w["Wl"][:], OUT_SLOPE, ident[:], ALU.mult, ALU.add)
                    dve.tensor_tensor(col["bl_br"][:], col["bl"][:], col["br"][:], ALU.add)
                    dve.tensor_tensor(col["bl_bias"][:], col["bl"][:], col["bias"][:], ALU.add)
                    for k in range(K):
                        at = slice(k * P, (k + 1) * P)
                        dve.tensor_tensor(row["xl_bias"][:, at], r["bl"][:], r["bias"][:], ALU.add)
                        dve.tensor_copy(row["b2"][:, at], r["b2"][:])
                        dve.tensor_copy(row["upd_b2"][:, at], r["upd_b2"][:])
                        dve.tensor_copy(wide["gamma"][:, at], raw_gamma[:])
                        dve.tensor_copy(wide["beta"][:, at], raw_beta[:])
                    dve.drain()
                    dve.tensor_scalar(row["xl_bias_lin"][:], row["xl_bias"][:], OUT_SLOPE, None, ALU.mult)
                    dve.tensor_copy(mask["source"][:], src_i[:])
                    dve.tensor_tensor(mask["goes_on"][:], win_i[:, 1:G + 1], win_i[:, 0:G], ALU.is_equal)
                    dve.tensor_tensor(mask["not_last"][:], win_i[:, 1:G + 1], win_i[:, 2:G + 2], ALU.is_equal)
                    dve.tensor_tensor(differs[:], dst_index[:], dst_next[:], ALU.not_equal)
                    dve.drain()
                    dve.tensor_scalar(mask["restart"][:], mask["goes_on"][:], -1.0, BIG, ALU.add, ALU.mult)
                    dve.tensor_scalar(mask["is_last"][:], mask["not_last"][:], -1.0, 1.0, ALU.mult,
                                      ALU.add).then_inc(made, 2)
                    dve.scalar_tensor_tensor(put_index[:], dst_index[:], -float(NOWHERE), differs[:], ALU.add, ALU.mult)
                    dve.drain()
                    dve.tensor_scalar(put_index[:], put_index[:], float(NOWHERE), None, ALU.add)
                    dve.tensor_scalar(dst_index[:], dst_index[:], float(N - 1), None, ALU.min)
                    dve.tensor_copy(src_value[:], src_index[:])
                    dve.drain()
                    dve.tensor_scalar(src_index[:], src_index[:], float(N - 1), None, ALU.min)
                    dve.wait_ge(products, 1)
                    dve.tensor_copy(w["W_nbr"][:], bank[1][:, 0:P])
                    dve.tensor_tensor(col["msg_c"][:], bank[2][:, 0:1], col["msg_b1"][:], ALU.add)
                    dve.tensor_tensor(col["upd_c_node"][:], bank[3][:, 0:1], col["upd_b1"][:], ALU.add)
                    dve.drain()
                    dve.scalar_tensor_tensor(w["W_self"][:], bank[0][:, 0:P], 1.0, w["W_nbr"][:], ALU.mult, ALU.subtract)
                    dve.tensor_tensor(col["upd_c_edge"][:], bank[4][:, 0:1], col["upd_c_node"][:], ALU.add)
                    dve.drain()
                    dve.tensor_tensor(w["W_self"][:], w["W_self"][:], ident[:], ALU.add)
                    dve.drain()

                @block.tensor
                def _(pe):
                    pe.wait_ge(ready, 1)
                    pe.transpose(bank[0][:, 0:P], W0[:, 0:P], ident[:])
                    pe.transpose(bank[1][:, 0:P], W0[:, P:2 * P], ident[:])
                    pe.matmul(bank[2][:, 0:1], w["msg1g"][:], col["glob"][:], start=True, stop=True)
                    pe.matmul(bank[3][:, 0:1], w["upd1g"][:], col["glob"][:], start=True, stop=True)
                    pe.matmul(bank[4][:, 0:1], w["upd1a"][:], col["msg_b2"][:], start=True, stop=True).then_inc(products, 1)

        def group_rows(table, b):
            base = min(b * G, N - G) if isinstance(b, int) else b * G
            return table[bass.ds(base, G), :].rearrange("(p k) f -> p (k f)", k=K)

        def edge_rows(table, b):
            return table[bass.ds(b * G, G), :].rearrange("(k p) f -> p k f", p=P)

        def as_tiles(buf):
            return buf.rearrange("p (k f) -> p k f", k=K)

        def turned_group(table, b):
            return table[bass.ds(b, 1), :, :].rearrange("a p e -> (a p) e")

        def mask_group(m, b):
            return mask_rows[m][bass.ds(b, 1), :].to_broadcast([P, G])

        def ln_statistics(dve, bufs, var_ready):
            n = len(bufs) * K
            for b, buf in enumerate(bufs):
                for k, tile in enumerate(tiles(buf)):
                    dve.bn_stats(stats[:, b * K + k, :], tile)
            dve.drain()
            dve.tensor_tensor(mean2[:, 0:n], stats[:, 0:n, 1], stats[:, 0:n, 4], ALU.add)
            dve.tensor_tensor(gap[:, 0:n], stats[:, 0:n, 1], stats[:, 0:n, 4], ALU.subtract)
            dve.scalar_tensor_tensor(spread[:, 0:n], stats[:, 0:n, 2], D * EPS, stats[:, 0:n, 5], ALU.add, ALU.add)
            dve.drain()
            dve.scalar_tensor_tensor(gap2[:, 0:n], gap[:, 0:n], 0.25, gap[:, 0:n], ALU.mult, ALU.mult)
            dve.drain()
            dve.scalar_tensor_tensor(var[:, 0:n], spread[:, 0:n], 1.0 / D, gap2[:, 0:n], ALU.mult,
                                     ALU.add).then_inc(var_ready, 1)

        def ln_rstd(pool, n, u, t, var_ready, rstd_ready):
            pool.wait_ge(var_ready, t + 1)
            return pool.tensor_tensor(rstd[u % 2][:, 0:n], var[:, 0:n], half_neg[:, 0:n],
                                      ALU.pow).then_inc(rstd_ready, 1)

        def ln_shift(dve, n, u, t, rstd_ready):
            dve.wait_ge(rstd_ready, t + 1)
            dve.scalar_tensor_tensor(shift[u % 2][:, 0:n], mean2[:, 0:n], -0.5, rstd[u % 2][:, 0:n],
                                     ALU.mult, ALU.mult)
            dve.drain()

        def ln_apply_dve(dve, to, of, at, u):
            for k in range(K):
                c = at * K + k
                last = dve.tensor_scalar(tiles(to)[k], tiles(of)[k], rstd[u % 2][:, c:c + 1],
                                         shift[u % 2][:, c:c + 1], ALU.mult, ALU.add)
            return last

        def ln_apply_act(act, to, of, at, u):
            for k in range(K):
                c = at * K + k
                last = act.activation(tiles(to)[k], tiles(of)[k], ACT.Identity,
                                      bias=shift[(u - 1) % 2][:, c:c + 1], scale=rstd[(u - 1) % 2][:, c:c + 1])
            return last

        def turn(pe, to, of, width=D):
            for k in range(K):
                last = pe.transpose(to[0:width, k * P:(k + 1) * P], of[:, k * width:(k + 1) * width], ident[:])
            return last

        def natural_product(pe, to, turned, weight, bias_row):
            rows = weight.shape[0]
            pe.matmul(to[:], ones_row[:], bias_row[:], start=True, stop=False, skip_group_check=True)
            for k in range(K):
                last = pe.matmul(to[:, k * P:(k + 1) * P], turned[0:rows, k * P:(k + 1) * P], weight[:],
                                 start=False, stop=k == K - 1, skip_group_check=True)
            return last

        def engine_steps(name):
            return [sem(f"{name}_{e}_step") for e in ("sp", "pool", "act", "dve", "pe")]

        def sp_program(sp, every, name, groups, loads, stores, steps, first_full, end_full):
            loaded = Tally(pair(f"{name}_loaded"), len(loads))
            stored = Tally(pair(f"{name}_stored"), len(stores))
            waited = sem(f"{name}_sp_waited")

            def start_loads(t, u):
                for use, ring, source in loads:
                    b = t + 2 - use
                    if not isinstance(t, int) or 0 <= b < groups:
                        to, of = source(ring[(u + 2 - use) % 4], b)
                        sp.dma_start(to, of).then_inc(loaded.add(u % 2), 16)

            def body(t, u):
                await_step(sp, t, every)
                sp.sem_inc(waited, 1)
                start_loads(t, u)
                stored.wait(sp, (u - 1) % 2)
                sp.sem_inc(waited, 1)
                for lag, ring, place in stores:
                    b = t - lag
                    if not isinstance(t, int) or 0 <= b < groups:
                        of, to = place(ring[(u - lag) % 4], b)
                        sp.dma_start(to, of).then_inc(stored.add(u % 2), 16)
                loaded.wait(sp, (u - 1) % 2)
                sp.sem_inc(every[0], 1)

            start_loads(-2, -2)
            start_loads(-1, -1)
            loaded.wait(sp, 0)
            sp.sem_inc(every[0], 1)
            dma_steps(sp, body, (loaded, stored), steps, first_full, end_full)
            for parity in range(2):
                stored.wait(sp, parity)

        def pool_program(pool, every, name, groups, gathers, scatter, steps, first_full, end_full, norms,
                         var_ready, rstd_ready, add_index=None):
            indexed = sem(f"{name}_index_copied")
            checked = sem(f"{name}_index_checked")
            gathered = Tally(pair(f"{name}_gathered"), K * len(gathers))
            scattered = Tally(pair(f"{name}_scattered"), K)
            per_step = len(gathers) + (add_index is None)
            at_lag, from_ring, to_table = scatter
            copies = [0, 0]

            def start_gathers(t, u):
                b = t + 2
                if isinstance(t, int) and not b < groups:
                    return
                for n, (ring, table, index) in enumerate(gathers):
                    now = index_now[u % 2][:, n * K:(n + 1) * K]
                    pool.tensor_copy(now, index[:, bass.ds(b * K, K)]).then_inc(indexed, 1)
                    copied(1)
                    for k in range(K):
                        pool.indirect_dma_start(
                            out=ring[(u + 2) % 4][:, k * P:(k + 1) * P], out_offset=None, in_=table,
                            in_offset=bass.IndirectOffsetOnAxis(ap=now[:, k:k + 1], axis=0),
                            bounds_check=N - 1, oob_is_err=False).then_inc(gathered.add(u % 2), 16)

            def copied(n):
                copies[0] += n
                pool.wait_ge(indexed, copies[0] + copies[1])
                pool.sem_inc(checked, 1)

            def body(t, u):
                await_step(pool, t, every)
                start_gathers(t, u)
                if norms:
                    ln_rstd(pool, norms * K, u, t, var_ready, rstd_ready)
                b = t - at_lag
                if not isinstance(t, int) or 0 <= b < groups:
                    if add_index is None:
                        pool.tensor_copy(put_now[u % 2][:], put_index[:, bass.ds(b * K, K)]).then_inc(indexed, 1)
                        copied(1)
                        for k in range(K):
                            pool.indirect_dma_start(
                                out=to_table,
                                out_offset=bass.IndirectOffsetOnAxis(ap=put_now[u % 2][:, k:k + 1], axis=0),
                                in_=from_ring[(u - at_lag) % 4][:, k * P:(k + 1) * P], in_offset=None,
                                bounds_check=N - 1, oob_is_err=False).then_inc(scattered.add(u % 2), 16)
                    else:
                        scattered.wait(pool, (u - 1) % 2)
                        pool.sem_inc(checked, 1)
                        for k in range(K):
                            pool.indirect_dma_start(
                                out=to_table,
                                out_offset=bass.IndirectOffsetOnAxis(
                                    ap=add_index[(u - at_lag) % 4][:, k:k + 1], axis=0),
                                in_=from_ring[(u - at_lag) % 4][:, k * P:(k + 1) * P], in_offset=None,
                                compute_op=ALU.add).then_inc(scattered.add(u % 2), 16)
                gathered.wait(pool, (u - 1) % 2)
                scattered.wait(pool, (u - 1) % 2)
                if norms:
                    pool.wait_ge(rstd_ready, t + 1)
                pool.sem_inc(every[1], 1)

            start_gathers(-2, -2)
            start_gathers(-1, -1)
            gathered.wait(pool, 0)
            pool.sem_inc(every[1], 1)
            for t in range(first_full):
                body(t, t % UNROLL)
            with pool.Fori(first_full, end_full - UNROLL + 1, UNROLL) as i:
                gathered.enter(i, first_full)
                scattered.enter(i, first_full)
                copies[1] = (i - first_full) * per_step
                for u in range(UNROLL):
                    body(i + u, u)
            trips = (end_full - first_full) // UNROLL
            gathered.leave(trips)
            scattered.leave(trips)
            copies[0] += (trips - 1) * UNROLL * per_step
            copies[1] = 0
            for t in range(end_full, steps):
                body(t, t % UNROLL)
            scattered.wait(pool, 0)
            scattered.wait(pool, 1)

        def load_rows(table):
            return lambda buf, b: (buf, group_rows(table, b))

        def load_edges(table, width=D):
            return lambda buf, b: (buf[:, 0:K * width].rearrange("p (k f) -> p k f", k=K), edge_rows(table, b))

        def load_turned(table):
            return lambda buf, b: (buf, turned_group(table, b))

        def load_mask(m):
            return lambda buf, b: (buf, mask_group(m, b))

        def full_range(groups, first_lag, last_ahead=2):
            return round_up(first_lag + 1, UNROLL), (groups - last_ahead) // UNROLL * UNROLL

        def pass_nodes_a():
            new = Rings()
            x, x1, x2 = (new(4) for _ in range(3))
            x1t, hr, y1 = (new(2) for _ in range(3))
            zeros = new(1)[0]
            b_x1t, b_h, b_lin = bank[0], bank[1], bank[2:4]
            every = engine_steps("na")
            sp_step, pool_step, act_step, dve_step, pe_step = every
            x1t_out, h_out = sem("na_x1_turned"), sem("na_h_done")
            var_ready, rstd_ready = sem("na_var"), sem("na_rstd")
            cleared, spare_cleared = sem("arena_cleared"), sem("spare_rows_cleared")
            LAST = 6
            STEPS = round_up(NODE_GROUPS + LAST + 1, UNROLL)
            RANGE = full_range(NODE_GROUPS, LAST, 3)
            with nc.Block() as block:
                @block.sync
                def _(sp):
                    sp.wait_ge(cleared, 2)
                    for i in range(2):
                        sp.dma_start(readout[N + i * G:N + (i + 1) * G, :].rearrange("(p k) f -> p (k f)", k=K),
                                     zeros).then_inc(spare_cleared, 16)
                    sp_program(sp, every, "na", NODE_GROUPS, [(0, x, load_rows(v["x"]))],
                               [(0, [zeros] * 4, load_rows(readout)), (2, x1, load_rows(tables[0])),
                                (6, x2, load_rows(tables[1]))], STEPS, *RANGE)
                    sp.wait_ge(spare_cleared, 32)

                @block.gpsimd
                def _(pool):
                    pool.memset(arena[:, RING // 2 * G:], 0.0).then_inc(cleared, 1)
                    pool.sem_inc(pool_step, 1)

                    def body(t, u):
                        await_step(pool, t, every)
                        ln_rstd(pool, 2 * K, u, t, var_ready, rstd_ready)
                        pool.wait_ge(rstd_ready, t + 1)
                        pool.sem_inc(pool_step, 1)

                    pool.wait_ge(cleared, 2)
                    steps_of(pool, body, STEPS)

                @block.scalar
                def _(act):
                    act.sem_inc(act_step, 1)

                    def body(t, u):
                        await_step(act, t, every)
                        ln_apply_act(act, x2[(u - 5) % 4], y1[(u - 5) % 2], 1, u)
                        act.wait_ge(x1t_out, t + 1)
                        act.activation(x1t[u % 2], b_x1t[:], ACT.Copy)
                        act.wait_ge(h_out, t + 1)
                        act.activation(hr[u % 2], b_h[:], ACT.Relu, scale=1.0 - OUT_SLOPE).then_inc(act_step, 1)

                    act.wait_ge(cleared, 2)
                    steps_of(act, body, STEPS)

                @block.vector
                def _(dve):
                    dve.memset(arena[:, 0:RING // 2 * G], 0.0).then_inc(cleared, 1)
                    dve.sem_inc(dve_step, 1)

                    def body(t, u):
                        await_step(dve, t, every)
                        dve.tensor_tensor(y1[(u - 4) % 2], hr[(u - 1) % 2], b_lin[(u - 1) % 2][:], ALU.add)
                        dve.drain()
                        ln_statistics(dve, (x[u % 4], y1[(u - 4) % 2]), var_ready)
                        ln_shift(dve, 2 * K, u, t, rstd_ready)
                        ln_apply_dve(dve, x1[u % 4], x[u % 4], 0, u).then_inc(dve_step, 1)

                    dve.wait_ge(cleared, 2)
                    steps_of(dve, body, STEPS)

                @block.tensor
                def _(pe):
                    pe.sem_inc(pe_step, 1)

                    def body(t, u):
                        await_step(pe, t, every)
                        turn(pe, b_x1t, x1[(u - 2) % 4]).then_inc(x1t_out, 1)
                        natural_product(pe, b_h, x1t[(u - 1) % 2], w["Wl"], row["xl_bias"]).then_inc(h_out, 1)
                        natural_product(pe, b_lin[u % 2], x1t[(u - 1) % 2], w["Wlin"],
                                        row["xl_bias_lin"]).then_inc(pe_step, 1)

                    pe.wait_ge(cleared, 2)
                    steps_of(pe, body, STEPS)

        def pass_nodes_b():
            new = Rings()
            read, x2, x3, x3b, y5, res = (new(4) for _ in range(6))
            readt, act1, x3t, h3, n4 = (new(2) for _ in range(5))
            y2, y4, scaled_n = (new(1)[0] for _ in range(3))
            b_readt, b_act1, b_prompt, b_x3t, b_u, b_delta = bank[0], bank[1], bank[2:4], bank[4], bank[5], bank[6:8]
            every = engine_steps("nb")
            sp_step, pool_step, act_step, dve_step, pe_step = every
            readt_out, act1_out, x3t_out, u_out = (
                sem(f"nb_{n}") for n in ("readout_turned", "prompt1_done", "x3_turned", "upd1_done"))
            var_ready, rstd_ready, scaled = sem("nb_var"), sem("nb_rstd"), sem("nb_scaled")
            LAST = 11
            STEPS = round_up(NODE_GROUPS + LAST + 1, UNROLL)
            RANGE = full_range(NODE_GROUPS, LAST, 3)
            with nc.Block() as block:
                @block.sync
                def _(sp):
                    sp_program(sp, every, "nb", NODE_GROUPS,
                               [(0, read, load_rows(readout)), (3, x2, load_rows(tables[1]))],
                               [(4, x3, load_rows(tables[2])), (11, res, load_rows(out))], STEPS, *RANGE)

                @block.gpsimd
                def _(pool):
                    pool.sem_inc(pool_step, 1)

                    def body(t, u):
                        await_step(pool, t, every)
                        pool.tensor_tensor(scaled_n, n4[(u - 8) % 2], wide["gamma"][:], ALU.mult).then_inc(scaled, 1)
                        pool.tensor_tensor(x3b[(u - 6) % 4], x3[(u - 6) % 4], wide["beta"][:], ALU.add)
                        pool.wait_ge(scaled, t + 1)
                        pool.tensor_tensor(y5[(u - 8) % 4], scaled_n, x3b[(u - 8) % 4], ALU.add)
                        ln_rstd(pool, 3 * K, u, t, var_ready, rstd_ready)
                        pool.wait_ge(rstd_ready, t + 1)
                        pool.sem_inc(pool_step, 1)

                    steps_of(pool, body, STEPS)

                @block.scalar
                def _(act):
                    act.sem_inc(act_step, 1)

                    def body(t, u):
                        await_step(act, t, every)
                        ln_apply_act(act, res[(u - 10) % 4], y5[(u - 10) % 4], 2, u)
                        act.wait_ge(readt_out, t + 1)
                        act.activation(readt[u % 2], b_readt[:], ACT.Copy)
                        act.wait_ge(x3t_out, t + 1)
                        act.activation(x3t[u % 2], b_x3t[:], ACT.Copy)
                        act.wait_ge(act1_out, t + 1)
                        act.activation(act1[u % 2][0:H, :], b_act1[0:H, :], ACT.Relu, bias=col["b1"][:])
                        act.wait_ge(u_out, t + 1)
                        act.activation(h3[u % 2], b_u[:], ACT.Relu, bias=col["upd_c_node"][:]).then_inc(act_step, 1)

                    steps_of(act, body, STEPS)

                @block.vector
                def _(dve):
                    dve.sem_inc(dve_step, 1)

                    def body(t, u):
                        await_step(dve, t, every)
                        dve.scalar_tensor_tensor(y2, x2[(u - 3) % 4], 2.0, b_prompt[(u - 1) % 2][:], ALU.mult, ALU.add)
                        dve.tensor_tensor(y4, x3[(u - 7) % 4], b_delta[(u - 1) % 2][:], ALU.add)
                        dve.drain()
                        ln_statistics(dve, (y2, y4, y5[(u - 9) % 4]), var_ready)
                        ln_shift(dve, 3 * K, u, t, rstd_ready)
                        ln_apply_dve(dve, x3[(u - 3) % 4], y2, 0, u)
                        ln_apply_dve(dve, n4[(u - 7) % 2], y4, 1, u).then_inc(dve_step, 1)

                    steps_of(dve, body, STEPS)

                @block.tensor
                def _(pe):
                    pe.sem_inc(pe_step, 1)

                    def body(t, u):
                        await_step(pe, t, every)
                        turn(pe, b_readt, read[u % 4]).then_inc(readt_out, 1)
                        turn(pe, b_x3t, x3[(u - 4) % 4]).then_inc(x3t_out, 1)
                        pe.matmul(b_act1[0:H, :], w["W1"][:], readt[(u - 1) % 2], start=True,
                                  stop=True).then_inc(act1_out, 1)
                        pe.matmul(b_u[:], w["upd1x"][:], x3t[(u - 1) % 2], start=True,
                                  stop=True).then_inc(u_out, 1)
                        natural_product(pe, b_prompt[u % 2], act1[(u - 1) % 2], w["W2"], row["b2"])
                        natural_product(pe, b_delta[u % 2], h3[(u - 1) % 2], w["upd2"],
                                        row["upd_b2"]).then_inc(pe_step, 1)

                    steps_of(pe, body, STEPS)

        def pass_l0():
            new = Rings()
            xs, xd, run, d1, d1t = (new(4) for _ in range(5))
            xst, xdt, own, yt, yn = (new(2) for _ in range(5))
            b_xs, b_xd, b_nbr, b_self, b_y, b_d1 = bank[0], bank[1], bank[2:4], bank[4], bank[5], bank[6]
            every = engine_steps("l0")
            sp_step, pool_step, act_step, dve_step, pe_step = every
            xs_out, xd_out, self_out, y_out, d1_out = (
                sem(f"l0_{n}") for n in ("src_turned", "dst_turned", "self_done", "sum_turned", "state_turned"))
            var_ready, rstd_ready = sem("l0_var"), sem("l0_rstd")
            STEPS = round_up(GROUPS + 6 + 1, UNROLL)
            RANGE = full_range(GROUPS, 6)
            with nc.Block() as block:
                @block.sync
                def _(sp):
                    sp_program(sp, every, "l0", GROUPS, [(2, restart, load_mask("restart"))],
                               [(6, d1t, load_turned(dst1_turned))], STEPS, *RANGE)

                @block.gpsimd
                def _(pool):
                    pool_program(pool, every, "l0", GROUPS, [(xs, v["x"], src_index), (xd, v["x"], dst_index)],
                                 (5, d1, tables[0]), STEPS, *RANGE, 1, var_ready, rstd_ready)

                @block.scalar
                def _(act):
                    act.sem_inc(act_step, 1)

                    def body(t, u):
                        await_step(act, t, every)
                        act.wait_ge(xs_out, t + 1)
                        act.activation(xst[u % 2], b_xs[:], ACT.Copy)
                        act.wait_ge(xd_out, t + 1)
                        act.activation(xdt[u % 2], b_xd[:], ACT.Copy)
                        act.wait_ge(self_out, t + 1)
                        act.activation(own[u % 2], b_self[:], ACT.Identity, bias=col["L0_b"][:])
                        act.wait_ge(y_out, t + 1)
                        act.activation(yn[u % 2], b_y[:], ACT.Copy)
                        act.wait_ge(d1_out, t + 1)
                        act.activation(d1t[(u - 5) % 4], b_d1[:], ACT.Copy).then_inc(act_step, 1)

                    steps_of(act, body, STEPS)

                @block.vector
                def _(dve):
                    dve.sem_inc(dve_step, 1)

                    def body(t, u):
                        await_step(dve, t, every)
                        dve.tensor_tensor_scan(run[(u - 2) % 4], restart[(u - 2) % 4], b_nbr[(u - 1) % 2][:],
                                               run[(u - 3) % 4][:, G - 1:G], ALU.add, ALU.max)
                        dve.drain()
                        dve.tensor_tensor(yt[u % 2], run[(u - 2) % 4], own[(u - 1) % 2], ALU.add)
                        ln_statistics(dve, (yn[(u - 1) % 2],), var_ready)
                        ln_shift(dve, K, u, t, rstd_ready)
                        ln_apply_dve(dve, d1[(u - 4) % 4], yn[(u - 1) % 2], 0, u).then_inc(dve_step, 1)

                    steps_of(dve, body, STEPS)

                @block.tensor
                def _(pe):
                    pe.sem_inc(pe_step, 1)

                    def body(t, u):
                        await_step(pe, t, every)
                        turn(pe, b_xs, xs[u % 4]).then_inc(xs_out, 1)
                        turn(pe, b_xd, xd[u % 4]).then_inc(xd_out, 1)
                        pe.matmul(b_self[:], w["W_self"][:], xdt[(u - 1) % 2], start=True,
                                  stop=True).then_inc(self_out, 1)
                        turn(pe, b_y, yt[(u - 1) % 2]).then_inc(y_out, 1)
                        turn(pe, b_d1, d1[(u - 5) % 4]).then_inc(d1_out, 1)
                        pe.matmul(b_nbr[u % 2][:], w["W_nbr"][:], xst[(u - 1) % 2], start=True,
                                  stop=True).then_inc(pe_step, 1)

                    steps_of(pe, body, STEPS)

        def pass_back():
            new = Rings()
            d1t, is_last, not_last, filled = (new(4) for _ in range(4))
            marked = new(1)[0]
            every = engine_steps("back")
            sp_step, pool_step, act_step, dve_step, pe_step = every
            two = (sp_step, dve_step)
            STEPS = round_up(GROUPS + 1, UNROLL)
            RANGE = full_range(GROUPS, 1)

            def from_end(load):
                return lambda buf, b: load(buf, GROUPS - 1 - b)

            with nc.Block() as block:
                @block.sync
                def _(sp):
                    sp_program(sp, two, "back", GROUPS,
                               [(0, d1t, from_end(load_turned(dst1_turned))), (0, is_last, from_end(load_mask("is_last"))),
                                (0, not_last, from_end(load_mask("not_last")))],
                               [(1, filled, from_end(load_turned(dst1_filled)))], STEPS, *RANGE)

                @block.vector
                def _(dve):
                    dve.sem_inc(dve_step, 1)

                    def body(t, u):
                        await_step(dve, t, two)
                        dve.tensor_tensor(marked, d1t[u % 4], is_last[u % 4], ALU.mult)
                        dve.drain()
                        dve.tensor_tensor_scan(filled[u % 4][:, ::-1], not_last[u % 4][:, ::-1], marked[:, ::-1],
                                               filled[(u - 1) % 4][:, 0:1], ALU.mult, ALU.add).then_inc(dve_step, 1)

                    steps_of(dve, body, STEPS)

        def pass_l1():
            new = Rings()
            xs, xst, d1t, d1t_late, xl, xl_own, d2 = (new(4) for _ in range(7))
            u_relu, u_lin, v_relu, v_lin, own_logit, z, o, mean_xl, ob, yt, yn = (new(2) for _ in range(11))
            at = new(6)
            below = [at[0:3], at[3:6]]
            at = new(6)
            weight = [at[0:3], at[3:6]]

            temp = new(4)
            b_xs, b_u, b_v, b_xl, b_own, b_logit, b_own_logit = (
                bank[0], bank[1], bank[2], bank[3], bank[4], bank[5:7], bank[7])
            every = engine_steps("l1")
            sp_step, pool_step, act_step, dve_step, pe_step = every
            xs_out, u_out, v_out, xl_out, own_out, own_logit_out, y_out, b0_free = (
                sem(f"l1_{n}") for n in ("src_turned", "u_done", "v_done", "xl_done", "own_done", "own_logit_done",
                                         "sum_turned", "src_copied"))
            var_ready, rstd_ready = sem("l1_var"), sem("l1_rstd")
            STEPS = round_up(GROUPS + 10 + 1, UNROLL)
            RANGE = full_range(GROUPS, 10)
            with nc.Block() as block:
                @block.sync
                def _(sp):
                    sp_program(sp, every, "l1", GROUPS,
                               [(1, d1t, load_turned(dst1_filled)), (3, restart, load_mask("restart")),
                                (7, d1t_late, load_turned(dst1_filled))],
                               [], STEPS, *RANGE)

                @block.gpsimd
                def _(pool):
                    pool_program(pool, every, "l1", GROUPS, [(xs, tables[0], src_index)], (10, d2, tables[1]),
                                 STEPS, *RANGE, 1, var_ready, rstd_ready)

                @block.scalar
                def _(act):
                    act.sem_inc(act_step, 1)

                    def body(t, u):
                        await_step(act, t, every)
                        for n in range(3):
                            act.activation(weight[u % 2][n], below[(u - 1) % 2][n], ACT.Exp)
                        act.activation(ob[u % 2], mean_xl[(u - 1) % 2], ACT.Identity, bias=col["bl_bias"][:])
                        act.wait_ge(xs_out, t + 1)
                        act.activation(xst[u % 4], b_xs[:], ACT.Copy).then_inc(b0_free, 1)
                        act.wait_ge(u_out, t + 1)
                        act.activation(u_relu[u % 2], b_u[:], ACT.Relu, bias=col["bl_br"][:])
                        act.activation(u_lin[u % 2], b_u[:], ACT.Identity, bias=col["bl_br"][:])
                        act.wait_ge(v_out, t + 1)
                        act.activation(v_relu[u % 2], b_v[:], ACT.Relu, bias=col["bl_br"][:])
                        act.activation(v_lin[u % 2], b_v[:], ACT.Identity, bias=col["bl_br"][:])
                        act.wait_ge(xl_out, t + 1)
                        act.activation(xl[(u - 2) % 4], b_xl[:], ACT.Copy)
                        act.wait_ge(own_out, t + 1)
                        act.activation(xl_own[(u - 2) % 4], b_own[:], ACT.Copy)
                        act.wait_ge(own_logit_out, t + 1)
                        act.activation(own_logit[u % 2], b_own_logit[:], ACT.Copy)
                        act.wait_ge(y_out, t + 1)
                        act.activation(yn[u % 2], b_xs[:], ACT.Copy).then_inc(act_step, 1)

                    steps_of(act, body, STEPS)

                @block.vector
                def _(dve):
                    for three in weight:
                        for buf in three:
                            dve.memset(buf, 1.0)
                    for buf in below[0] + below[1] + z + o:
                        dve.memset(buf, 0.0)
                    dve.memset(max_run[0][:], 0.0)
                    dve.memset(max_run[1][:], 0.0).then_inc(dve_step, 1)

                    def body(t, u):
                        await_step(dve, t, every)
                        logit, own, m, before = b_logit[(u - 1) % 2], own_logit[(u - 1) % 2], max_run[u % 2], max_run[(u - 1) % 2]
                        d = below[u % 2]
                        shrink, p, p_own = weight[(u - 1) % 2]
                        dve.tensor_tensor(temp[0], logit[:], own, ALU.max)
                        dve.tensor_copy(m[:, 0:1], before[:, G:G + 1])
                        dve.tensor_tensor(temp[1], p, xl[(u - 5) % 4], ALU.mult)
                        dve.tensor_tensor(temp[2], p_own, xl_own[(u - 5) % 4], ALU.mult)
                        dve.tensor_tensor_scan(z[u % 2], shrink, p, z[(u - 1) % 2][:, G - 1:G], ALU.mult, ALU.add)
                        dve.drain()
                        dve.tensor_tensor_scan(m[:, 1:G + 1], restart[(u - 3) % 4], temp[0], before[:, G:G + 1],
                                               ALU.add, ALU.max)
                        dve.tensor_tensor_scan(o[u % 2], shrink, temp[1], o[(u - 1) % 2][:, G - 1:G], ALU.mult, ALU.add)
                        dve.tensor_tensor(temp[3], z[u % 2], p_own, ALU.add)
                        dve.drain()
                        dve.tensor_tensor(d[0], m[:, 0:G], restart[(u - 3) % 4], ALU.add)
                        dve.tensor_tensor(d[1], logit[:], m[:, 1:G + 1], ALU.subtract)
                        dve.tensor_tensor(d[2], own, m[:, 1:G + 1], ALU.subtract)
                        dve.tensor_tensor(temp[2], temp[2], o[u % 2], ALU.add)
                        dve.reciprocal(temp[3], temp[3])
                        dve.scalar_tensor_tensor(temp[0], ob[(u - 1) % 2], OUT_SLOPE, ob[(u - 1) % 2], ALU.mult, ALU.max)
                        dve.drain()
                        dve.tensor_tensor(d[0], d[0], m[:, 1:G + 1], ALU.subtract)
                        dve.tensor_tensor(mean_xl[u % 2], temp[2], temp[3], ALU.mult)
                        dve.tensor_tensor(yt[u % 2], temp[0], d1t_late[(u - 7) % 4], ALU.add)
                        ln_statistics(dve, (yn[(u - 1) % 2],), var_ready)
                        ln_shift(dve, K, u, t, rstd_ready)
                        ln_apply_dve(dve, d2[(u - 9) % 4], yn[(u - 1) % 2], 0, u).then_inc(dve_step, 1)

                    steps_of(dve, body, STEPS)

                @block.tensor
                def _(pe):
                    pe.sem_inc(pe_step, 1)

                    def product(to, parts):
                        for n, (weights, turned) in enumerate(parts):
                            last = pe.matmul(to[:], w[weights][:], turned, start=n == 0, stop=n == len(parts) - 1)
                        return last

                    def body(t, u):
                        await_step(pe, t, every)
                        turn(pe, b_xs, xs[u % 4]).then_inc(xs_out, 1)
                        product(b_u, (("Wl", xst[(u - 1) % 4]), ("Wr", d1t[(u - 1) % 4]))).then_inc(u_out, 1)
                        product(b_v, (("Wlr", d1t[(u - 1) % 4]),)).then_inc(v_out, 1)
                        product(b_xl, (("Wl", xst[(u - 2) % 4]),)).then_inc(xl_out, 1)
                        product(b_own, (("Wl", d1t[(u - 2) % 4]),)).then_inc(own_out, 1)
                        product(b_own_logit, (("att_relu", v_relu[(u - 1) % 2]),
                                              ("att_lin", v_lin[(u - 1) % 2]))).then_inc(own_logit_out, 1)
                        product(b_logit[u % 2], (("att_relu", u_relu[(u - 1) % 2]), ("att_lin", u_lin[(u - 1) % 2])))
                        pe.wait_ge(b0_free, t + 1)
                        turn(pe, b_xs, yt[(u - 1) % 2]).then_inc(y_out, 1)
                        pe.wait_ge(y_out, t + 1)
                        pe.sem_inc(pe_step, 1)

                    steps_of(pe, body, STEPS)

        def pass_l2():
            new = Rings()
            xd, xd_late, source, summed = (new(4) for _ in range(4))
            xdt, hidden, msg = (new(2) for _ in range(3))
            at = new(2 * K)
            same = [at[0:K], at[K:2 * K]]
            unused = new(1)[0]
            b_xd, b_hidden, b_gate, b_sum = bank[0], bank[1], bank[2], bank[3]
            every = engine_steps("l2")
            sp_step, pool_step, act_step, dve_step, pe_step = every
            xd_out, hidden_out, gate_out, sum_out = (
                sem(f"l2_{n}") for n in ("dst_turned", "hidden_done", "gate_done", "sum_done"))
            src_copied = sem("l2_src_copied")
            STEPS = round_up(GROUPS + 5 + 1, UNROLL)
            RANGE = full_range(GROUPS, 5)
            with nc.Block() as block:
                @block.sync
                def _(sp):
                    sp_program(sp, every, "l2", GROUPS, [(3, source, load_mask("source"))], [], STEPS, *RANGE)

                @block.gpsimd
                def _(pool):
                    pool_program(pool, every, "l2", GROUPS, [(xd, tables[1], dst_index)], (5, summed, readout),
                                 STEPS, *RANGE, 0, None, None, add_index=add_now)

                @block.scalar
                def _(act):
                    act.sem_inc(act_step, 1)

                    def body(t, u):
                        await_step(act, t, every)
                        act.activation(xd_late[(u - 1) % 4], xd[(u - 1) % 4], ACT.Copy)
                        act.wait_ge(xd_out, t + 1)
                        act.activation(xdt[u % 2], b_xd[:], ACT.Copy)
                        act.wait_ge(hidden_out, t + 1)
                        act.activation(hidden[u % 2][0:H, :], b_hidden[0:H, :], ACT.Tanh, bias=col["b_sim"][:])
                        act.wait_ge(gate_out, t + 1)
                        act.activation(gate[u % 2][:], b_gate[:, 0:K], ACT.Sigmoid, bias=col["b_vec"][:])
                        act.wait_ge(sum_out, t + 1)
                        act.activation(summed[(u - 4) % 4], b_sum[:], ACT.Copy).then_inc(act_step, 1)

                    steps_of(act, body, STEPS)

                @block.vector
                def _(dve):
                    dve.sem_inc(dve_step, 1)

                    def body(t, u):
                        await_step(dve, t, every)
                        last_group = GROUPS - 1
                        b = (min(max(t - 3, 0), last_group) if isinstance(t, int) else t - 3)
                        dve.tensor_copy(src_now[:], src_value[:, bass.ds(b * K, K)])
                        for k in range(K):
                            dve.tensor_scalar(tiles(msg[u % 2])[k], tiles(xd_late[(u - 3) % 4])[k],
                                              gate[(u - 1) % 2][:, k:k + 1], None, ALU.mult)
                        dve.drain()
                        for k in range(K):
                            dve.tensor_scalar(same[u % 2][k], source[(u - 3) % 4], src_now[:, k:k + 1], None,
                                              ALU.is_equal)
                        dve.drain()
                        for k in range(K):
                            dve.scalar_tensor_tensor(unused, same[u % 2][k], 1.0, earlier[:, k, :], ALU.mult,
                                                     ALU.mult, accum_out=repeats[:, k:k + 1])
                            dve.drain()
                        dve.tensor_scalar(repeats[:], repeats[:], 0.0, None, ALU.is_gt)
                        dve.tensor_tensor(detour[:], spare_row[:], src_now[:], ALU.subtract)
                        dve.drain()
                        dve.tensor_tensor(detour[:], detour[:], repeats[:], ALU.mult)
                        dve.drain()
                        dve.tensor_tensor(add_now[(u - 3) % 4][:], detour[:], src_now[:], ALU.add).then_inc(dve_step, 1)

                    dma_steps(dve, body, (), STEPS, *RANGE)

                @block.tensor
                def _(pe):
                    pe.sem_inc(pe_step, 1)

                    def body(t, u):
                        await_step(pe, t, every)
                        turn(pe, b_xd, xd[u % 4]).then_inc(xd_out, 1)
                        pe.matmul(b_hidden[0:H, :], w["W_sim"][:], xdt[(u - 1) % 2], start=True,
                                  stop=True).then_inc(hidden_out, 1)
                        for k in range(K):
                            last = pe.matmul(b_gate[:, k:k + 1], hidden[(u - 1) % 2][0:H, k * P:(k + 1) * P],
                                             col["w_vec"][:], start=True, stop=True)
                        last.then_inc(gate_out, 1)
                        for m in range(K):
                            for k in range(K):
                                last = pe.matmul(tiles(b_sum)[m], tiles(same[(u - 1) % 2][k])[m],
                                                 tiles(msg[(u - 1) % 2])[k], start=k == 0, stop=k == K - 1)
                        last.then_inc(sum_out, 1)
                        pe.wait_ge(sum_out, t + 1)
                        pe.sem_inc(pe_step, 1)

                    steps_of(pe, body, STEPS)

        def pass_l3():
            new = Rings()
            xs, attr, d3, goes_on, d3_late, d3t, res = (new(4) for _ in range(7))
            xst, attrt, m1, total, degree, mean, h, y5 = (new(2) for _ in range(8))
            ones, y4, n4, scaled, count = (new(1)[0] for _ in range(5))
            b_xs, b_msg1, b_d3, b_msg, b_u, b_delta = bank[0], bank[1], bank[2], bank[3:5], bank[5], bank[6:8]
            every = engine_steps("l3")
            sp_step, pool_step, act_step, dve_step, pe_step = every
            xs_out, attr_out, attr_free, d3_out, m1_out, u_out = (
                sem(f"l3_{n}") for n in ("src_turned", "attr_turned", "attr_copied", "dst_turned", "msg1_done",
                                         "upd1_done"))
            var_ready, rstd_ready = sem("l3_var"), sem("l3_rstd")
            STEPS = round_up(GROUPS + 8 + 1, UNROLL)
            RANGE = full_range(GROUPS, 8)
            with nc.Block() as block:
                @block.sync
                def _(sp):
                    sp_program(sp, every, "l3", GROUPS,
                               [(0, attr, load_edges(v["edge_attr_64"], H)), (3, goes_on, load_mask("goes_on")),
                                (6, d3_late, load_edges(dst3))],
                               [(0, d3, load_edges(dst3))], STEPS, *RANGE)

                @block.gpsimd
                def _(pool):
                    pool_program(pool, every, "l3", GROUPS, [(xs, tables[2], src_index), (d3, tables[2], dst_index)], (8, res, out),
                                 STEPS, *RANGE, 2, var_ready, rstd_ready)

                @block.scalar
                def _(act):
                    act.sem_inc(act_step, 1)

                    def body(t, u):
                        await_step(act, t, every)
                        act.wait_ge(xs_out, t + 1)
                        act.activation(xst[u % 2], b_xs[:], ACT.Copy)
                        act.wait_ge(attr_out, t + 1)
                        act.activation(attrt[u % 2][0:H, :], b_msg1[0:H, :], ACT.Copy).then_inc(attr_free, 1)
                        act.wait_ge(d3_out, t + 1)
                        act.activation(d3t[(u - 1) % 4], b_d3[:], ACT.Copy)
                        act.wait_ge(u_out, t + 1)
                        act.activation(h[u % 2], b_u[:], ACT.Relu, bias=col["upd_c_edge"][:])
                        act.wait_ge(m1_out, t + 1)
                        act.activation(m1[u % 2], b_msg1[:], ACT.Relu, bias=col["msg_c"][:]).then_inc(act_step, 1)

                    steps_of(act, body, STEPS)

                @block.vector
                def _(dve):
                    dve.memset(ones, 1.0).then_inc(dve_step, 1)

                    def body(t, u):
                        await_step(dve, t, every)
                        dve.tensor_tensor_scan(total[u % 2], goes_on[(u - 3) % 4], b_msg[(u - 1) % 2][:],
                                               total[(u - 1) % 2][:, G - 1:G], ALU.mult, ALU.add)
                        dve.tensor_tensor_scan(degree[u % 2], goes_on[(u - 3) % 4], ones,
                                               degree[(u - 1) % 2][:, G - 1:G], ALU.mult, ALU.add)
                        dve.tensor_tensor(y4, d3_late[(u - 6) % 4], b_delta[(u - 1) % 2][:], ALU.add)
                        dve.drain()
                        dve.tensor_scalar(count, degree[u % 2], 1.0, None, ALU.max)
                        ln_statistics(dve, (y4, y5[(u - 7) % 2]), var_ready)
                        dve.reciprocal(count, count)
                        ln_shift(dve, 2 * K, u, t, rstd_ready)
                        dve.tensor_tensor(mean[u % 2], total[u % 2], count, ALU.mult)
                        ln_apply_dve(dve, n4, y4, 0, u)
                        ln_apply_dve(dve, res[(u - 7) % 4], y5[(u - 7) % 2], 1, u)
                        dve.drain()
                        dve.tensor_tensor(scaled, n4, wide["gamma"][:], ALU.mult)
                        dve.tensor_tensor(y4, d3_late[(u - 6) % 4], wide["beta"][:], ALU.add)
                        dve.drain()
                        dve.tensor_tensor(y5[(u - 6) % 2], scaled, y4, ALU.add).then_inc(dve_step, 1)

                    steps_of(dve, body, STEPS)

                @block.tensor
                def _(pe):
                    pe.sem_inc(pe_step, 1)

                    def body(t, u):
                        await_step(pe, t, every)
                        turn(pe, b_xs, xs[u % 4]).then_inc(xs_out, 1)
                        turn(pe, b_msg1, attr[u % 4], H).then_inc(attr_out, 1)
                        turn(pe, b_d3, d3[(u - 1) % 4]).then_inc(d3_out, 1)
                        pe.matmul(b_u[:], w["upd1x"][:], d3t[(u - 4) % 4], start=True, stop=False)
                        pe.matmul(b_u[:], w["upd1a"][:], mean[(u - 1) % 2], start=False, stop=True).then_inc(u_out, 1)
                        pe.wait_ge(attr_free, t + 1)
                        pe.matmul(b_msg1[:], w["msg1x"][:], xst[(u - 1) % 2], start=True, stop=False)
                        pe.matmul(b_msg1[:], w["msg1e"][:], attrt[(u - 1) % 2][0:H, :], start=False,
                                  stop=True).then_inc(m1_out, 1)
                        pe.matmul(b_msg[u % 2][:], w["msg2"][:], m1[(u - 1) % 2], start=True, stop=True)
                        natural_product(pe, b_delta[u % 2], h[(u - 1) % 2], w["upd2"],
                                        row["upd_b2"]).then_inc(pe_step, 1)

                    steps_of(pe, body, STEPS)

        prepare()
        pass_nodes_a()
        pass_l0()
        pass_back()
        pass_l1()
        pass_l2()
        pass_nodes_b()
        pass_l3()


_N, _D = 100000, 128
_OUTS = [((_N, _D), 'float32')]


def kernel(**inputs):
    import numpy as _np
    import concourse.bacc as _bacc
    from concourse import mybir as _mybir
    from concourse.bass_utils import run_bass_kernel_spmd as _run

    group = 512
    src, dst = _np.asarray(inputs["src"]), _np.asarray(inputs["dst"])
    edges = src.shape[0]
    groups = -(-edges // group)
    pad = groups * group - edges
    src_pad = _np.concatenate([src, _np.full(pad, _N + group, src.dtype)])
    dst_pad = _np.concatenate([_np.full(1, -1, dst.dtype), dst, _np.full(pad + 1, _N, dst.dtype)])
    laid = {
        "src_tiles": src_pad.reshape(-1, 128).T,
        "src_rows": src_pad.reshape(-1, group),
        "dst_tiles": dst_pad[1:-1].reshape(-1, 128).T,
        "dst_next_tiles": dst_pad[2:].reshape(-1, 128).T,
        "dst_windows": _np.lib.stride_tricks.sliding_window_view(dst_pad, group + 2)[::group],
    }
    for name, a in inputs.items():
        if name in ("src", "dst", "edge_attr_16"):
            continue
        a = _np.asarray(a)
        if name == "edge_attr_64":
            a = _np.concatenate([a, _np.zeros((pad, a.shape[1]), a.dtype)])
        laid[name] = a

    nc = _bacc.Bacc("TRN2", target_bir_lowering=False, num_devices=1)
    arrays, views = {}, {}
    for name, a in laid.items():
        a = _np.ascontiguousarray(a)
        arrays[f"in_{name}_dram"] = a
        views[name] = nc.dram_tensor(f"in_{name}_dram", a.shape, _mybir.dt.from_np(a.dtype), kind="ExternalInput").ap()
    outs = [nc.dram_tensor(f"out_{i}_dram", shape, _mybir.dt.from_np(_np.dtype(dtype)), kind="ExternalOutput").ap()
            for i, (shape, dtype) in enumerate(_OUTS)]
    build(nc, views, outs[0])
    r = _run(nc, [arrays], core_ids=[0])
    return r.results[0]["out_0_dram"]
```

```python
import concourse.bass as bass
from concourse import mybir
from contextlib import ExitStack

F32 = mybir.dt.float32
I32 = mybir.dt.int32
BF16 = mybir.dt.bfloat16
ALU = mybir.AluOpType
ACT = mybir.ActivationFunctionType

P = 128
D = 128
K = 4
G = K * P
H = 64
UNROLL = 4
EPS = 1e-5
BIG = 1e38
NOWHERE = 1 << 20
ATT_SLOPE = 0.2
OUT_SLOPE = 0.01


def round_up(n, m):
    return -(-n // m) * m


class Tally:

    def __init__(self, sems, per_step):
        self.sems, self.per_step, self.count, self.into = sems, per_step, [0, 0], 0

    def add(self, parity):
        self.count[parity] += 1
        return self.sems[parity]

    def enter(self, i, first):
        self.into = (i - first) * (UNROLL // 2 * self.per_step * 16 // UNROLL)

    def leave(self, trips):
        self.into = 0
        for parity in range(2):
            self.count[parity] += (trips - 1) * (UNROLL // 2) * self.per_step

    def wait(self, eng, parity):
        if self.count[parity]:
            eng.wait_ge(self.sems[parity], self.into + 16 * self.count[parity])


def dma_steps(eng, body, tallies, steps, first, last):
    for t in range(first):
        body(t, t % UNROLL)
    with eng.Fori(first, last - UNROLL + 1, UNROLL) as i:
        for tally in tallies:
            tally.enter(i, first)
        for u in range(UNROLL):
            body(i + u, u)
    for tally in tallies:
        tally.leave((last - first) // UNROLL)
    for t in range(last, steps):
        body(t, t % UNROLL)


def steps_of(eng, body, steps):
    with eng.Fori(0, steps - UNROLL + 1, UNROLL) as i:
        for u in range(UNROLL):
            body(i + u, u)


def await_step(eng, t, step_sems):
    for s in step_sems:
        eng.wait_ge(s, t + 1)


def tiles(buf):
    return [buf[:, k * P:(k + 1) * P] for k in range(K)]


def build(nc, v, out):
    N = v["x"].shape[0]
    GROUPS = v["dst_windows"].shape[0]
    NODE_GROUPS = -(-N // G)

    ctx = ExitStack()
    with ctx:
        def sb(name, shape, dt=F32):
            return ctx.enter_context(nc.sbuf_tensor(name, shape, dt))

        def sem(name):
            return ctx.enter_context(nc.semaphore(name))

        def pair(name):
            return [sem(f"{name}_even"), sem(f"{name}_odd")]

        def dram(name, shape):
            return nc.dram_tensor(name, shape, F32, kind="Internal").ap()

        tables = [dram(f"state_{n}", (N, D)) for n in (1, 2, 3)]
        dst1_turned = dram("dst1_turned", (GROUPS, P, G))
        dst1_filled = dram("dst1_filled", (GROUPS, P, G))
        dst3 = dram("dst_state_3", (GROUPS * G, D))
        edge_x = [dram(f"x_at_{n}", (GROUPS * 2 * P, G // 2)) for n in ("src", "dst")]
        readout = dram("readout", (N + 2 * G, D))
        MASKS = ("goes_on", "restart", "is_last", "not_last")
        mask_rows = {m: dram(m, (GROUPS, G)) for m in (*MASKS, "source")}

        RING = 74
        arena = sb("arena", [P, RING * G])
        bank = [ctx.enter_context(nc.psum_tensor(f"bank{i}", [P, G], F32)) for i in range(8)]

        class Rings:

            def __init__(self):
                self.used = 0

            def __call__(self, n):
                at = [arena[:, (self.used + i) * G:(self.used + i + 1) * G] for i in range(n)]
                self.used += n
                assert self.used <= RING - 4
                return at

        restart = [arena[:, i * G:(i + 1) * G] for i in range(RING - 4, RING)]
        ident = sb("ident", [P, P])
        half_neg = sb("half_neg", [P, 3 * K])
        w = {}
        for name in ("Wl", "Wr", "Wlr", "W_self", "W_nbr", "Wlin", "att_relu", "att_lin", "msg1x", "msg2",
                     "upd1x", "upd1a", "upd2"):
            w[name] = sb("w_" + name, [P, P])
        w["W_sim"] = sb("w_W_sim", [P, H])
        w["W1"] = sb("w_W1", [P, H])
        for name in ("W2", "msg1e", "msg1g", "upd1g"):
            w[name] = sb("w_" + name, [H, P])
        col = {}
        for name in ("L0_b", "bl", "br", "bias", "b_vec", "msg_b1", "msg_b2", "upd_b1", "bl_br", "bl_bias",
                     "msg_c", "upd_c_node", "upd_c_edge", "att"):
            col[name] = sb("c_" + name, [P, 1])
        for name in ("b_sim", "b1", "glob", "w_vec"):
            col[name] = sb("c_" + name, [H, 1])
        row = {}
        for name in ("xl_bias", "xl_bias_lin", "b2", "upd_b2"):
            row[name] = sb("r_" + name, [96, G], BF16)
        selector = sb("selector", [96, P], BF16)
        wide = {}
        for name in ("gamma", "beta"):
            wide[name] = sb("n_" + name, [P, G])
        src_index = sb("src_index", [P, GROUPS * K], I32)
        dst_index = sb("dst_index", [P, GROUPS * K], I32)
        src_value = sb("src_value", [P, GROUPS * K])
        spare_row = sb("spare_row", [P, K])
        earlier = sb("earlier", [P, K, G])
        put_index = sb("put_index", [P, GROUPS * K], I32)
        index_now = [sb(f"index_now{i}", [P, 2 * K], I32) for i in range(2)]
        put_now = [sb(f"put_now{i}", [P, K], I32) for i in range(2)]
        add_now = [sb(f"add_now{i}", [P, K], I32) for i in range(4)]
        src_now = sb("src_now", [P, K])
        repeats = sb("repeats", [P, K])
        detour = sb("detour", [P, K])
        gate = [sb(f"gate{i}", [P, K]) for i in range(2)]
        stats = sb("stats", [P, 3 * K, 6])
        gap, spread, gap2, shift = (sb(n, [P, 3 * K]) for n in ("gap", "spread", "gap2", "shift"))
        mean2, var, rstd = ([sb(f"{n}{i}", [P, 3 * K]) for i in range(2)] for n in ("mean2", "var", "rstd"))
        max_run = [sb(f"max_run{i}", [P, G + 1]) for i in range(2)]

        def prepare():
            loads = sem("weights_loaded")
            idm = sem("identity_made")
            ready = sem("operands_ready")
            products = sem("products_ready")
            made = sem("prep_made")
            stored = sem("masks_stored")
            W0 = arena[:, 0:2 * P]
            win_i = sb("windows", [GROUPS, G + 2], I32)
            dst_next = sb("dst_next", [P, GROUPS * K], I32)
            differs = sb("differs", [P, GROUPS * K])
            mask = {m: arena[0:GROUPS, (i + 1) * G:(i + 2) * G] for i, m in enumerate((*MASKS, "source"))}
            r = {n: sb("raw_" + n, [96, P]) for n in ("bl", "bias", "b2", "upd_b2")}
            bias_row = {n: sb("bias_" + n, [96, P]) for n in ("xl_bias", "xl_bias_lin")}
            part = {n: [sb(f"part{i}_{n}", [96, P], BF16) for i in range(3)] for n in row}
            rest = {n: [sb(f"rest{i}_{n}", [96, P]) for i in range(2)] for n in row}
            src_i = sb("src_row_i", [GROUPS, G], I32)
            ones_wide = sb("ones_wide", [P, P])
            att_s = sb("att_s", [P, 2])
            raw_gamma, raw_beta = sb("raw_gamma", [P, P]), sb("raw_beta", [P, P])

            def as_col(a):
                return a.rearrange("(p a) -> p a", a=1)

            def as_row(a):
                return a.rearrange("(a p) -> a p", a=1)

            pieces = [
                (W0, v["L0_gnn_W"]), (w["Wl"][:], v["L1_gnn_Wl"]), (w["Wr"][:], v["L1_gnn_Wr"]),
                (w["W_sim"][:], v["L2_gnn_W_sim"]), (w["W1"][:], v["L2_gnn_W1"]), (w["W2"][:], v["L2_gnn_W2"]),
                (w["msg1x"][:], v["L3_gnn_msg_w1"][0:D, :]), (w["msg1e"][:], v["L3_gnn_msg_w1"][D:D + H, :]),
                (w["msg1g"][:], v["L3_gnn_msg_w1"][D + H:D + 2 * H, :]), (w["msg2"][:], v["L3_gnn_msg_w2"]),
                (w["upd1x"][:], v["L3_gnn_upd_w1"][0:D, :]), (w["upd1a"][:], v["L3_gnn_upd_w1"][D:2 * D, :]),
                (w["upd1g"][:], v["L3_gnn_upd_w1"][2 * D:2 * D + H, :]), (w["upd2"][:], v["L3_gnn_upd_w2"]),
                (col["L0_b"][:], as_col(v["L0_gnn_b"])), (col["bl"][:], as_col(v["L1_gnn_bl"])),
                (col["br"][:], as_col(v["L1_gnn_br"])), (col["bias"][:], as_col(v["L1_gnn_bias"])),
                (col["att"][:], as_col(v["L1_gnn_att"])), (col["b_sim"][:], as_col(v["L2_gnn_b_sim"])),
                (col["b1"][:], as_col(v["L2_gnn_b1"])), (col["w_vec"][:], v["L2_gnn_w_vec"]),
                (col["b_vec"][:], as_row(v["L2_gnn_b_vec"]).to_broadcast([P, 1])),
                (col["glob"][:], as_col(v["L3_gnn_global_state"])), (col["msg_b1"][:], as_col(v["L3_gnn_msg_b1"])),
                (col["msg_b2"][:], as_col(v["L3_gnn_msg_b2"])), (col["upd_b1"][:], as_col(v["L3_gnn_upd_b1"])),
                (r["bl"][:], as_row(v["L1_gnn_bl"]).to_broadcast([96, P])),
                (r["bias"][:], as_row(v["L1_gnn_bias"]).to_broadcast([96, P])),
                (r["b2"][:], as_row(v["L2_gnn_b2"]).to_broadcast([96, P])),
                (r["upd_b2"][:], as_row(v["L3_gnn_upd_b2"]).to_broadcast([96, P])),
                (raw_gamma[:], as_row(v["L3_gnn_ln_gamma"]).to_broadcast([P, P])),
                (raw_beta[:], as_row(v["L3_gnn_ln_beta"]).to_broadcast([P, P])),
                (win_i[:], v["dst_windows"]), (src_index[:], v["src_tiles"]), (dst_index[:], v["dst_tiles"]),
                (dst_next[:], v["dst_next_tiles"]), (src_i[:], v["src_rows"]),
            ]
            with nc.Block() as block:
                @block.sync
                def _(sp):
                    for to, of in pieces:
                        sp.dma_start(to, of).then_inc(loads, 16)
                    sp.wait_ge(made, 2)
                    for m in mask_rows:
                        sp.dma_start(mask_rows[m], mask[m]).then_inc(stored, 16)
                    sp.wait_ge(stored, 16 * len(mask_rows))

                @block.gpsimd
                def _(pool):
                    pool.memset(ident[:], 0.0).then_inc(idm, 1)
                    pool.wait_ge(idm, 1)
                    pool.affine_select(out=ident[:], in_=ident[:], compare_op=ALU.not_equal, fill=1.0, base=0,
                                       pattern=[[-1, P]], channel_multiplier=1).then_inc(idm, 1)
                    pool.iota(spare_row[:], pattern=[[P, K]], base=N, channel_multiplier=1,
                              allow_small_or_imprecise_dtypes=True)
                    pool.memset(earlier[:], 1.0).then_inc(idm, 1)
                    pool.wait_ge(idm, 3)
                    pool.affine_select(out=earlier[:], in_=earlier[:], compare_op=ALU.is_gt, fill=0.0, base=0,
                                       pattern=[[P, K], [-1, G]], channel_multiplier=1).then_inc(idm, 1)

                @block.vector
                def _(dve):
                    dve.memset(selector[:], 0.0)
                    dve.memset(ones_wide[:], 1.0)
                    dve.memset(half_neg[:], -0.5)
                    for b in bank:
                        dve.memset(b[:], 0.0)
                    for i in range(2):
                        dve.memset(gate[i][:], 0.0)
                        dve.memset(max_run[i][:], 0.0)
                    for i in range(2):
                        dve.memset(mean2[i][:], 0.0)
                        dve.memset(var[i][:], 1.0)
                        dve.memset(rstd[i][:], 1.0)
                    dve.wait_ge(loads, 16 * len(pieces))
                    dve.wait_ge(idm, 4)
                    dve.drain()
                    for i in range(3):
                        dve.memset(selector[32 * i:32 * i + 1, :], 1.0)
                    dve.tensor_scalar(att_s[:, 0:1], col["att"][:], 1.0 - ATT_SLOPE, None, ALU.mult)
                    dve.tensor_scalar(att_s[:, 1:2], col["att"][:], ATT_SLOPE, None, ALU.mult).then_inc(ready, 1)
                    dve.drain()
                    dve.tensor_scalar(w["att_relu"][:], ones_wide[:], att_s[:, 0:1], None, ALU.mult)
                    dve.tensor_scalar(w["att_lin"][:], ones_wide[:], att_s[:, 1:2], None, ALU.mult)
                    dve.tensor_tensor(w["Wlr"][:], w["Wl"][:], w["Wr"][:], ALU.add)
                    dve.scalar_tensor_tensor(w["Wlin"][:], w["Wl"][:], OUT_SLOPE, ident[:], ALU.mult, ALU.add)
                    dve.tensor_tensor(col["bl_br"][:], col["bl"][:], col["br"][:], ALU.add)
                    dve.tensor_tensor(col["bl_bias"][:], col["bl"][:], col["bias"][:], ALU.add)
                    for k in range(K):
                        at = slice(k * P, (k + 1) * P)
                        dve.tensor_copy(wide["gamma"][:, at], raw_gamma[:])
                        dve.tensor_copy(wide["beta"][:, at], raw_beta[:])
                    dve.tensor_tensor(bias_row["xl_bias"][:], r["bl"][:], r["bias"][:], ALU.add)
                    dve.drain()
                    dve.tensor_scalar(bias_row["xl_bias_lin"][:], bias_row["xl_bias"][:], OUT_SLOPE, None, ALU.mult)
                    dve.drain()
                    left = {n: bias_row.get(n, r.get(n)) for n in row}
                    for i in range(3):
                        for n in row:
                            dve.tensor_copy(part[n][i][:], left[n][:])
                        dve.drain()
                        for n in row:
                            for k in range(K):
                                at = slice(k * P, (k + 1) * P)
                                dve.tensor_copy(row[n][32 * i:32 * i + 32, at], part[n][i][32 * i:32 * i + 32, :])
                            if i < 2:
                                dve.tensor_tensor(rest[n][i][:], left[n][:], part[n][i][:], ALU.subtract)
                                left[n] = rest[n][i]
                        dve.drain()
                    dve.tensor_copy(mask["source"], src_i[:])
                    dve.tensor_tensor(mask["goes_on"], win_i[:, 1:G + 1], win_i[:, 0:G], ALU.is_equal)
                    dve.tensor_tensor(mask["not_last"], win_i[:, 1:G + 1], win_i[:, 2:G + 2], ALU.is_equal)
                    dve.tensor_tensor(differs[:], dst_index[:], dst_next[:], ALU.not_equal)
                    dve.drain()
                    dve.tensor_scalar(mask["restart"], mask["goes_on"], -1.0, BIG, ALU.add, ALU.mult)
                    dve.tensor_scalar(mask["is_last"], mask["not_last"], -1.0, 1.0, ALU.mult,
                                      ALU.add).then_inc(made, 2)
                    dve.scalar_tensor_tensor(put_index[:], dst_index[:], -float(NOWHERE), differs[:], ALU.add, ALU.mult)
                    dve.drain()
                    dve.tensor_scalar(put_index[:], put_index[:], float(NOWHERE), None, ALU.add)
                    dve.tensor_scalar(dst_index[:], dst_index[:], float(N - 1), None, ALU.min)
                    dve.tensor_copy(src_value[:], src_index[:])
                    dve.drain()
                    dve.tensor_scalar(src_index[:], src_index[:], float(N - 1), None, ALU.min)
                    dve.wait_ge(products, 1)
                    dve.tensor_copy(w["W_nbr"][:], bank[1][:, 0:P])
                    dve.tensor_tensor(col["msg_c"][:], bank[2][:, 0:1], col["msg_b1"][:], ALU.add)
                    dve.tensor_tensor(col["upd_c_node"][:], bank[3][:, 0:1], col["upd_b1"][:], ALU.add)
                    dve.drain()
                    dve.scalar_tensor_tensor(w["W_self"][:], bank[0][:, 0:P], 1.0, w["W_nbr"][:], ALU.mult, ALU.subtract)
                    dve.tensor_tensor(col["upd_c_edge"][:], bank[4][:, 0:1], col["upd_c_node"][:], ALU.add)
                    dve.drain()
                    dve.tensor_tensor(w["W_self"][:], w["W_self"][:], ident[:], ALU.add)
                    dve.drain()

                @block.tensor
                def _(pe):
                    pe.wait_ge(ready, 1)
                    pe.transpose(bank[0][:, 0:P], W0[:, 0:P], ident[:])
                    pe.transpose(bank[1][:, 0:P], W0[:, P:2 * P], ident[:])
                    pe.matmul(bank[2][:, 0:1], w["msg1g"][:], col["glob"][:], start=True, stop=True)
                    pe.matmul(bank[3][:, 0:1], w["upd1g"][:], col["glob"][:], start=True, stop=True)
                    pe.matmul(bank[4][:, 0:1], w["upd1a"][:], col["msg_b2"][:], start=True, stop=True).then_inc(products, 1)

        def group_rows(table, b):
            base = min(b * G, N - G) if isinstance(b, int) else b * G
            return table[bass.ds(base, G), :].rearrange("(p k) f -> p (k f)", k=K)

        def edge_rows(table, b):
            return table[bass.ds(b * G, G), :].rearrange("(k p) f -> p k f", p=P)

        def as_tiles(buf):
            return buf.rearrange("p (k f) -> p k f", k=K)

        def turned_group(table, b):
            return table[bass.ds(b, 1), :, :].rearrange("a p e -> (a p) e")

        def load_edge_x(table):
            return lambda buf, b: (buf.rearrange("p (h f) -> p h f", h=2),
                                   table[bass.ds(b * 2 * P, 2 * P), :].rearrange("(h p) f -> p h f", p=P))

        def mask_group(m, b):
            return mask_rows[m][bass.ds(b, 1), :].to_broadcast([P, G])

        def ln_stats(dve, buf, at):
            for k, tile in enumerate(tiles(buf)):
                dve.bn_stats(stats[:, at * K + k, :], tile)

        def ln_variance(dve, n, u):
            dve.drain()
            dve.tensor_tensor(gap[:, 0:n], stats[:, 0:n, 1], stats[:, 0:n, 4], ALU.subtract)
            dve.scalar_tensor_tensor(spread[:, 0:n], stats[:, 0:n, 2], D * EPS, stats[:, 0:n, 5], ALU.add, ALU.add)
            dve.tensor_tensor(mean2[u % 2][:, 0:n], stats[:, 0:n, 1], stats[:, 0:n, 4], ALU.add)
            dve.drain()
            dve.scalar_tensor_tensor(gap2[:, 0:n], gap[:, 0:n], 0.25, gap[:, 0:n], ALU.mult, ALU.mult)
            dve.drain()
            return dve.scalar_tensor_tensor(var[u % 2][:, 0:n], spread[:, 0:n], 1.0 / D, gap2[:, 0:n], ALU.mult,
                                            ALU.add)

        def ln_power(pool, n, u):
            return pool.tensor_tensor(rstd[u % 2][:, 0:n], var[(u - 1) % 2][:, 0:n], half_neg[:, 0:n], ALU.pow)

        def ln_shift(dve, n, u, ago=2):
            made = dve.scalar_tensor_tensor(shift[:, 0:n], mean2[(u - ago) % 2][:, 0:n], -0.5,
                                            rstd[(u - ago + 1) % 2][:, 0:n], ALU.mult, ALU.mult)
            dve.drain()
            return made

        def ln_apply_dve(dve, to, of, at, u, ago=2, some=range(K)):
            for k in some:
                c = at * K + k
                last = dve.tensor_scalar(tiles(to)[k], tiles(of)[k], rstd[(u - ago + 1) % 2][:, c:c + 1],
                                         shift[:, c:c + 1], ALU.mult, ALU.add)
            return last

        def ln_apply_act(act, to, of, at, u, ago=2, some=range(K)):
            for k in some:
                c = at * K + k
                last = act.activation(tiles(to)[k], tiles(of)[k], ACT.Identity, bias=shift[:, c:c + 1],
                                      scale=rstd[(u - ago + 1) % 2][:, c:c + 1])
            return last

        def turn(pe, to, of, width=D):
            for k in range(K):
                last = pe.transpose(to[0:width, k * P:(k + 1) * P], of[:, k * width:(k + 1) * width], ident[:])
            return last

        def natural_product(pe, to, turned, weight, bias_row):
            rows = weight.shape[0]
            pe.matmul(to[:], selector[:], bias_row[:], start=True, stop=False, skip_group_check=True)
            for k in range(K):
                last = pe.matmul(to[:, k * P:(k + 1) * P], turned[0:rows, k * P:(k + 1) * P], weight[:],
                                 start=False, stop=k == K - 1, skip_group_check=True)
            return last

        def engine_steps(name, *engines):
            return [sem(f"{name}_{e}_step") for e in engines or ("sp", "pool", "act", "dve", "pe")]

        def sp_program(sp, every, name, groups, loads, stores, steps, first_full, end_full):
            loaded = Tally(pair(f"{name}_loaded"), len(loads))
            stored = Tally(pair(f"{name}_stored"), len(stores))
            waited = sem(f"{name}_sp_waited")

            def start_loads(t, u):
                for use, ring, source in loads:
                    b = t + 2 - use
                    if not isinstance(t, int) or 0 <= b < groups:
                        to, of = source(ring[(u + 2 - use) % 4], b)
                        sp.dma_start(to, of).then_inc(loaded.add(u % 2), 16)

            def body(t, u):
                await_step(sp, t, every)
                sp.sem_inc(waited, 1)
                start_loads(t, u)
                stored.wait(sp, (u - 1) % 2)
                sp.sem_inc(waited, 1)
                for lag, ring, place in stores:
                    b = t - lag
                    if not isinstance(t, int) or 0 <= b < groups:
                        of, to = place(ring[(u - lag) % 4], b)
                        sp.dma_start(to, of).then_inc(stored.add(u % 2), 16)
                loaded.wait(sp, (u - 1) % 2)
                sp.sem_inc(every[0], 1)

            start_loads(-2, -2)
            start_loads(-1, -1)
            loaded.wait(sp, 0)
            sp.sem_inc(every[0], 1)
            dma_steps(sp, body, (loaded, stored), steps, first_full, end_full)
            for parity in range(2):
                stored.wait(sp, parity)

        def pool_program(pool, every, name, groups, gathers, scatter, steps, first_full, end_full, norms=0,
                         add_index=None):
            indexed = sem(f"{name}_index_copied")
            checked = sem(f"{name}_index_checked")
            powered = sem(f"{name}_powered")
            gathered = Tally(pair(f"{name}_gathered"), K * len(gathers))
            scattered = Tally(pair(f"{name}_scattered"), K)
            per_step = len(gathers) + (add_index is None)
            at_lag, from_ring, to_table = scatter
            copies = [0, 0]

            def start_gathers(t, u):
                b = t + 2
                if isinstance(t, int) and not b < groups:
                    return
                for n, (ring, table, index) in enumerate(gathers):
                    now = index_now[u % 2][:, n * K:(n + 1) * K]
                    pool.tensor_copy(now, index[:, bass.ds(b * K, K)]).then_inc(indexed, 1)
                    copied(1)
                    for k in range(K):
                        pool.indirect_dma_start(
                            out=ring[(u + 2) % 4][:, k * P:(k + 1) * P], out_offset=None, in_=table,
                            in_offset=bass.IndirectOffsetOnAxis(ap=now[:, k:k + 1], axis=0),
                            bounds_check=N - 1, oob_is_err=False).then_inc(gathered.add(u % 2), 16)

            def copied(n):
                copies[0] += n
                pool.wait_ge(indexed, copies[0] + copies[1])
                pool.sem_inc(checked, 1)

            def body(t, u):
                await_step(pool, t, every)
                if norms:
                    ln_power(pool, norms * K, u).then_inc(powered, 1)
                start_gathers(t, u)
                b = t - at_lag
                if not isinstance(t, int) or 0 <= b < groups:
                    if add_index is None:
                        pool.tensor_copy(put_now[u % 2][:], put_index[:, bass.ds(b * K, K)]).then_inc(indexed, 1)
                        copied(1)
                        for k in range(K):
                            pool.indirect_dma_start(
                                out=to_table,
                                out_offset=bass.IndirectOffsetOnAxis(ap=put_now[u % 2][:, k:k + 1], axis=0),
                                in_=from_ring[(u - at_lag) % 4][:, k * P:(k + 1) * P], in_offset=None,
                                bounds_check=N - 1, oob_is_err=False).then_inc(scattered.add(u % 2), 16)
                    else:
                        scattered.wait(pool, (u - 1) % 2)
                        pool.sem_inc(checked, 1)
                        for k in range(K):
                            pool.indirect_dma_start(
                                out=to_table,
                                out_offset=bass.IndirectOffsetOnAxis(
                                    ap=add_index[(u - at_lag) % 4][:, k:k + 1], axis=0),
                                in_=from_ring[(u - at_lag) % 4][:, k * P:(k + 1) * P], in_offset=None,
                                compute_op=ALU.add).then_inc(scattered.add(u % 2), 16)
                gathered.wait(pool, (u - 1) % 2)
                scattered.wait(pool, (u - 1) % 2)
                if norms:
                    pool.wait_ge(powered, t + 1)
                pool.sem_inc(every[1], 1)

            start_gathers(-2, -2)
            start_gathers(-1, -1)
            gathered.wait(pool, 0)
            pool.sem_inc(every[1], 1)
            for t in range(first_full):
                body(t, t % UNROLL)
            with pool.Fori(first_full, end_full - UNROLL + 1, UNROLL) as i:
                gathered.enter(i, first_full)
                scattered.enter(i, first_full)
                copies[1] = (i - first_full) * per_step
                for u in range(UNROLL):
                    body(i + u, u)
            trips = (end_full - first_full) // UNROLL
            gathered.leave(trips)
            scattered.leave(trips)
            copies[0] += (trips - 1) * UNROLL * per_step
            copies[1] = 0
            for t in range(end_full, steps):
                body(t, t % UNROLL)
            scattered.wait(pool, 0)
            scattered.wait(pool, 1)

        def load_rows(table):
            return lambda buf, b: (buf, group_rows(table, b))

        def load_edges(table, width=D):
            return lambda buf, b: (buf[:, 0:K * width].rearrange("p (k f) -> p k f", k=K), edge_rows(table, b))

        def load_turned(table):
            return lambda buf, b: (buf, turned_group(table, b))

        def load_mask(m):
            return lambda buf, b: (buf, mask_group(m, b))

        def full_range(groups, first_lag, last_ahead=2):
            return round_up(first_lag + 1, UNROLL), (groups - last_ahead) // UNROLL * UNROLL

        def pass_nodes_a():
            assert NODE_GROUPS == UNROLL * GROUPS
            new = Rings()
            at = new(2)
            halves = [(q, at[q // 2][:, q % 2 * G // 2:(q % 2 + 1) * G // 2]) for q in range(UNROLL)]
            x, x1, x2 = (new(4) for _ in range(3))
            x1t, hr, y1 = (new(2) for _ in range(3))
            zeros = new(1)[0]
            b_x1t, b_h, b_lin = bank[0], bank[1], bank[2:4]
            every = engine_steps("na")
            sp_step, pool_step, act_step, dve_step, pe_step = every
            x1t_out, h_out = sem("na_x1_turned"), sem("na_h_done")
            rstd_ready, shift_ready = sem("na_rstd"), sem("na_shift")
            cleared, spare_cleared = sem("arena_cleared"), sem("spare_rows_cleared")
            indexed, checked = sem("na_index_copied"), sem("na_index_checked")
            gathered = Tally(pair("na_gathered"), 2)
            LAST = 6
            ON_DVE, ON_ACT = range(K - 1), range(K - 1, K)
            STEPS = round_up(NODE_GROUPS + LAST + 1, UNROLL)
            RANGE = full_range(NODE_GROUPS, LAST, 3)

            def place_half(quarter, step):
                q, buf = quarter
                return buf, edge_x[q // 2][bass.ds((step - q) * (2 * P // UNROLL) + q % 2 * P, P), :]

            with nc.Block() as block:
                @block.sync
                def _(sp):
                    sp.wait_ge(cleared, 2)
                    for i in range(2):
                        sp.dma_start(readout[N + i * G:N + (i + 1) * G, :].rearrange("(p k) f -> p (k f)", k=K),
                                     zeros).then_inc(spare_cleared, 16)
                    sp_program(sp, every, "na", NODE_GROUPS, [(0, x, load_rows(v["x"]))],
                               [(0, [zeros] * 4, load_rows(readout)), (2, x1, load_rows(tables[0])),
                                (6, x2, load_rows(tables[1])), (2, halves, place_half)], STEPS, *RANGE)
                    sp.wait_ge(spare_cleared, 32)

                @block.gpsimd
                def _(pool):
                    pool.memset(arena[:, RING // 2 * G:], 0.0).then_inc(cleared, 1)
                    pool.sem_inc(pool_step, 1)

                    copies = [0, 0]

                    def body(t, u):
                        await_step(pool, t, every)
                        ln_power(pool, 2 * K, u).then_inc(rstd_ready, 1)
                        if not isinstance(t, int) or t < NODE_GROUPS:
                            index, now = (src_index, dst_index)[u // 2], index_now[0][:, 2 * u:2 * u + 2]
                            pool.tensor_copy(now, index[:, bass.ds(t - u + u % 2 * 2, 2)]).then_inc(indexed, 1)
                            copies[0] += 1
                            pool.wait_ge(indexed, copies[0] + copies[1])
                            pool.sem_inc(checked, 1)
                            for k in range(2):
                                pool.indirect_dma_start(
                                    out=halves[u][1][:, k * P:(k + 1) * P], out_offset=None, in_=v["x"],
                                    in_offset=bass.IndirectOffsetOnAxis(ap=now[:, k:k + 1], axis=0),
                                    bounds_check=N - 1, oob_is_err=False).then_inc(gathered.add(u % 2), 16)
                        gathered.wait(pool, (u - 1) % 2)
                        pool.wait_ge(rstd_ready, t + 1)
                        pool.sem_inc(pool_step, 1)

                    pool.wait_ge(cleared, 2)
                    first, last = RANGE
                    for t in range(first):
                        body(t, t % UNROLL)
                    with pool.Fori(first, last - UNROLL + 1, UNROLL) as i:
                        gathered.enter(i, first)
                        copies[1] = i - first
                        for u in range(UNROLL):
                            body(i + u, u)
                    gathered.leave((last - first) // UNROLL)
                    copies[0] += last - first - UNROLL
                    copies[1] = 0
                    for t in range(last, STEPS):
                        body(t, t % UNROLL)

                @block.scalar
                def _(act):
                    act.sem_inc(act_step, 1)

                    def body(t, u):
                        await_step(act, t, every)
                        act.wait_ge(x1t_out, t + 1)
                        act.activation(x1t[u % 2], b_x1t[:], ACT.Copy)
                        act.wait_ge(h_out, t + 1)
                        act.activation(hr[u % 2], b_h[:], ACT.Relu, scale=1.0 - OUT_SLOPE)
                        act.wait_ge(shift_ready, t + 1)
                        ln_apply_act(act, x1[(u - 1) % 4], x[(u - 1) % 4], 0, u, 1, ON_ACT)
                        ln_apply_act(act, x2[(u - 5) % 4], y1[(u - 5) % 2], 1, u, 1).then_inc(act_step, 1)

                    act.wait_ge(cleared, 2)
                    steps_of(act, body, STEPS)

                @block.vector
                def _(dve):
                    dve.memset(arena[:, 0:RING // 2 * G], 0.0).then_inc(cleared, 1)
                    dve.sem_inc(dve_step, 1)

                    def body(t, u):
                        await_step(dve, t, every)
                        ln_stats(dve, x[u % 4], 0)
                        dve.tensor_tensor(y1[(u - 4) % 2], hr[(u - 1) % 2], b_lin[(u - 1) % 2][:], ALU.add)
                        dve.wait_ge(rstd_ready, t + 1)
                        ln_shift(dve, 2 * K, u, 1).then_inc(shift_ready, 1)
                        ln_apply_dve(dve, x1[(u - 1) % 4], x[(u - 1) % 4], 0, u, 1, ON_DVE)
                        ln_stats(dve, y1[(u - 4) % 2], 1)
                        ln_variance(dve, 2 * K, u).then_inc(dve_step, 1)

                    dve.wait_ge(cleared, 2)
                    steps_of(dve, body, STEPS)

                @block.tensor
                def _(pe):
                    pe.sem_inc(pe_step, 1)

                    def body(t, u):
                        await_step(pe, t, every)
                        turn(pe, b_x1t, x1[(u - 2) % 4]).then_inc(x1t_out, 1)
                        natural_product(pe, b_h, x1t[(u - 1) % 2], w["Wl"], row["xl_bias"]).then_inc(h_out, 1)
                        natural_product(pe, b_lin[u % 2], x1t[(u - 1) % 2], w["Wlin"],
                                        row["xl_bias_lin"]).then_inc(pe_step, 1)

                    pe.wait_ge(cleared, 2)
                    steps_of(pe, body, STEPS)

        def pass_nodes_b():
            new = Rings()
            read, x2, y2, x3, x3b, y4, y5, res = (new(4) for _ in range(8))
            readt, act1, x3t, h3, n4 = (new(2) for _ in range(5))
            scaled_n = new(1)[0]
            b_readt, b_act1, b_prompt, b_x3t, b_u, b_delta = bank[0], bank[1], bank[2:4], bank[4], bank[5], bank[6:8]
            every = engine_steps("nb")
            sp_step, pool_step, act_step, dve_step, pe_step = every
            readt_out, act1_out, x3t_out, u_out = (
                sem(f"nb_{n}") for n in ("readout_turned", "prompt1_done", "x3_turned", "upd1_done"))
            shift_ready, scaled, summed = sem("nb_shift"), sem("nb_scaled"), sem("nb_summed")
            LAST = 16
            STEPS = round_up(NODE_GROUPS + LAST + 1, UNROLL)
            RANGE = full_range(NODE_GROUPS, LAST, 3)
            with nc.Block() as block:
                @block.sync
                def _(sp):
                    sp_program(sp, every, "nb", NODE_GROUPS,
                               [(0, read, load_rows(readout)), (3, x2, load_rows(tables[1]))],
                               [(6, x3, load_rows(tables[2])), (16, res, load_rows(out))], STEPS, *RANGE)

                @block.gpsimd
                def _(pool):
                    pool.sem_inc(pool_step, 1)

                    def body(t, u):
                        await_step(pool, t, every)
                        pool.tensor_tensor(scaled_n, n4[(u - 12) % 2], wide["gamma"][:], ALU.mult).then_inc(scaled, 1)
                        pool.wait_ge(scaled, t + 1)
                        pool.tensor_tensor(y5[(u - 12) % 4], scaled_n, x3b[(u - 12) % 4],
                                           ALU.add).then_inc(summed, 1)
                        ln_power(pool, 3 * K, u)
                        pool.wait_ge(summed, t + 1)
                        pool.tensor_tensor(x3b[(u - 8) % 4], x3[(u - 8) % 4], wide["beta"][:],
                                           ALU.add).then_inc(pool_step, 1)

                    steps_of(pool, body, STEPS)

                @block.scalar
                def _(act):
                    act.sem_inc(act_step, 1)

                    def body(t, u):
                        await_step(act, t, every)
                        act.wait_ge(shift_ready, t + 1)
                        ln_apply_act(act, n4[(u - 11) % 2], y4[(u - 11) % 4], 1, u)
                        act.wait_ge(readt_out, t + 1)
                        act.activation(readt[u % 2], b_readt[:], ACT.Copy)
                        act.wait_ge(x3t_out, t + 1)
                        act.activation(x3t[u % 2], b_x3t[:], ACT.Copy)
                        act.wait_ge(act1_out, t + 1)
                        act.activation(act1[u % 2][0:H, :], b_act1[0:H, :], ACT.Relu, bias=col["b1"][:])
                        act.wait_ge(u_out, t + 1)
                        act.activation(h3[u % 2], b_u[:], ACT.Relu, bias=col["upd_c_node"][:])
                        ln_apply_act(act, res[(u - 15) % 4], y5[(u - 15) % 4], 2, u).then_inc(act_step, 1)

                    steps_of(act, body, STEPS)

                @block.vector
                def _(dve):
                    dve.sem_inc(dve_step, 1)

                    def body(t, u):
                        await_step(dve, t, every)
                        ln_shift(dve, 3 * K, u).then_inc(shift_ready, 1)
                        dve.scalar_tensor_tensor(y2[(u - 3) % 4], x2[(u - 3) % 4], 2.0, b_prompt[(u - 1) % 2][:],
                                                 ALU.mult, ALU.add)
                        dve.tensor_tensor(y4[(u - 9) % 4], x3[(u - 9) % 4], b_delta[(u - 1) % 2][:], ALU.add)
                        ln_stats(dve, y5[(u - 13) % 4], 2)
                        dve.drain()
                        ln_apply_dve(dve, x3[(u - 5) % 4], y2[(u - 5) % 4], 0, u)
                        ln_stats(dve, y2[(u - 3) % 4], 0)
                        ln_stats(dve, y4[(u - 9) % 4], 1)
                        ln_variance(dve, 3 * K, u).then_inc(dve_step, 1)

                    steps_of(dve, body, STEPS)

                @block.tensor
                def _(pe):
                    pe.sem_inc(pe_step, 1)

                    def body(t, u):
                        await_step(pe, t, every)
                        turn(pe, b_readt, read[u % 4]).then_inc(readt_out, 1)
                        turn(pe, b_x3t, x3[(u - 6) % 4]).then_inc(x3t_out, 1)
                        pe.matmul(b_act1[0:H, :], w["W1"][:], readt[(u - 1) % 2], start=True,
                                  stop=True).then_inc(act1_out, 1)
                        pe.matmul(b_u[:], w["upd1x"][:], x3t[(u - 1) % 2], start=True,
                                  stop=True).then_inc(u_out, 1)
                        natural_product(pe, b_prompt[u % 2], act1[(u - 1) % 2], w["W2"], row["b2"])
                        natural_product(pe, b_delta[u % 2], h3[(u - 1) % 2], w["upd2"],
                                        row["upd_b2"]).then_inc(pe_step, 1)

                    steps_of(pe, body, STEPS)

        def pass_l0():
            new = Rings()
            xs, xd, run, d1, d1t, yn = (new(4) for _ in range(6))
            xst, xdt, own, yt = (new(2) for _ in range(4))
            b_xs, b_xd, b_nbr, b_self, b_y, b_d1 = bank[0], bank[1], bank[2:4], bank[4], bank[5], bank[6]
            every = engine_steps("l0")
            sp_step, pool_step, act_step, dve_step, pe_step = every
            xs_out, xd_out, self_out, y_out, d1_out = (
                sem(f"l0_{n}") for n in ("src_turned", "dst_turned", "self_done", "sum_turned", "state_turned"))
            STEPS = round_up(GROUPS + 8 + 1, UNROLL)
            RANGE = full_range(GROUPS, 8)
            with nc.Block() as block:
                @block.sync
                def _(sp):
                    sp_program(sp, every, "l0", GROUPS,
                               [(0, xs, load_edge_x(edge_x[0])), (0, xd, load_edge_x(edge_x[1])),
                                (2, restart, load_mask("restart"))],
                               [(8, d1t, load_turned(dst1_turned))], STEPS, *RANGE)

                @block.gpsimd
                def _(pool):
                    pool_program(pool, every, "l0", GROUPS, [],
                                 (7, d1, tables[0]), STEPS, *RANGE, 1)

                @block.scalar
                def _(act):
                    act.sem_inc(act_step, 1)

                    def body(t, u):
                        await_step(act, t, every)
                        act.wait_ge(xs_out, t + 1)
                        act.activation(xst[u % 2], b_xs[:], ACT.Copy)
                        act.wait_ge(xd_out, t + 1)
                        act.activation(xdt[u % 2], b_xd[:], ACT.Copy)
                        act.wait_ge(self_out, t + 1)
                        act.activation(own[u % 2], b_self[:], ACT.Identity, bias=col["L0_b"][:])
                        act.wait_ge(y_out, t + 1)
                        act.activation(yn[(u - 3) % 4], b_y[:], ACT.Copy)
                        act.wait_ge(d1_out, t + 1)
                        act.activation(d1t[(u - 7) % 4], b_d1[:], ACT.Copy).then_inc(act_step, 1)

                    steps_of(act, body, STEPS)

                @block.vector
                def _(dve):
                    dve.sem_inc(dve_step, 1)

                    def body(t, u):
                        await_step(dve, t, every)
                        dve.tensor_tensor_scan(run[(u - 2) % 4], restart[(u - 2) % 4], b_nbr[(u - 1) % 2][:],
                                               run[(u - 3) % 4][:, G - 1:G], ALU.add, ALU.max)
                        ln_stats(dve, yn[(u - 4) % 4], 0)
                        dve.drain()
                        dve.tensor_tensor(yt[u % 2], run[(u - 2) % 4], own[(u - 1) % 2], ALU.add)
                        ln_shift(dve, K, u)
                        ln_apply_dve(dve, d1[(u - 6) % 4], yn[(u - 6) % 4], 0, u)
                        ln_variance(dve, K, u).then_inc(dve_step, 1)

                    steps_of(dve, body, STEPS)

                @block.tensor
                def _(pe):
                    pe.sem_inc(pe_step, 1)

                    def body(t, u):
                        await_step(pe, t, every)
                        turn(pe, b_xs, xs[u % 4]).then_inc(xs_out, 1)
                        turn(pe, b_xd, xd[u % 4]).then_inc(xd_out, 1)
                        pe.matmul(b_self[:], w["W_self"][:], xdt[(u - 1) % 2], start=True,
                                  stop=True).then_inc(self_out, 1)
                        turn(pe, b_y, yt[(u - 1) % 2]).then_inc(y_out, 1)
                        turn(pe, b_d1, d1[(u - 7) % 4]).then_inc(d1_out, 1)
                        pe.matmul(b_nbr[u % 2][:], w["W_nbr"][:], xst[(u - 1) % 2], start=True,
                                  stop=True).then_inc(pe_step, 1)

                    steps_of(pe, body, STEPS)

        def pass_back():
            new = Rings()
            d1t, is_last, not_last, filled = (new(4) for _ in range(4))
            marked = new(1)[0]
            every = engine_steps("back")
            sp_step, pool_step, act_step, dve_step, pe_step = every
            two = (sp_step, dve_step)
            STEPS = round_up(GROUPS + 1, UNROLL)
            RANGE = full_range(GROUPS, 1)

            def from_end(load):
                return lambda buf, b: load(buf, GROUPS - 1 - b)

            with nc.Block() as block:
                @block.sync
                def _(sp):
                    sp_program(sp, two, "back", GROUPS,
                               [(0, d1t, from_end(load_turned(dst1_turned))), (0, is_last, from_end(load_mask("is_last"))),
                                (0, not_last, from_end(load_mask("not_last")))],
                               [(1, filled, from_end(load_turned(dst1_filled)))], STEPS, *RANGE)

                @block.vector
                def _(dve):
                    dve.sem_inc(dve_step, 1)

                    def body(t, u):
                        await_step(dve, t, two)
                        dve.tensor_tensor(marked, d1t[u % 4], is_last[u % 4], ALU.mult)
                        dve.drain()
                        dve.tensor_tensor_scan(filled[u % 4][:, ::-1], not_last[u % 4][:, ::-1], marked[:, ::-1],
                                               filled[(u - 1) % 4][:, 0:1], ALU.mult, ALU.add).then_inc(dve_step, 1)

                    steps_of(dve, body, STEPS)

        def pass_l1():
            new = Rings()
            xs, xst, d1t, d1t_late, xl, xl_own, d2, yn = (new(4) for _ in range(8))
            u_relu, u_lin, v_relu, v_lin, own_logit, z, o, mean_xl, ob, yt = (new(2) for _ in range(10))
            at = new(6)
            weight = [at[0:3], at[3:6]]
            temp = new(4)
            at = new(6)
            below = [at[0:3], at[3:6]]
            b_xs, b_u, b_v, b_xl, b_own, b_logit, b_own_logit = (
                bank[0], bank[1], bank[2], bank[3], bank[4], bank[5:7], bank[7])
            every = engine_steps("l1")
            sp_step, pool_step, act_step, dve_step, pe_step = every
            xs_out, u_out, v_out, xl_out, own_out, own_logit_out, y_out, b0_free = (
                sem(f"l1_{n}") for n in ("src_turned", "u_done", "v_done", "xl_done", "own_done", "own_logit_done",
                                         "sum_turned", "src_copied"))
            STEPS = round_up(GROUPS + 12 + 1, UNROLL)
            RANGE = full_range(GROUPS, 12)
            with nc.Block() as block:
                @block.sync
                def _(sp):
                    sp_program(sp, every, "l1", GROUPS,
                               [(1, d1t, load_turned(dst1_filled)), (3, restart, load_mask("restart")),
                                (7, d1t_late, load_turned(dst1_filled))],
                               [], STEPS, *RANGE)

                @block.gpsimd
                def _(pool):
                    pool_program(pool, every, "l1", GROUPS, [(xs, tables[0], src_index)], (12, d2, tables[1]),
                                 STEPS, *RANGE, 1)

                @block.scalar
                def _(act):
                    act.sem_inc(act_step, 1)

                    def body(t, u):
                        await_step(act, t, every)
                        for n in range(3):
                            act.activation(weight[u % 2][n], below[(u - 1) % 2][n], ACT.Exp)
                        act.activation(ob[u % 2], mean_xl[(u - 1) % 2], ACT.Identity, bias=col["bl_bias"][:])
                        act.wait_ge(xs_out, t + 1)
                        act.activation(xst[u % 4], b_xs[:], ACT.Copy).then_inc(b0_free, 1)
                        act.wait_ge(u_out, t + 1)
                        act.activation(u_relu[u % 2], b_u[:], ACT.Relu, bias=col["bl_br"][:])
                        act.activation(u_lin[u % 2], b_u[:], ACT.Identity, bias=col["bl_br"][:])
                        act.wait_ge(v_out, t + 1)
                        act.activation(v_relu[u % 2], b_v[:], ACT.Relu, bias=col["bl_br"][:])
                        act.activation(v_lin[u % 2], b_v[:], ACT.Identity, bias=col["bl_br"][:])
                        act.wait_ge(xl_out, t + 1)
                        act.activation(xl[(u - 2) % 4], b_xl[:], ACT.Copy)
                        act.wait_ge(own_out, t + 1)
                        act.activation(xl_own[(u - 2) % 4], b_own[:], ACT.Copy)
                        act.wait_ge(own_logit_out, t + 1)
                        act.activation(own_logit[u % 2], b_own_logit[:], ACT.Copy)
                        act.wait_ge(y_out, t + 1)
                        act.activation(yn[(u - 8) % 4], b_xs[:], ACT.Copy).then_inc(act_step, 1)

                    steps_of(act, body, STEPS)

                @block.vector
                def _(dve):
                    for three in weight:
                        for buf in three:
                            dve.memset(buf, 1.0)
                    for buf in below[0] + below[1] + z + o:
                        dve.memset(buf, 0.0)
                    dve.memset(max_run[0][:], 0.0)
                    dve.memset(max_run[1][:], 0.0).then_inc(dve_step, 1)

                    def body(t, u):
                        await_step(dve, t, every)
                        logit, own, m, before = b_logit[(u - 1) % 2], own_logit[(u - 1) % 2], max_run[u % 2], max_run[(u - 1) % 2]
                        d = below[u % 2]
                        shrink, p, p_own = weight[(u - 1) % 2]
                        dve.tensor_tensor(temp[0], logit[:], own, ALU.max)
                        dve.tensor_copy(m[:, 0:1], before[:, G:G + 1])
                        dve.tensor_tensor(temp[1], p, xl[(u - 5) % 4], ALU.mult)
                        dve.tensor_tensor(temp[2], p_own, xl_own[(u - 5) % 4], ALU.mult)
                        dve.tensor_tensor_scan(z[u % 2], shrink, p, z[(u - 1) % 2][:, G - 1:G], ALU.mult, ALU.add)
                        dve.drain()
                        dve.tensor_tensor_scan(m[:, 1:G + 1], restart[(u - 3) % 4], temp[0], before[:, G:G + 1],
                                               ALU.add, ALU.max)
                        dve.tensor_tensor_scan(o[u % 2], shrink, temp[1], o[(u - 1) % 2][:, G - 1:G], ALU.mult, ALU.add)
                        dve.tensor_tensor(temp[3], z[u % 2], p_own, ALU.add)
                        dve.drain()
                        dve.tensor_tensor(d[0], m[:, 0:G], restart[(u - 3) % 4], ALU.add)
                        dve.tensor_tensor(d[1], logit[:], m[:, 1:G + 1], ALU.subtract)
                        dve.tensor_tensor(d[2], own, m[:, 1:G + 1], ALU.subtract)
                        dve.tensor_tensor(temp[2], temp[2], o[u % 2], ALU.add)
                        dve.reciprocal(temp[3], temp[3])
                        dve.scalar_tensor_tensor(temp[0], ob[(u - 1) % 2], OUT_SLOPE, ob[(u - 1) % 2], ALU.mult, ALU.max)
                        dve.drain()
                        dve.tensor_tensor(d[0], d[0], m[:, 1:G + 1], ALU.subtract)
                        dve.tensor_tensor(mean_xl[u % 2], temp[2], temp[3], ALU.mult)
                        dve.tensor_tensor(yt[u % 2], temp[0], d1t_late[(u - 7) % 4], ALU.add)
                        ln_shift(dve, K, u)
                        ln_apply_dve(dve, d2[(u - 11) % 4], yn[(u - 11) % 4], 0, u)
                        ln_stats(dve, yn[(u - 9) % 4], 0)
                        ln_variance(dve, K, u).then_inc(dve_step, 1)

                    steps_of(dve, body, STEPS)

                @block.tensor
                def _(pe):
                    pe.sem_inc(pe_step, 1)

                    def product(to, parts):
                        for n, (weights, turned) in enumerate(parts):
                            last = pe.matmul(to[:], w[weights][:], turned, start=n == 0, stop=n == len(parts) - 1)
                        return last

                    def body(t, u):
                        await_step(pe, t, every)
                        turn(pe, b_xs, xs[u % 4]).then_inc(xs_out, 1)
                        product(b_u, (("Wl", xst[(u - 1) % 4]), ("Wr", d1t[(u - 1) % 4]))).then_inc(u_out, 1)
                        product(b_v, (("Wlr", d1t[(u - 1) % 4]),)).then_inc(v_out, 1)
                        product(b_xl, (("Wl", xst[(u - 2) % 4]),)).then_inc(xl_out, 1)
                        product(b_own, (("Wl", d1t[(u - 2) % 4]),)).then_inc(own_out, 1)
                        product(b_own_logit, (("att_relu", v_relu[(u - 1) % 2]),
                                              ("att_lin", v_lin[(u - 1) % 2]))).then_inc(own_logit_out, 1)
                        product(b_logit[u % 2], (("att_relu", u_relu[(u - 1) % 2]), ("att_lin", u_lin[(u - 1) % 2])))
                        pe.wait_ge(b0_free, t + 1)
                        turn(pe, b_xs, yt[(u - 1) % 2]).then_inc(y_out, 1)
                        pe.wait_ge(y_out, t + 1)
                        pe.sem_inc(pe_step, 1)

                    steps_of(pe, body, STEPS)

        def pass_l2():
            new = Rings()
            xd, xd_late, source, summed = (new(4) for _ in range(4))
            xdt, hidden, msg = (new(2) for _ in range(3))
            at = new(2 * K)
            same = [at[0:K], at[K:2 * K]]
            unused = new(1)[0]
            b_xd, b_hidden, b_gate, b_sum = bank[0], bank[1], bank[2], bank[3]
            every = engine_steps("l2")
            sp_step, pool_step, act_step, dve_step, pe_step = every
            xd_out, hidden_out, gate_out, sum_out = (
                sem(f"l2_{n}") for n in ("dst_turned", "hidden_done", "gate_done", "sum_done"))
            src_copied = sem("l2_src_copied")
            STEPS = round_up(GROUPS + 5 + 1, UNROLL)
            RANGE = full_range(GROUPS, 5)
            with nc.Block() as block:
                @block.sync
                def _(sp):
                    sp_program(sp, every, "l2", GROUPS, [(3, source, load_mask("source"))], [], STEPS, *RANGE)

                @block.gpsimd
                def _(pool):
                    pool_program(pool, every, "l2", GROUPS, [(xd, tables[1], dst_index)], (5, summed, readout),
                                 STEPS, *RANGE, add_index=add_now)

                @block.scalar
                def _(act):
                    act.sem_inc(act_step, 1)

                    def body(t, u):
                        await_step(act, t, every)
                        act.activation(xd_late[(u - 1) % 4], xd[(u - 1) % 4], ACT.Copy)
                        act.wait_ge(xd_out, t + 1)
                        act.activation(xdt[u % 2], b_xd[:], ACT.Copy)
                        act.wait_ge(hidden_out, t + 1)
                        act.activation(hidden[u % 2][0:H, :], b_hidden[0:H, :], ACT.Tanh, bias=col["b_sim"][:])
                        act.wait_ge(gate_out, t + 1)
                        act.activation(gate[u % 2][:], b_gate[:, 0:K], ACT.Sigmoid, bias=col["b_vec"][:])
                        act.wait_ge(sum_out, t + 1)
                        act.activation(summed[(u - 4) % 4], b_sum[:], ACT.Copy).then_inc(act_step, 1)

                    steps_of(act, body, STEPS)

                @block.vector
                def _(dve):
                    dve.sem_inc(dve_step, 1)

                    def body(t, u):
                        await_step(dve, t, every)
                        last_group = GROUPS - 1
                        b = (min(max(t - 3, 0), last_group) if isinstance(t, int) else t - 3)
                        dve.tensor_copy(src_now[:], src_value[:, bass.ds(b * K, K)])
                        for k in range(K):
                            dve.tensor_scalar(tiles(msg[u % 2])[k], tiles(xd_late[(u - 3) % 4])[k],
                                              gate[(u - 1) % 2][:, k:k + 1], None, ALU.mult)
                        dve.drain()
                        for k in range(K):
                            dve.tensor_scalar(same[u % 2][k], source[(u - 3) % 4], src_now[:, k:k + 1], None,
                                              ALU.is_equal)
                        dve.drain()
                        for k in range(K):
                            dve.scalar_tensor_tensor(unused, same[u % 2][k], 1.0, earlier[:, k, :], ALU.mult,
                                                     ALU.mult, accum_out=repeats[:, k:k + 1])
                            dve.drain()
                        dve.tensor_scalar(repeats[:], repeats[:], 0.0, None, ALU.is_gt)
                        dve.tensor_tensor(detour[:], spare_row[:], src_now[:], ALU.subtract)
                        dve.drain()
                        dve.tensor_tensor(detour[:], detour[:], repeats[:], ALU.mult)
                        dve.drain()
                        dve.tensor_tensor(add_now[(u - 3) % 4][:], detour[:], src_now[:], ALU.add).then_inc(dve_step, 1)

                    dma_steps(dve, body, (), STEPS, *RANGE)

                @block.tensor
                def _(pe):
                    pe.sem_inc(pe_step, 1)

                    def body(t, u):
                        await_step(pe, t, every)
                        turn(pe, b_xd, xd[u % 4]).then_inc(xd_out, 1)
                        pe.matmul(b_hidden[0:H, :], w["W_sim"][:], xdt[(u - 1) % 2], start=True,
                                  stop=True).then_inc(hidden_out, 1)
                        for k in range(K):
                            last = pe.matmul(b_gate[:, k:k + 1], hidden[(u - 1) % 2][0:H, k * P:(k + 1) * P],
                                             col["w_vec"][:], start=True, stop=True)
                        last.then_inc(gate_out, 1)
                        for m in range(K):
                            for k in range(K):
                                last = pe.matmul(tiles(b_sum)[m], tiles(same[(u - 1) % 2][k])[m],
                                                 tiles(msg[(u - 1) % 2])[k], start=k == 0, stop=k == K - 1)
                        last.then_inc(sum_out, 1)
                        pe.wait_ge(sum_out, t + 1)
                        pe.sem_inc(pe_step, 1)

                    steps_of(pe, body, STEPS)

        def pass_l3():
            new = Rings()
            xs, attr, d3, goes_on, d3_late, d3t, d3b, y4, y5, res = (new(4) for _ in range(10))
            xst, attrt, m1, total, degree, mean, h, n4 = (new(2) for _ in range(8))
            ones, scaled, count = (new(1)[0] for _ in range(3))
            b_xs, b_msg1, b_d3, b_msg, b_u, b_delta = bank[0], bank[1], bank[2], bank[3:5], bank[5], bank[6:8]
            every = engine_steps("l3")
            sp_step, pool_step, act_step, dve_step, pe_step = every
            xs_out, attr_out, attr_free, d3_out, m1_out, u_out = (
                sem(f"l3_{n}") for n in ("src_turned", "attr_turned", "attr_copied", "dst_turned", "msg1_done",
                                         "upd1_done"))
            shift_ready = sem("l3_shift")
            STEPS = round_up(GROUPS + 12 + 1, UNROLL)
            RANGE = full_range(GROUPS, 12)
            with nc.Block() as block:
                @block.sync
                def _(sp):
                    sp_program(sp, every, "l3", GROUPS,
                               [(0, attr, load_edges(v["edge_attr_64"], H)), (3, goes_on, load_mask("goes_on")),
                                (6, d3_late, load_edges(dst3))],
                               [(0, d3, load_edges(dst3))], STEPS, *RANGE)

                @block.gpsimd
                def _(pool):
                    pool_program(pool, every, "l3", GROUPS, [(xs, tables[2], src_index), (d3, tables[2], dst_index)],
                                 (12, res, out), STEPS, *RANGE, 2)

                @block.scalar
                def _(act):
                    act.sem_inc(act_step, 1)

                    def body(t, u):
                        await_step(act, t, every)
                        act.wait_ge(xs_out, t + 1)
                        act.activation(xst[u % 2], b_xs[:], ACT.Copy)
                        act.wait_ge(attr_out, t + 1)
                        act.activation(attrt[u % 2][0:H, :], b_msg1[0:H, :], ACT.Copy).then_inc(attr_free, 1)
                        act.wait_ge(d3_out, t + 1)
                        act.activation(d3t[(u - 1) % 4], b_d3[:], ACT.Copy)
                        act.wait_ge(u_out, t + 1)
                        act.activation(h[u % 2], b_u[:], ACT.Relu, bias=col["upd_c_edge"][:])
                        act.wait_ge(m1_out, t + 1)
                        act.activation(m1[u % 2], b_msg1[:], ACT.Relu, bias=col["msg_c"][:])
                        act.wait_ge(shift_ready, t + 1)
                        ln_apply_act(act, n4[(u - 8) % 2], y4[(u - 8) % 4], 0, u)
                        ln_apply_act(act, res[(u - 11) % 4], y5[(u - 11) % 4], 1, u).then_inc(act_step, 1)

                    steps_of(act, body, STEPS)

                @block.vector
                def _(dve):
                    dve.memset(ones, 1.0).then_inc(dve_step, 1)

                    def body(t, u):
                        await_step(dve, t, every)
                        dve.tensor_tensor_scan(total[u % 2], goes_on[(u - 3) % 4], b_msg[(u - 1) % 2][:],
                                               total[(u - 1) % 2][:, G - 1:G], ALU.mult, ALU.add)
                        dve.tensor_tensor_scan(degree[u % 2], goes_on[(u - 3) % 4], ones,
                                               degree[(u - 1) % 2][:, G - 1:G], ALU.mult, ALU.add)
                        ln_shift(dve, 2 * K, u).then_inc(shift_ready, 1)
                        dve.tensor_tensor(y4[(u - 6) % 4], d3_late[(u - 6) % 4], b_delta[(u - 1) % 2][:], ALU.add)
                        dve.tensor_tensor(d3b[(u - 6) % 4], d3_late[(u - 6) % 4], wide["beta"][:], ALU.add)
                        dve.drain()
                        dve.tensor_scalar(count, degree[u % 2], 1.0, None, ALU.max)
                        dve.tensor_tensor(scaled, n4[(u - 9) % 2], wide["gamma"][:], ALU.mult)
                        dve.drain()
                        dve.reciprocal(count, count)
                        dve.tensor_tensor(y5[(u - 9) % 4], scaled, d3b[(u - 9) % 4], ALU.add)
                        dve.drain()
                        dve.tensor_tensor(mean[u % 2], total[u % 2], count, ALU.mult)
                        ln_stats(dve, y4[(u - 6) % 4], 0)
                        ln_stats(dve, y5[(u - 9) % 4], 1)
                        ln_variance(dve, 2 * K, u).then_inc(dve_step, 1)

                    steps_of(dve, body, STEPS)

                @block.tensor
                def _(pe):
                    pe.sem_inc(pe_step, 1)

                    def body(t, u):
                        await_step(pe, t, every)
                        turn(pe, b_xs, xs[u % 4]).then_inc(xs_out, 1)
                        turn(pe, b_msg1, attr[u % 4], H).then_inc(attr_out, 1)
                        turn(pe, b_d3, d3[(u - 1) % 4]).then_inc(d3_out, 1)
                        pe.matmul(b_u[:], w["upd1x"][:], d3t[(u - 4) % 4], start=True, stop=False)
                        pe.matmul(b_u[:], w["upd1a"][:], mean[(u - 1) % 2], start=False, stop=True).then_inc(u_out, 1)
                        pe.wait_ge(attr_free, t + 1)
                        pe.matmul(b_msg1[:], w["msg1x"][:], xst[(u - 1) % 2], start=True, stop=False)
                        pe.matmul(b_msg1[:], w["msg1e"][:], attrt[(u - 1) % 2][0:H, :], start=False,
                                  stop=True).then_inc(m1_out, 1)
                        pe.matmul(b_msg[u % 2][:], w["msg2"][:], m1[(u - 1) % 2], start=True, stop=True)
                        natural_product(pe, b_delta[u % 2], h[(u - 1) % 2], w["upd2"],
                                        row["upd_b2"]).then_inc(pe_step, 1)

                    steps_of(pe, body, STEPS)

        prepare()
        pass_nodes_a()
        pass_l0()
        pass_back()
        pass_l1()
        pass_l2()
        pass_nodes_b()
        pass_l3()


_N, _D = 100000, 128
_OUTS = [((_N, _D), 'float32')]


def kernel(**inputs):
    import numpy as _np
    import concourse.bacc as _bacc
    from concourse import mybir as _mybir
    from concourse.bass_utils import run_bass_kernel_spmd as _run

    group = 512
    src, dst = _np.asarray(inputs["src"]), _np.asarray(inputs["dst"])
    edges = src.shape[0]
    groups = -(-edges // group)
    pad = groups * group - edges
    src_pad = _np.concatenate([src, _np.full(pad, _N + group, src.dtype)])
    dst_pad = _np.concatenate([_np.full(1, -1, dst.dtype), dst, _np.full(pad + 1, _N, dst.dtype)])
    laid = {
        "src_tiles": src_pad.reshape(-1, 128).T,
        "src_rows": src_pad.reshape(-1, group),
        "dst_tiles": dst_pad[1:-1].reshape(-1, 128).T,
        "dst_next_tiles": dst_pad[2:].reshape(-1, 128).T,
        "dst_windows": _np.lib.stride_tricks.sliding_window_view(dst_pad, group + 2)[::group],
    }
    for name, a in inputs.items():
        if name in ("src", "dst", "edge_attr_16"):
            continue
        a = _np.asarray(a)
        if name == "edge_attr_64":
            a = _np.concatenate([a, _np.zeros((pad, a.shape[1]), a.dtype)])
        laid[name] = a

    nc = _bacc.Bacc("TRN2", target_bir_lowering=False, num_devices=1)
    arrays, views = {}, {}
    for name, a in laid.items():
        a = _np.ascontiguousarray(a)
        arrays[f"in_{name}_dram"] = a
        views[name] = nc.dram_tensor(f"in_{name}_dram", a.shape, _mybir.dt.from_np(a.dtype), kind="ExternalInput").ap()
    outs = [nc.dram_tensor(f"out_{i}_dram", shape, _mybir.dt.from_np(_np.dtype(dtype)), kind="ExternalOutput").ap()
            for i, (shape, dtype) in enumerate(_OUTS)]
    build(nc, views, outs[0])
    r = _run(nc, [arrays], core_ids=[0])
    return r.results[0]["out_0_dram"]
```

```python
import concourse.bass as bass
from concourse import mybir
from contextlib import ExitStack

F32 = mybir.dt.float32
I32 = mybir.dt.int32
BF16 = mybir.dt.bfloat16
ALU = mybir.AluOpType
ACT = mybir.ActivationFunctionType

P = 128
D = 128
K = 4
G = K * P
H = 64
UNROLL = 4
EPS = 1e-5
BIG = 1e38
NOWHERE = 1 << 20
ATT_SLOPE = 0.2
OUT_SLOPE = 0.01


def round_up(n, m):
    return -(-n // m) * m


class Tally:

    def __init__(self, sems, per_step):
        self.sems, self.per_step, self.count, self.into = sems, per_step, [0, 0], 0

    def add(self, parity):
        self.count[parity] += 1
        return self.sems[parity]

    def enter(self, i, first):
        self.into = (i - first) * (UNROLL // 2 * self.per_step * 16 // UNROLL)

    def leave(self, trips):
        self.into = 0
        for parity in range(2):
            self.count[parity] += (trips - 1) * (UNROLL // 2) * self.per_step

    def wait(self, eng, parity):
        if self.count[parity]:
            eng.wait_ge(self.sems[parity], self.into + 16 * self.count[parity])


def dma_steps(eng, body, tallies, steps, first, last):
    for t in range(first):
        body(t, t % UNROLL)
    with eng.Fori(first, last - UNROLL + 1, UNROLL) as i:
        for tally in tallies:
            tally.enter(i, first)
        for u in range(UNROLL):
            body(i + u, u)
    for tally in tallies:
        tally.leave((last - first) // UNROLL)
    for t in range(last, steps):
        body(t, t % UNROLL)


def steps_of(eng, body, steps):
    looped = steps // UNROLL * UNROLL
    with eng.Fori(0, looped - UNROLL + 1, UNROLL) as i:
        for u in range(UNROLL):
            body(i + u, u)
    for t in range(looped, steps):
        body(t, t % UNROLL)


def await_step(eng, t, step_sems):
    for s in step_sems:
        eng.wait_ge(s, t + 1)


def tiles(buf):
    return [buf[:, k * P:(k + 1) * P] for k in range(K)]


def build(nc, v, out):
    N = v["x"].shape[0]
    GROUPS = v["dst_windows"].shape[0]
    NODE_GROUPS = -(-N // G)

    ctx = ExitStack()
    with ctx:
        def sb(name, shape, dt=F32):
            return ctx.enter_context(nc.sbuf_tensor(name, shape, dt))

        def sem(name):
            return ctx.enter_context(nc.semaphore(name))

        def pair(name):
            return [sem(f"{name}_even"), sem(f"{name}_odd")]

        def dram(name, shape):
            return nc.dram_tensor(name, shape, F32, kind="Internal").ap()

        tables = [dram(f"state_{n}", (N, D)) for n in (1, 2, 3)]
        dst1_turned = dram("dst1_turned", (GROUPS, P, G))
        dst3 = dram("dst_state_3", (GROUPS * G, D))
        edge_x = [dram(f"x_at_{n}", (GROUPS * 2 * P, G // 2)) for n in ("src", "dst")]
        readout = dram("readout", (N + 2 * G, D))
        MASKS = ("goes_on", "restart", "is_first", "restart_back")
        mask_rows = {m: dram(m, (GROUPS, G)) for m in (*MASKS, "source")}

        RING = 79
        arena = sb("arena", [P, RING * G])
        bank = [ctx.enter_context(nc.psum_tensor(f"bank{i}", [P, G], F32)) for i in range(8)]

        class Rings:

            def __init__(self):
                self.used = 0

            def __call__(self, n):
                at = [arena[:, (self.used + i) * G:(self.used + i + 1) * G] for i in range(n)]
                self.used += n
                assert self.used <= RING - 4
                return at

        restart = [arena[:, i * G:(i + 1) * G] for i in range(RING - 4, RING)]
        ident = sb("ident", [P, P])
        one = sb("one", [1, 1])
        half_neg = sb("half_neg", [P, 3 * K])
        w = {}
        for name in ("Wl", "Wr", "Wlr", "W_self", "W_nbr", "Wlin", "att_relu", "att_lin", "msg1x", "msg2",
                     "upd1x", "upd1a", "upd2"):
            w[name] = sb("w_" + name, [P, P])
        w["W_sim"] = sb("w_W_sim", [P, H])
        w["W1"] = sb("w_W1", [P, H])
        for name in ("W2", "msg1e", "msg1g", "upd1g"):
            w[name] = sb("w_" + name, [H, P])
        col = {}
        for name in ("L0_b", "bl", "br", "bias", "b_vec", "msg_b1", "msg_b2", "upd_b1", "bl_br", "bl_bias",
                     "msg_c", "upd_c_node", "upd_c_edge", "att"):
            col[name] = sb("c_" + name, [P, 1])
        for name in ("b_sim", "b1", "glob", "w_vec"):
            col[name] = sb("c_" + name, [H, 1])
        row = {}
        for name in ("xl_bias", "xl_bias_lin", "b2", "upd_b2"):
            row[name] = sb("r_" + name, [96, G], BF16)
        selector = sb("selector", [96, P], BF16)
        wide = {}
        for name in ("gamma", "beta"):
            wide[name] = sb("n_" + name, [P, G])
        src_index = sb("src_index", [P, GROUPS * K], I32)
        dst_index = sb("dst_index", [P, GROUPS * K], I32)
        src_value = sb("src_value", [P, GROUPS * K])
        spare_row = sb("spare_row", [P, K])
        earlier = sb("earlier", [P, K, G])
        put_first, put_last = (sb(f"put_at_{n}", [P, GROUPS * K], I32) for n in ("first", "last"))
        index_now = [sb(f"index_now{i}", [P, 2 * K], I32) for i in range(2)]
        put_now = [sb(f"put_now{i}", [P, K], I32) for i in range(2)]
        add_now = [sb(f"add_now{i}", [P, K], I32) for i in range(4)]
        src_now = sb("src_now", [P, K])
        repeats = sb("repeats", [P, K])
        detour = sb("detour", [P, K])
        gate = [sb(f"gate{i}", [P, K]) for i in range(2)]
        stats = sb("stats", [P, 3 * K, 6])
        gap, spread, gap2, shift = (sb(n, [P, 3 * K]) for n in ("gap", "spread", "gap2", "shift"))
        root, inverse_root, square, product, factor = (
            sb(n, [P, 3 * K]) for n in ("root", "inverse_root", "square", "product", "factor"))
        mean2, var, rstd = ([sb(f"{n}{i}", [P, 3 * K]) for i in range(2)] for n in ("mean2", "var", "rstd"))
        max_run = [sb(f"max_run{i}", [P, G + 1]) for i in range(2)]

        def prepare():
            loads = sem("weights_loaded")
            idm = sem("identity_made")
            ready = sem("operands_ready")
            products = sem("products_ready")
            made = sem("prep_made")
            stored = sem("masks_stored")
            W0 = arena[:, 0:2 * P]
            used = [6 * G]

            def scratch(partitions, n):
                used[0] += n
                return arena[0:partitions, used[0] - n:used[0]]

            win_i = sb("windows", [GROUPS, G + 2], I32)
            neighbour = [sb(f"dst_{n}", [P, GROUPS * K], I32) for n in ("before", "next")]
            differs = [scratch(P, GROUPS * K) for i in range(2)]
            mask = {m: arena[0:GROUPS, (i + 1) * G:(i + 2) * G] for i, m in enumerate((*MASKS, "source"))}
            r = {n: scratch(96, P) for n in ("bl", "bias", "b2", "upd_b2")}
            bias_row = {n: scratch(96, P) for n in ("xl_bias", "xl_bias_lin")}
            part = {n: [sb(f"part{i}_{n}", [96, P], BF16) for i in range(3)] for n in row}
            rest = {n: [scratch(96, P) for i in range(2)] for n in row}
            src_i = sb("src_row_i", [GROUPS, G], I32)
            ones_wide = scratch(P, P)
            att_s = sb("att_s", [P, 2])
            raw_gamma, raw_beta = scratch(P, P), scratch(P, P)

            def as_col(a):
                return a.rearrange("(p a) -> p a", a=1)

            def as_row(a):
                return a.rearrange("(a p) -> a p", a=1)

            pieces = [
                (W0, v["L0_gnn_W"]), (w["Wl"][:], v["L1_gnn_Wl"]), (w["Wr"][:], v["L1_gnn_Wr"]),
                (w["W_sim"][:], v["L2_gnn_W_sim"]), (w["W1"][:], v["L2_gnn_W1"]), (w["W2"][:], v["L2_gnn_W2"]),
                (w["msg1x"][:], v["L3_gnn_msg_w1"][0:D, :]), (w["msg1e"][:], v["L3_gnn_msg_w1"][D:D + H, :]),
                (w["msg1g"][:], v["L3_gnn_msg_w1"][D + H:D + 2 * H, :]), (w["msg2"][:], v["L3_gnn_msg_w2"]),
                (w["upd1x"][:], v["L3_gnn_upd_w1"][0:D, :]), (w["upd1a"][:], v["L3_gnn_upd_w1"][D:2 * D, :]),
                (w["upd1g"][:], v["L3_gnn_upd_w1"][2 * D:2 * D + H, :]), (w["upd2"][:], v["L3_gnn_upd_w2"]),
                (col["L0_b"][:], as_col(v["L0_gnn_b"])), (col["bl"][:], as_col(v["L1_gnn_bl"])),
                (col["br"][:], as_col(v["L1_gnn_br"])), (col["bias"][:], as_col(v["L1_gnn_bias"])),
                (col["att"][:], as_col(v["L1_gnn_att"])), (col["b_sim"][:], as_col(v["L2_gnn_b_sim"])),
                (col["b1"][:], as_col(v["L2_gnn_b1"])), (col["w_vec"][:], v["L2_gnn_w_vec"]),
                (col["b_vec"][:], as_row(v["L2_gnn_b_vec"]).to_broadcast([P, 1])),
                (col["glob"][:], as_col(v["L3_gnn_global_state"])), (col["msg_b1"][:], as_col(v["L3_gnn_msg_b1"])),
                (col["msg_b2"][:], as_col(v["L3_gnn_msg_b2"])), (col["upd_b1"][:], as_col(v["L3_gnn_upd_b1"])),
                (r["bl"][:], as_row(v["L1_gnn_bl"]).to_broadcast([96, P])),
                (r["bias"][:], as_row(v["L1_gnn_bias"]).to_broadcast([96, P])),
                (r["b2"][:], as_row(v["L2_gnn_b2"]).to_broadcast([96, P])),
                (r["upd_b2"][:], as_row(v["L3_gnn_upd_b2"]).to_broadcast([96, P])),
                (raw_gamma[:], as_row(v["L3_gnn_ln_gamma"]).to_broadcast([P, P])),
                (raw_beta[:], as_row(v["L3_gnn_ln_beta"]).to_broadcast([P, P])),
                (win_i[:], v["dst_windows"]), (src_index[:], v["src_tiles"]), (dst_index[:], v["dst_tiles"]),
                (neighbour[0][:], v["dst_before_tiles"]), (neighbour[1][:], v["dst_next_tiles"]),
                (src_i[:], v["src_rows"]),
            ]
            with nc.Block() as block:
                @block.sync
                def _(sp):
                    for to, of in pieces:
                        sp.dma_start(to, of).then_inc(loads, 16)
                    sp.wait_ge(made, 2)
                    for m in mask_rows:
                        sp.dma_start(mask_rows[m], mask[m]).then_inc(stored, 16)
                    sp.wait_ge(stored, 16 * len(mask_rows))

                @block.gpsimd
                def _(pool):
                    pool.memset(ident[:], 0.0).then_inc(idm, 1)
                    pool.wait_ge(idm, 1)
                    pool.affine_select(out=ident[:], in_=ident[:], compare_op=ALU.not_equal, fill=1.0, base=0,
                                       pattern=[[-1, P]], channel_multiplier=1).then_inc(idm, 1)
                    pool.iota(spare_row[:], pattern=[[P, K]], base=N, channel_multiplier=1,
                              allow_small_or_imprecise_dtypes=True)
                    pool.memset(earlier[:], 1.0).then_inc(idm, 1)
                    pool.wait_ge(idm, 3)
                    pool.affine_select(out=earlier[:], in_=earlier[:], compare_op=ALU.is_gt, fill=0.0, base=0,
                                       pattern=[[P, K], [-1, G]], channel_multiplier=1).then_inc(idm, 1)

                @block.vector
                def _(dve):
                    dve.memset(selector[:], 0.0)
                    dve.memset(ones_wide[:], 1.0)
                    dve.memset(half_neg[:], -0.5)
                    dve.memset(one[:], 1.0)
                    for b in bank:
                        dve.memset(b[:], 0.0)
                    for i in range(2):
                        dve.memset(gate[i][:], 0.0)
                        dve.memset(max_run[i][:], 0.0)
                    for i in range(2):
                        dve.memset(mean2[i][:], 0.0)
                        dve.memset(var[i][:], 1.0)
                        dve.memset(rstd[i][:], 1.0)
                    dve.wait_ge(loads, 16 * len(pieces))
                    dve.wait_ge(idm, 4)
                    dve.drain()
                    for i in range(3):
                        dve.memset(selector[32 * i:32 * i + 1, :], 1.0)
                    dve.tensor_scalar(att_s[:, 0:1], col["att"][:], 1.0 - ATT_SLOPE, None, ALU.mult)
                    dve.tensor_scalar(att_s[:, 1:2], col["att"][:], ATT_SLOPE, None, ALU.mult).then_inc(ready, 1)
                    dve.drain()
                    dve.tensor_scalar(w["att_relu"][:], ones_wide[:], att_s[:, 0:1], None, ALU.mult)
                    dve.tensor_scalar(w["att_lin"][:], ones_wide[:], att_s[:, 1:2], None, ALU.mult)
                    dve.tensor_tensor(w["Wlr"][:], w["Wl"][:], w["Wr"][:], ALU.add)
                    dve.scalar_tensor_tensor(w["Wlin"][:], w["Wl"][:], OUT_SLOPE, ident[:], ALU.mult, ALU.add)
                    dve.tensor_tensor(col["bl_br"][:], col["bl"][:], col["br"][:], ALU.add)
                    dve.tensor_tensor(col["bl_bias"][:], col["bl"][:], col["bias"][:], ALU.add)
                    for k in range(K):
                        at = slice(k * P, (k + 1) * P)
                        dve.tensor_copy(wide["gamma"][:, at], raw_gamma[:])
                        dve.tensor_copy(wide["beta"][:, at], raw_beta[:])
                    dve.tensor_tensor(bias_row["xl_bias"][:], r["bl"][:], r["bias"][:], ALU.add)
                    dve.drain()
                    dve.tensor_scalar(bias_row["xl_bias_lin"][:], bias_row["xl_bias"][:], OUT_SLOPE, None, ALU.mult)
                    dve.drain()
                    left = {n: bias_row.get(n, r.get(n)) for n in row}
                    for i in range(3):
                        for n in row:
                            dve.tensor_copy(part[n][i][:], left[n][:])
                        dve.drain()
                        for n in row:
                            for k in range(K):
                                at = slice(k * P, (k + 1) * P)
                                dve.tensor_copy(row[n][32 * i:32 * i + 32, at], part[n][i][32 * i:32 * i + 32, :])
                            if i < 2:
                                dve.tensor_tensor(rest[n][i][:], left[n][:], part[n][i][:], ALU.subtract)
                                left[n] = rest[n][i]
                        dve.drain()
                    dve.tensor_copy(mask["source"], src_i[:])
                    dve.tensor_tensor(mask["goes_on"], win_i[:, 1:G + 1], win_i[:, 0:G], ALU.is_equal)
                    dve.tensor_tensor(mask["restart_back"], win_i[:, 1:G + 1], win_i[:, 2:G + 2], ALU.is_equal)
                    for i in range(2):
                        dve.tensor_tensor(differs[i][:], dst_index[:], neighbour[i][:], ALU.not_equal)
                    dve.drain()
                    dve.tensor_scalar(mask["restart"], mask["goes_on"], -1.0, BIG, ALU.add, ALU.mult)
                    dve.tensor_scalar(mask["restart_back"], mask["restart_back"], -1.0, BIG, ALU.add, ALU.mult)
                    dve.tensor_scalar(mask["is_first"], mask["goes_on"], -1.0, 1.0, ALU.mult,
                                      ALU.add).then_inc(made, 1)
                    for put, at_end in ((put_first, differs[0]), (put_last, differs[1])):
                        dve.scalar_tensor_tensor(put[:], dst_index[:], -float(NOWHERE), at_end[:], ALU.add, ALU.mult)
                    dve.drain()
                    dve.sem_inc(made, 1)
                    for put in (put_first, put_last):
                        dve.tensor_scalar(put[:], put[:], float(NOWHERE), None, ALU.add)
                    dve.tensor_scalar(dst_index[:], dst_index[:], float(N - 1), None, ALU.min)
                    dve.tensor_copy(src_value[:], src_index[:])
                    dve.drain()
                    dve.tensor_scalar(src_index[:], src_index[:], float(N - 1), None, ALU.min)
                    dve.wait_ge(products, 1)
                    dve.tensor_copy(w["W_nbr"][:], bank[1][:, 0:P])
                    dve.tensor_tensor(col["msg_c"][:], bank[2][:, 0:1], col["msg_b1"][:], ALU.add)
                    dve.tensor_tensor(col["upd_c_node"][:], bank[3][:, 0:1], col["upd_b1"][:], ALU.add)
                    dve.drain()
                    dve.scalar_tensor_tensor(w["W_self"][:], bank[0][:, 0:P], 1.0, w["W_nbr"][:], ALU.mult, ALU.subtract)
                    dve.tensor_tensor(col["upd_c_edge"][:], bank[4][:, 0:1], col["upd_c_node"][:], ALU.add)
                    dve.drain()
                    dve.tensor_tensor(w["W_self"][:], w["W_self"][:], ident[:], ALU.add)
                    dve.drain()

                @block.tensor
                def _(pe):
                    pe.wait_ge(ready, 1)
                    pe.transpose(bank[0][:, 0:P], W0[:, 0:P], ident[:])
                    pe.transpose(bank[1][:, 0:P], W0[:, P:2 * P], ident[:])
                    pe.matmul(bank[2][:, 0:1], w["msg1g"][:], col["glob"][:], start=True, stop=True)
                    pe.matmul(bank[3][:, 0:1], w["upd1g"][:], col["glob"][:], start=True, stop=True)
                    pe.matmul(bank[4][:, 0:1], w["upd1a"][:], col["msg_b2"][:], start=True, stop=True).then_inc(products, 1)

        def group_rows(table, b):
            base = min(b * G, N - G) if isinstance(b, int) else b * G
            return table[bass.ds(base, G), :].rearrange("(p k) f -> p (k f)", k=K)

        def edge_rows(table, b):
            return table[bass.ds(b * G, G), :].rearrange("(k p) f -> p k f", p=P)

        def as_tiles(buf):
            return buf.rearrange("p (k f) -> p k f", k=K)

        def turned_group(table, b):
            return table[bass.ds(b, 1), :, :].rearrange("a p e -> (a p) e")

        def load_edge_x(table):
            return lambda buf, b: (buf.rearrange("p (h f) -> p h f", h=2),
                                   table[bass.ds(b * 2 * P, 2 * P), :].rearrange("(h p) f -> p h f", p=P))

        def mask_group(m, b):
            return mask_rows[m][bass.ds(b, 1), :].to_broadcast([P, G])

        def ln_stats(dve, buf, at):
            for k, tile in enumerate(tiles(buf)):
                dve.bn_stats(stats[:, at * K + k, :], tile)

        def ln_means(dve, n, u):
            dve.tensor_tensor(gap[:, 0:n], stats[:, 0:n, 1], stats[:, 0:n, 4], ALU.subtract)
            dve.scalar_tensor_tensor(spread[:, 0:n], stats[:, 0:n, 2], D * EPS, stats[:, 0:n, 5], ALU.add, ALU.add)
            dve.tensor_tensor(mean2[u % 2][:, 0:n], stats[:, 0:n, 1], stats[:, 0:n, 4], ALU.add)

        def ln_gap_squared(dve, n):
            dve.scalar_tensor_tensor(gap2[:, 0:n], gap[:, 0:n], 0.25, gap[:, 0:n], ALU.mult, ALU.mult)

        def ln_sum(dve, n, u):
            return dve.scalar_tensor_tensor(var[u % 2][:, 0:n], spread[:, 0:n], 1.0 / D, gap2[:, 0:n], ALU.mult,
                                            ALU.add)

        def ln_variance(dve, n, u):
            dve.drain()
            ln_means(dve, n, u)
            dve.drain()
            ln_gap_squared(dve, n)
            dve.drain()
            return ln_sum(dve, n, u)

        def ln_power(pool, n, u):
            return pool.tensor_tensor(rstd[u % 2][:, 0:n], var[(u - 1) % 2][:, 0:n], half_neg[:, 0:n], ALU.pow)

        def ln_root(act, n, u, root_ready):
            act.activation(root[:, 0:n], var[(u - 1) % 2][:, 0:n], ACT.Sqrt).then_inc(root_ready, 1)

        def ln_newton_1(dve, n, t, root_ready):
            dve.wait_ge(root_ready, t + 1)
            dve.reciprocal(inverse_root[:, 0:n], root[:, 0:n])

        def ln_newton_2(dve, n):
            dve.tensor_tensor(square[:, 0:n], inverse_root[:, 0:n], inverse_root[:, 0:n], ALU.mult)

        def ln_newton_3(dve, n, u):
            dve.tensor_tensor(product[:, 0:n], square[:, 0:n], var[(u - 1) % 2][:, 0:n], ALU.mult)

        def ln_newton_4(dve, n):
            dve.tensor_scalar(factor[:, 0:n], product[:, 0:n], -0.5, 1.5, ALU.mult, ALU.add)

        def ln_newton_5(dve, n, u):
            return dve.tensor_tensor(rstd[u % 2][:, 0:n], inverse_root[:, 0:n], factor[:, 0:n], ALU.mult)

        def ln_shift(dve, n, u, ago=2):
            made = dve.scalar_tensor_tensor(shift[:, 0:n], mean2[(u - ago) % 2][:, 0:n], -0.5,
                                            rstd[(u - ago + 1) % 2][:, 0:n], ALU.mult, ALU.mult)
            dve.drain()
            return made

        def ln_apply(eng, to, of, at, u, ago=2):
            for k in range(K):
                c = at * K + k
                last = eng.tensor_scalar(tiles(to)[k], tiles(of)[k], rstd[(u - ago + 1) % 2][:, c:c + 1],
                                         shift[:, c:c + 1], ALU.mult, ALU.add)
            return last

        def ln_apply_act(act, to, of, at, u, ago=2):
            for k in range(K):
                c = at * K + k
                last = act.activation(tiles(to)[k], tiles(of)[k], ACT.Identity, bias=shift[:, c:c + 1],
                                      scale=rstd[(u - ago + 1) % 2][:, c:c + 1])
            return last

        def turn(pe, to, of, width=D):
            for k in range(K):
                last = pe.transpose(to[0:width, k * P:(k + 1) * P], of[:, k * width:(k + 1) * width], ident[:])
            return last

        def natural_product(pe, to, turned, weight, bias_row):
            rows = weight.shape[0]
            pe.matmul(to[:], selector[:], bias_row[:], start=True, stop=False, skip_group_check=True)
            for k in range(K):
                last = pe.matmul(to[:, k * P:(k + 1) * P], turned[0:rows, k * P:(k + 1) * P], weight[:],
                                 start=False, stop=k == K - 1, skip_group_check=True)
            return last

        def engine_steps(name, *engines):
            return [sem(f"{name}_{e}_step") for e in engines or ("sp", "pool", "act", "dve", "pe")]

        def sp_program(sp, every, name, groups, loads, stores, steps, first_full, end_full):
            loaded = Tally(pair(f"{name}_loaded"), len(loads))
            stored = Tally(pair(f"{name}_stored"), len(stores))
            waited = sem(f"{name}_sp_waited")

            def start_loads(t, u):
                for use, ring, source in loads:
                    b = t + 2 - use
                    if not isinstance(t, int) or 0 <= b < groups:
                        to, of = source(ring[(u + 2 - use) % 4], b)
                        sp.dma_start(to, of).then_inc(loaded.add(u % 2), 16)

            def await_stores(u):
                if stores:
                    stored.wait(sp, (u - 1) % 2)
                    sp.sem_inc(waited, 1)

            def body(t, u):
                await_step(sp, t, every)
                sp.sem_inc(waited, 1)
                start_loads(t, u)
                if isinstance(t, int):
                    await_stores(u)
                for lag, ring, place in stores:
                    b = t - lag
                    if not isinstance(t, int) or 0 <= b < groups:
                        of, to = place(ring[(u - lag) % 4], b)
                        sp.dma_start(to, of).then_inc(stored.add(u % 2), 16)
                if not isinstance(t, int):
                    await_stores(u)
                loaded.wait(sp, (u - 1) % 2)
                sp.sem_inc(every[0], 1)

            start_loads(-2, -2)
            start_loads(-1, -1)
            loaded.wait(sp, 0)
            sp.sem_inc(every[0], 1)
            dma_steps(sp, body, (loaded, stored), steps, first_full, end_full)
            for parity in range(2):
                stored.wait(sp, parity)

        def pool_program(pool, every, name, groups, gathers, scatter, steps, first_full, end_full, norms=0,
                         put=None, add_index=None):
            indexed = sem(f"{name}_index_copied")
            checked = sem(f"{name}_index_checked")
            powered = sem(f"{name}_powered")
            gathered = Tally(pair(f"{name}_gathered"), K * len(gathers))
            scattered = Tally(pair(f"{name}_scattered"), K)
            per_step = len(gathers) + (add_index is None)
            at_lag, from_ring, to_table = scatter
            copies = [0, 0]

            def copy_indexes(t, u):
                if not isinstance(t, int) or t + 2 < groups:
                    for n, (ring, table, index) in enumerate(gathers):
                        pool.tensor_copy(index_now[u % 2][:, n * K:(n + 1) * K],
                                         index[:, bass.ds((t + 2) * K, K)]).then_inc(indexed, 1)
                        copies[0] += 1
                if add_index is None and (not isinstance(t, int) or 0 <= t - at_lag < groups):
                    pool.tensor_copy(put_now[u % 2][:], put(t - at_lag)).then_inc(indexed, 1)
                    copies[0] += 1

            def await_copies():
                if copies[0]:
                    pool.wait_ge(indexed, copies[0] + copies[1])
                    pool.sem_inc(checked, 1)

            def start_gathers(t, u):
                if isinstance(t, int) and not t + 2 < groups:
                    return
                for n, (ring, table, index) in enumerate(gathers):
                    for k in range(K):
                        at = n * K + k
                        pool.indirect_dma_start(
                            out=ring[(u + 2) % 4][:, k * P:(k + 1) * P], out_offset=None, in_=table,
                            in_offset=bass.IndirectOffsetOnAxis(ap=index_now[u % 2][:, at:at + 1], axis=0),
                            bounds_check=N - 1, oob_is_err=False).then_inc(gathered.add(u % 2), 16)

            def body(t, u):
                await_step(pool, t, every)
                await_copies()
                if norms:
                    ln_power(pool, norms * K, u).then_inc(powered, 1)
                start_gathers(t, u)
                b = t - at_lag
                if not isinstance(t, int) or 0 <= b < groups:
                    if add_index is None:
                        for k in range(K):
                            pool.indirect_dma_start(
                                out=to_table,
                                out_offset=bass.IndirectOffsetOnAxis(ap=put_now[u % 2][:, k:k + 1], axis=0),
                                in_=from_ring[(u - at_lag) % 4][:, k * P:(k + 1) * P], in_offset=None,
                                bounds_check=N - 1, oob_is_err=False).then_inc(scattered.add(u % 2), 16)
                    else:
                        scattered.wait(pool, (u - 1) % 2)
                        pool.sem_inc(checked, 1)
                        for k in range(K):
                            pool.indirect_dma_start(
                                out=to_table,
                                out_offset=bass.IndirectOffsetOnAxis(
                                    ap=add_index[(u - at_lag) % 4][:, k:k + 1], axis=0),
                                in_=from_ring[(u - at_lag) % 4][:, k * P:(k + 1) * P], in_offset=None,
                                compute_op=ALU.add).then_inc(scattered.add(u % 2), 16)
                gathered.wait(pool, (u - 1) % 2)
                scattered.wait(pool, (u - 1) % 2)
                pool.sem_inc(checked, 1)
                copy_indexes(t + 1, u + 1)
                if norms:
                    pool.wait_ge(powered, t + 1)
                pool.sem_inc(every[1], 1)

            copy_indexes(-2, -2)
            copy_indexes(-1, -1)
            await_copies()
            start_gathers(-2, -2)
            start_gathers(-1, -1)
            gathered.wait(pool, 0)
            copy_indexes(0, 0)
            pool.sem_inc(every[1], 1)
            for t in range(first_full):
                body(t, t % UNROLL)
            with pool.Fori(first_full, end_full - UNROLL + 1, UNROLL) as i:
                gathered.enter(i, first_full)
                scattered.enter(i, first_full)
                copies[1] = (i - first_full) * per_step
                for u in range(UNROLL):
                    body(i + u, u)
            trips = (end_full - first_full) // UNROLL
            gathered.leave(trips)
            scattered.leave(trips)
            copies[0] += (trips - 1) * UNROLL * per_step
            copies[1] = 0
            for t in range(end_full, steps):
                body(t, t % UNROLL)
            scattered.wait(pool, 0)
            scattered.wait(pool, 1)

        def put_at_last(b):
            return put_last[:, bass.ds(b * K, K)]

        def load_rows(table):
            return lambda buf, b: (buf, group_rows(table, b))

        def load_edges(table, width=D):
            return lambda buf, b: (buf[:, 0:K * width].rearrange("p (k f) -> p k f", k=K), edge_rows(table, b))

        def load_turned(table):
            return lambda buf, b: (buf, turned_group(table, b))

        def load_mask(m):
            return lambda buf, b: (buf, mask_group(m, b))

        def from_end(load):
            return lambda buf, b: load(buf, GROUPS - 1 - b)

        def full_range(groups, first_lag, last_ahead=3):
            return round_up(first_lag + 1, UNROLL), (groups - last_ahead) // UNROLL * UNROLL

        def pass_nodes_a():
            assert NODE_GROUPS == UNROLL * GROUPS
            new = Rings()
            at = new(2)
            halves = [(q, at[q // 2][:, q % 2 * G // 2:(q % 2 + 1) * G // 2]) for q in range(UNROLL)]
            x, x1, x2, y1 = (new(4) for _ in range(4))
            x1t, hr = (new(2) for _ in range(2))
            zeros = new(1)[0]
            b_x1t, b_h, b_lin = bank[0], bank[1], bank[2:4]
            every = engine_steps("na")
            sp_step, pool_step, act_step, dve_step, pe_step = every
            x1t_out, h_out = sem("na_x1_turned"), sem("na_h_done")
            rstd_ready, shift_ready = sem("na_rstd"), sem("na_shift")
            warm = sem("na_table_loaded")
            cleared, spare_cleared = sem("arena_cleared"), sem("spare_rows_cleared")
            indexed, checked = sem("na_index_copied"), sem("na_index_checked")
            gathered = Tally(pair("na_gathered"), 2)
            LAST = 7
            STEPS = NODE_GROUPS + LAST
            RANGE = full_range(NODE_GROUPS, LAST, 3)

            def place_half(quarter, step):
                q, buf = quarter
                return buf, edge_x[q // 2][bass.ds((step - q) * (2 * P // UNROLL) + q % 2 * P, P), :]

            with nc.Block() as block:
                @block.sync
                def _(sp):
                    sp.wait_ge(cleared, 2)
                    for i in range(2):
                        sp.dma_start(readout[N + i * G:N + (i + 1) * G, :].rearrange("(p k) f -> p (k f)", k=K),
                                     zeros).then_inc(spare_cleared, 16)
                    sp_program(sp, every, "na", NODE_GROUPS, [(0, x, load_rows(v["x"]))],
                               [(0, [zeros] * 4, load_rows(readout)), (2, x1, load_rows(tables[0])),
                                (7, x2, load_rows(tables[1])), (2, halves, place_half)], STEPS, *RANGE)
                    sp.wait_ge(spare_cleared, 32)

                @block.gpsimd
                def _(pool):
                    pool.memset(arena[:, RING // 2 * G:], 0.0).then_inc(cleared, 1)
                    pool.sem_inc(pool_step, 1)

                    copies = [0, 0]

                    def body(t, u):
                        await_step(pool, t, every)
                        ln_power(pool, 2 * K, u).then_inc(rstd_ready, 1)
                        if not isinstance(t, int) or t < NODE_GROUPS:
                            index, now = (src_index, dst_index)[u // 2], index_now[0][:, 2 * u:2 * u + 2]
                            pool.tensor_copy(now, index[:, bass.ds(t - u + u % 2 * 2, 2)]).then_inc(indexed, 1)
                            copies[0] += 1
                            pool.wait_ge(indexed, copies[0] + copies[1])
                            pool.sem_inc(checked, 1)
                            for k in range(2):
                                pool.indirect_dma_start(
                                    out=halves[u][1][:, k * P:(k + 1) * P], out_offset=None, in_=v["x"],
                                    in_offset=bass.IndirectOffsetOnAxis(ap=now[:, k:k + 1], axis=0),
                                    bounds_check=N - 1, oob_is_err=False).then_inc(gathered.add(u % 2), 16)
                        gathered.wait(pool, (u - 1) % 2)
                        pool.wait_ge(rstd_ready, t + 1)
                        pool.sem_inc(pool_step, 1)

                    pool.wait_ge(cleared, 2)
                    first, last = RANGE
                    for t in range(first):
                        body(t, t % UNROLL)
                    with pool.Fori(first, last - UNROLL + 1, UNROLL) as i:
                        gathered.enter(i, first)
                        copies[1] = i - first
                        for u in range(UNROLL):
                            body(i + u, u)
                    gathered.leave((last - first) // UNROLL)
                    copies[0] += last - first - UNROLL
                    copies[1] = 0
                    for t in range(last, STEPS):
                        body(t, t % UNROLL)

                @block.scalar
                def _(act):
                    act.sem_inc(act_step, 1)

                    def body(t, u):
                        await_step(act, t, every)
                        act.wait_ge(x1t_out, t + 1)
                        act.activation(x1t[u % 2], b_x1t[:], ACT.Copy)
                        act.wait_ge(shift_ready, t + 1)
                        ln_apply_act(act, x2[(u - 6) % 4], y1[(u - 6) % 4], 1, u, 1)
                        act.wait_ge(h_out, t + 1)
                        act.activation(hr[u % 2], b_h[:], ACT.Relu, scale=1.0 - OUT_SLOPE).then_inc(act_step, 1)

                    act.wait_ge(cleared, 2)
                    act.activation(x1t[0], zeros, ACT.Copy).then_inc(warm, 1)
                    act.wait_ge(warm, 1)
                    steps_of(act, body, STEPS)

                @block.vector
                def _(dve):
                    dve.memset(arena[:, 0:RING // 2 * G], 0.0).then_inc(cleared, 1)
                    dve.sem_inc(dve_step, 1)

                    def body(t, u):
                        await_step(dve, t, every)
                        ln_stats(dve, x[u % 4], 0)
                        ln_stats(dve, y1[(u - 5) % 4], 1)
                        dve.drain()
                        ln_means(dve, 2 * K, u)
                        dve.wait_ge(rstd_ready, t + 1)
                        ln_shift(dve, 2 * K, u, 1).then_inc(shift_ready, 1)
                        ln_gap_squared(dve, 2 * K)
                        ln_apply(dve, x1[(u - 1) % 4], x[(u - 1) % 4], 0, u, 1)
                        dve.drain()
                        ln_sum(dve, 2 * K, u)
                        dve.tensor_tensor(y1[(u - 4) % 4], hr[(u - 1) % 2], b_lin[(u - 1) % 2][:],
                                          ALU.add).then_inc(dve_step, 1)

                    dve.wait_ge(cleared, 2)
                    steps_of(dve, body, STEPS)

                @block.tensor
                def _(pe):
                    pe.sem_inc(pe_step, 1)

                    def body(t, u):
                        await_step(pe, t, every)
                        turn(pe, b_x1t, x1[(u - 2) % 4]).then_inc(x1t_out, 1)
                        natural_product(pe, b_h, x1t[(u - 1) % 2], w["Wl"], row["xl_bias"]).then_inc(h_out, 1)
                        natural_product(pe, b_lin[u % 2], x1t[(u - 1) % 2], w["Wlin"],
                                        row["xl_bias_lin"]).then_inc(pe_step, 1)

                    pe.wait_ge(cleared, 2)
                    steps_of(pe, body, STEPS)

        def pass_nodes_b():
            new = Rings()
            read, x2, y2, x3, x3b, y4, y5, res = (new(4) for _ in range(8))
            readt, act1, x3t, h3, n4 = (new(2) for _ in range(5))
            scaled_n = new(1)[0]
            b_readt, b_act1, b_prompt, b_x3t, b_u, b_delta = bank[0], bank[1], bank[2:4], bank[4], bank[5], bank[6:8]
            every = engine_steps("nb")
            sp_step, pool_step, act_step, dve_step, pe_step = every
            readt_out, act1_out, x3t_out, u_out = (
                sem(f"nb_{n}") for n in ("readout_turned", "prompt1_done", "x3_turned", "upd1_done"))
            shift_ready, scaled, summed, x3_read, root_ready, warm, waited = (
                sem(f"nb_{n}") for n in ("shift", "scaled", "summed", "x3_read", "root", "table_loaded",
                                         "pool_waited"))
            LAST = 16
            STEPS = NODE_GROUPS + LAST
            RANGE = full_range(NODE_GROUPS, LAST, 3)
            with nc.Block() as block:
                @block.sync
                def _(sp):
                    sp_program(sp, every, "nb", NODE_GROUPS,
                               [(0, read, load_rows(readout)), (3, x2, load_rows(tables[1]))],
                               [(6, x3, load_rows(tables[2])), (16, res, load_rows(out))], STEPS, *RANGE)

                @block.gpsimd
                def _(pool):
                    pool.sem_inc(pool_step, 1)

                    def body(t, u):
                        await_step(pool, t, every)
                        pool.tensor_tensor(scaled_n, n4[(u - 12) % 2], wide["gamma"][:], ALU.mult).then_inc(scaled, 1)
                        pool.wait_ge(scaled, t + 1)
                        pool.tensor_tensor(y5[(u - 12) % 4], scaled_n, x3b[(u - 12) % 4],
                                           ALU.add).then_inc(summed, 1)
                        pool.wait_ge(shift_ready, t + 1)
                        pool.wait_ge(x3_read, t + 1)
                        pool.sem_inc(waited, 1)
                        ln_apply(pool, x3[(u - 5) % 4], y2[(u - 5) % 4], 0, u)
                        pool.wait_ge(summed, t + 1)
                        pool.tensor_tensor(x3b[(u - 8) % 4], x3[(u - 8) % 4], wide["beta"][:],
                                           ALU.add).then_inc(pool_step, 1)

                    steps_of(pool, body, STEPS)

                @block.scalar
                def _(act):
                    act.sem_inc(act_step, 1)

                    def body(t, u):
                        await_step(act, t, every)
                        ln_root(act, 3 * K, u, root_ready)
                        act.wait_ge(shift_ready, t + 1)
                        ln_apply_act(act, n4[(u - 11) % 2], y4[(u - 11) % 4], 1, u)
                        act.wait_ge(readt_out, t + 1)
                        act.activation(readt[u % 2], b_readt[:], ACT.Copy)
                        act.wait_ge(x3t_out, t + 1)
                        act.activation(x3t[u % 2], b_x3t[:], ACT.Copy)
                        act.wait_ge(act1_out, t + 1)
                        act.activation(act1[u % 2][0:H, :], b_act1[0:H, :], ACT.Relu, bias=col["b1"][:])
                        act.wait_ge(u_out, t + 1)
                        act.activation(h3[u % 2], b_u[:], ACT.Relu, bias=col["upd_c_node"][:])
                        ln_apply_act(act, res[(u - 15) % 4], y5[(u - 15) % 4], 2, u).then_inc(act_step, 1)

                    act.activation(root[:], var[0][:], ACT.Sqrt).then_inc(warm, 1)
                    act.wait_ge(warm, 1)
                    steps_of(act, body, STEPS)

                @block.vector
                def _(dve):
                    dve.sem_inc(dve_step, 1)

                    def body(t, u):
                        await_step(dve, t, every)
                        ln_shift(dve, 3 * K, u).then_inc(shift_ready, 1)
                        dve.scalar_tensor_tensor(y2[(u - 3) % 4], x2[(u - 3) % 4], 2.0, b_prompt[(u - 1) % 2][:],
                                                 ALU.mult, ALU.add)
                        dve.tensor_tensor(y4[(u - 9) % 4], x3[(u - 9) % 4], b_delta[(u - 1) % 2][:],
                                          ALU.add).then_inc(x3_read, 1)
                        ln_newton_1(dve, 3 * K, t, root_ready)
                        ln_stats(dve, y5[(u - 13) % 4], 2)
                        dve.drain()
                        ln_newton_2(dve, 3 * K)
                        ln_stats(dve, y2[(u - 3) % 4], 0)
                        ln_stats(dve, y4[(u - 9) % 4], 1)
                        dve.drain()
                        ln_newton_3(dve, 3 * K, u)
                        ln_means(dve, 3 * K, u)
                        dve.drain()
                        ln_newton_4(dve, 3 * K)
                        ln_gap_squared(dve, 3 * K)
                        dve.drain()
                        ln_newton_5(dve, 3 * K, u)
                        ln_sum(dve, 3 * K, u).then_inc(dve_step, 1)

                    steps_of(dve, body, STEPS)

                @block.tensor
                def _(pe):
                    pe.sem_inc(pe_step, 1)

                    def body(t, u):
                        await_step(pe, t, every)
                        turn(pe, b_readt, read[u % 4]).then_inc(readt_out, 1)
                        turn(pe, b_x3t, x3[(u - 6) % 4]).then_inc(x3t_out, 1)
                        pe.matmul(b_act1[0:H, :], w["W1"][:], readt[(u - 1) % 2], start=True,
                                  stop=True).then_inc(act1_out, 1)
                        pe.matmul(b_u[:], w["upd1x"][:], x3t[(u - 1) % 2], start=True,
                                  stop=True).then_inc(u_out, 1)
                        natural_product(pe, b_prompt[u % 2], act1[(u - 1) % 2], w["W2"], row["b2"])
                        natural_product(pe, b_delta[u % 2], h3[(u - 1) % 2], w["upd2"],
                                        row["upd_b2"]).then_inc(pe_step, 1)

                    steps_of(pe, body, STEPS)

        def pass_l0():
            new = Rings()
            xs, xd, run, d1, d1t, yn, is_first = (new(4) for _ in range(7))
            xst, xdt, own, yt = (new(2) for _ in range(4))
            b_xs, b_xd, b_nbr, b_self, b_y, b_d1 = bank[0], bank[1], bank[2:4], bank[4], bank[5], bank[6]
            every = engine_steps("l0")
            sp_step, pool_step, act_step, dve_step, pe_step = every
            xs_out, xd_out, self_out, y_out, d1_out = (
                sem(f"l0_{n}") for n in ("src_turned", "dst_turned", "self_done", "sum_turned", "state_turned"))
            STEPS = GROUPS + 8
            RANGE = full_range(GROUPS, 8)
            with nc.Block() as block:
                @block.sync
                def _(sp):
                    sp_program(sp, every, "l0", GROUPS,
                               [(0, xs, from_end(load_edge_x(edge_x[0]))), (0, xd, from_end(load_edge_x(edge_x[1]))),
                                (2, restart, from_end(load_mask("restart_back"))),
                                (7, is_first, from_end(load_mask("is_first")))],
                               [(8, d1t, from_end(load_turned(dst1_turned)))], STEPS, *RANGE)

                @block.gpsimd
                def _(pool):
                    pool_program(pool, every, "l0", GROUPS, [],
                                 (7, d1, tables[0]), STEPS, *RANGE, 1,
                                 put=lambda b: put_first[:, bass.ds((GROUPS - 1 - b) * K, K)])

                @block.scalar
                def _(act):
                    act.sem_inc(act_step, 1)

                    def body(t, u):
                        await_step(act, t, every)
                        act.wait_ge(xs_out, t + 1)
                        act.activation(xst[u % 2], b_xs[:], ACT.Copy)
                        act.wait_ge(xd_out, t + 1)
                        act.activation(xdt[u % 2], b_xd[:], ACT.Copy)
                        act.wait_ge(self_out, t + 1)
                        act.activation(own[u % 2], b_self[:], ACT.Identity, bias=col["L0_b"][:])
                        act.wait_ge(y_out, t + 1)
                        act.activation(yn[(u - 3) % 4], b_y[:], ACT.Copy).then_inc(act_step, 1)

                    steps_of(act, body, STEPS)

                @block.vector
                def _(dve):
                    dve.sem_inc(dve_step, 1)

                    def body(t, u):
                        await_step(dve, t, every)
                        dve.tensor_tensor_scan(run[(u - 2) % 4][:, ::-1], restart[(u - 2) % 4][:, ::-1],
                                               b_nbr[(u - 1) % 2][:, ::-1], run[(u - 3) % 4][:, 0:1],
                                               ALU.add, ALU.max)
                        ln_stats(dve, yn[(u - 4) % 4], 0)
                        dve.drain()
                        dve.tensor_tensor(yt[u % 2], run[(u - 2) % 4], own[(u - 1) % 2], ALU.add)
                        ln_shift(dve, K, u)
                        ln_apply(dve, d1[(u - 6) % 4], yn[(u - 6) % 4], 0, u)
                        dve.wait_ge(d1_out, t + 1)
                        dve.tensor_tensor(d1t[(u - 7) % 4], b_d1[:], is_first[(u - 7) % 4], ALU.mult)
                        ln_variance(dve, K, u).then_inc(dve_step, 1)

                    steps_of(dve, body, STEPS)

                @block.tensor
                def _(pe):
                    pe.sem_inc(pe_step, 1)

                    def body(t, u):
                        await_step(pe, t, every)
                        turn(pe, b_xs, xs[u % 4]).then_inc(xs_out, 1)
                        turn(pe, b_xd, xd[u % 4]).then_inc(xd_out, 1)
                        pe.matmul(b_self[:], w["W_self"][:], xdt[(u - 1) % 2], start=True,
                                  stop=True).then_inc(self_out, 1)
                        turn(pe, b_y, yt[(u - 1) % 2]).then_inc(y_out, 1)
                        turn(pe, b_d1, d1[(u - 7) % 4]).then_inc(d1_out, 1)
                        pe.matmul(b_nbr[u % 2][:], w["W_nbr"][:], xst[(u - 1) % 2], start=True,
                                  stop=True).then_inc(pe_step, 1)

                    steps_of(pe, body, STEPS)

        def pass_l1():
            new = Rings()
            xs, xst, goes_on, d1_first, d1t, d1t_late, xl, xl_own, d2, yt, yn = (new(4) for _ in range(11))
            u_relu, u_lin, v_relu, v_lin, own_logit, z, o = (new(2) for _ in range(7))
            z_all = new(2)
            inverse_z = [sb(f"inverse_z{i}", [P, K]) for i in range(2)]
            at = new(6)
            weight = [at[0:3], at[3:6]]
            temp = new(3)
            at = new(6)
            below = [at[0:3], at[3:6]]
            b_xs, b_u, b_v, b_xl, b_own, b_logit, b_own_logit = (
                bank[0], bank[1], bank[2], bank[3], bank[4], bank[5:7], bank[7])
            every = engine_steps("l1")
            sp_step, pool_step, act_step, dve_step, pe_step = every
            xs_out, u_out, v_out, xl_out, own_out, own_logit_out, y_out, z_out, b0_free, v_free = (
                sem(f"l1_{n}") for n in ("src_turned", "u_done", "v_done", "xl_done", "own_done", "own_logit_done",
                                         "sum_turned", "z_turned", "src_copied", "v_used"))
            shift_ready = sem("l1_shift")
            STEPS = GROUPS + 11
            RANGE = full_range(GROUPS, 11)
            to_late = [(d1t[i], d1t_late[i]) for i in range(4)]
            with nc.Block() as block:
                @block.sync
                def _(sp):
                    sp_program(sp, every, "l1", GROUPS,
                               [(0, d1_first, load_turned(dst1_turned)), (0, goes_on, load_mask("goes_on")),
                                (3, restart, load_mask("restart"))],
                               [(2, to_late, lambda pair, b: pair)], STEPS, *RANGE)

                @block.gpsimd
                def _(pool):
                    pool_program(pool, every, "l1", GROUPS, [(xs, tables[0], src_index)], (11, d2, tables[1]),
                                 STEPS, *RANGE, 1, put=put_at_last)

                @block.scalar
                def _(act):
                    act.sem_inc(act_step, 1)

                    def body(t, u):
                        await_step(act, t, every)
                        act.wait_ge(v_out, t + 1)
                        act.activation(v_relu[u % 2], b_v[:], ACT.Relu, bias=col["bl_br"][:])
                        act.activation(v_lin[u % 2], b_v[:], ACT.Identity, bias=col["bl_br"][:]).then_inc(v_free, 1)
                        act.wait_ge(xs_out, t + 1)
                        act.activation(xst[u % 4], b_xs[:], ACT.Copy).then_inc(b0_free, 1)
                        act.wait_ge(shift_ready, t + 1)
                        ln_apply_act(act, d2[(u - 10) % 4], yn[(u - 10) % 4], 0, u)
                        act.wait_ge(u_out, t + 1)
                        act.activation(u_relu[u % 2], b_u[:], ACT.Relu, bias=col["bl_br"][:])
                        act.activation(u_lin[u % 2], b_u[:], ACT.Identity, bias=col["bl_br"][:])
                        act.wait_ge(y_out, t + 1)
                        for k in range(K):
                            act.activation(tiles(yn[(u - 7) % 4])[k], tiles(b_xs)[k], ACT.Copy,
                                           scale=inverse_z[(u - 1) % 2][:, k:k + 1])
                        for n in range(3):
                            act.activation(weight[u % 2][n], below[(u - 1) % 2][n], ACT.Exp)
                        act.wait_ge(xl_out, t + 1)
                        act.activation(xl[(u - 2) % 4], b_xl[:], ACT.Identity, bias=col["bl_bias"][:])
                        act.wait_ge(own_out, t + 1)
                        act.activation(xl_own[(u - 2) % 4], b_own[:], ACT.Identity, bias=col["bl_bias"][:])
                        act.wait_ge(own_logit_out, t + 1)
                        act.activation(own_logit[u % 2], b_own_logit[:], ACT.Copy).then_inc(act_step, 1)

                    steps_of(act, body, STEPS)

                @block.vector
                def _(dve):
                    for three in weight:
                        for buf in three:
                            dve.memset(buf, 1.0)
                    for buf in below[0] + below[1] + z + o + d1t:
                        dve.memset(buf, 0.0)
                    for i in range(2):
                        dve.memset(z_all[i], 1.0)
                        dve.memset(inverse_z[i][:], 1.0)
                    dve.memset(max_run[0][:], 0.0)
                    dve.memset(max_run[1][:], 0.0).then_inc(dve_step, 1)

                    def body(t, u):
                        await_step(dve, t, every)
                        logit, own = b_logit[(u - 1) % 2], own_logit[(u - 1) % 2]
                        m, before = max_run[u % 2], max_run[(u - 1) % 2]
                        d = below[u % 2]
                        ln_shift(dve, K, u).then_inc(shift_ready, 1)
                        shrink, p, p_own = weight[(u - 1) % 2]
                        dve.tensor_tensor(temp[0], logit[:], own, ALU.max)
                        dve.tensor_copy(m[:, 0:1], before[:, G:G + 1])
                        dve.tensor_tensor_scan(d1t[u % 4], goes_on[u % 4], d1_first[u % 4],
                                               d1t[(u - 1) % 4][:, G - 1:G], ALU.mult, ALU.add)
                        dve.tensor_tensor(temp[1], p, xl[(u - 5) % 4], ALU.mult)
                        dve.tensor_tensor(temp[2], p_own, xl_own[(u - 5) % 4], ALU.mult)
                        dve.tensor_tensor_scan(z[u % 2], shrink, p, z[(u - 1) % 2][:, G - 1:G], ALU.mult, ALU.add)
                        dve.drain()
                        dve.tensor_tensor_scan(m[:, 1:G + 1], restart[(u - 3) % 4], temp[0], before[:, G:G + 1],
                                               ALU.add, ALU.max)
                        dve.tensor_tensor_scan(o[u % 2], shrink, temp[1], o[(u - 1) % 2][:, G - 1:G], ALU.mult, ALU.add)
                        dve.tensor_tensor(z_all[u % 2], z[u % 2], p_own, ALU.add)
                        dve.drain()
                        dve.tensor_tensor(d[0], m[:, 0:G], restart[(u - 3) % 4], ALU.add)
                        dve.tensor_tensor(d[1], logit[:], m[:, 1:G + 1], ALU.subtract)
                        dve.tensor_tensor(d[2], own, m[:, 1:G + 1], ALU.subtract)
                        dve.tensor_tensor(temp[2], temp[2], o[u % 2], ALU.add)
                        dve.tensor_tensor(temp[1], z_all[u % 2], d1t_late[(u - 5) % 4], ALU.mult)
                        dve.drain()
                        dve.tensor_tensor(d[0], d[0], m[:, 1:G + 1], ALU.subtract)
                        dve.scalar_tensor_tensor(temp[2], temp[2], OUT_SLOPE, temp[2], ALU.mult, ALU.max)
                        ln_stats(dve, yn[(u - 8) % 4], 0)
                        dve.drain()
                        dve.tensor_tensor(yt[(u - 5) % 4], temp[2], temp[1], ALU.add)
                        dve.wait_ge(z_out, t + 1)
                        dve.reciprocal(inverse_z[u % 2][:], b_v[:, 0:K])
                        ln_variance(dve, K, u).then_inc(dve_step, 1)

                    steps_of(dve, body, STEPS)

                @block.tensor
                def _(pe):
                    pe.sem_inc(pe_step, 1)

                    def product(to, parts):
                        for n, (weights, turned) in enumerate(parts):
                            last = pe.matmul(to[:], w[weights][:], turned, start=n == 0, stop=n == len(parts) - 1)
                        return last

                    def body(t, u):
                        await_step(pe, t, every)
                        product(b_v, (("Wlr", d1t[(u - 1) % 4]),)).then_inc(v_out, 1)
                        turn(pe, b_xs, xs[u % 4]).then_inc(xs_out, 1)
                        product(b_u, (("Wl", xst[(u - 1) % 4]), ("Wr", d1t[(u - 1) % 4]))).then_inc(u_out, 1)
                        pe.wait_ge(v_free, t + 1)
                        for k in range(K):
                            last = pe.matmul(b_v[:, k:k + 1], tiles(z_all[(u - 1) % 2])[k][0:1, :], one[:],
                                             start=True, stop=True)
                        last.then_inc(z_out, 1)
                        pe.wait_ge(b0_free, t + 1)
                        turn(pe, b_xs, yt[(u - 7) % 4]).then_inc(y_out, 1)
                        product(b_xl, (("Wl", xst[(u - 2) % 4]),)).then_inc(xl_out, 1)
                        product(b_own, (("Wl", d1t[(u - 2) % 4]),)).then_inc(own_out, 1)
                        product(b_own_logit, (("att_relu", v_relu[(u - 1) % 2]),
                                              ("att_lin", v_lin[(u - 1) % 2]))).then_inc(own_logit_out, 1)
                        product(b_logit[u % 2], (("att_relu", u_relu[(u - 1) % 2]),
                                                  ("att_lin", u_lin[(u - 1) % 2]))).then_inc(pe_step, 1)

                    steps_of(pe, body, STEPS)

        def pass_l2():
            new = Rings()
            xd, xd_late, source, summed = (new(4) for _ in range(4))
            xdt, hidden, msg = (new(2) for _ in range(3))
            at = new(2 * K)
            same = [at[0:K], at[K:2 * K]]
            unused = new(1)[0]
            b_xd, b_hidden, b_gate, b_sum = bank[0], bank[1], bank[2], bank[3]
            every = engine_steps("l2")
            sp_step, pool_step, act_step, dve_step, pe_step = every
            xd_out, hidden_out, gate_out, sum_out = (
                sem(f"l2_{n}") for n in ("dst_turned", "hidden_done", "gate_done", "sum_done"))
            src_copied = sem("l2_src_copied")
            STEPS = GROUPS + 5
            RANGE = full_range(GROUPS, 5)
            with nc.Block() as block:
                @block.sync
                def _(sp):
                    sp_program(sp, every, "l2", GROUPS, [(3, source, load_mask("source"))], [], STEPS, *RANGE)

                @block.gpsimd
                def _(pool):
                    pool_program(pool, every, "l2", GROUPS, [(xd, tables[1], dst_index)], (5, summed, readout),
                                 STEPS, *RANGE, add_index=add_now)

                @block.scalar
                def _(act):
                    act.sem_inc(act_step, 1)

                    def body(t, u):
                        await_step(act, t, every)
                        act.activation(xd_late[(u - 1) % 4], xd[(u - 1) % 4], ACT.Copy)
                        act.wait_ge(xd_out, t + 1)
                        act.activation(xdt[u % 2], b_xd[:], ACT.Copy)
                        act.wait_ge(hidden_out, t + 1)
                        act.activation(hidden[u % 2][0:H, :], b_hidden[0:H, :], ACT.Tanh, bias=col["b_sim"][:])
                        act.wait_ge(gate_out, t + 1)
                        act.activation(gate[u % 2][:], b_gate[:, 0:K], ACT.Sigmoid, bias=col["b_vec"][:])
                        act.wait_ge(sum_out, t + 1)
                        act.activation(summed[(u - 4) % 4], b_sum[:], ACT.Copy).then_inc(act_step, 1)

                    steps_of(act, body, STEPS)

                @block.vector
                def _(dve):
                    dve.sem_inc(dve_step, 1)

                    def body(t, u):
                        await_step(dve, t, every)
                        last_group = GROUPS - 1
                        b = (min(max(t - 3, 0), last_group) if isinstance(t, int) else t - 3)
                        dve.tensor_copy(src_now[:], src_value[:, bass.ds(b * K, K)])
                        for k in range(K):
                            dve.tensor_scalar(tiles(msg[u % 2])[k], tiles(xd_late[(u - 3) % 4])[k],
                                              gate[(u - 1) % 2][:, k:k + 1], None, ALU.mult)
                        dve.drain()
                        for k in range(K):
                            dve.tensor_scalar(same[u % 2][k], source[(u - 3) % 4], src_now[:, k:k + 1], None,
                                              ALU.is_equal)
                        dve.drain()
                        for k in range(K):
                            dve.scalar_tensor_tensor(unused, same[u % 2][k], 1.0, earlier[:, k, :], ALU.mult,
                                                     ALU.mult, accum_out=repeats[:, k:k + 1])
                            dve.drain()
                        dve.tensor_scalar(repeats[:], repeats[:], 0.0, None, ALU.is_gt)
                        dve.tensor_tensor(detour[:], spare_row[:], src_now[:], ALU.subtract)
                        dve.drain()
                        dve.tensor_tensor(detour[:], detour[:], repeats[:], ALU.mult)
                        dve.drain()
                        dve.tensor_tensor(add_now[(u - 3) % 4][:], detour[:], src_now[:], ALU.add).then_inc(dve_step, 1)

                    dma_steps(dve, body, (), STEPS, *RANGE)

                @block.tensor
                def _(pe):
                    pe.sem_inc(pe_step, 1)

                    def body(t, u):
                        await_step(pe, t, every)
                        turn(pe, b_xd, xd[u % 4]).then_inc(xd_out, 1)
                        pe.matmul(b_hidden[0:H, :], w["W_sim"][:], xdt[(u - 1) % 2], start=True,
                                  stop=True).then_inc(hidden_out, 1)
                        for k in range(K):
                            last = pe.matmul(b_gate[:, k:k + 1], hidden[(u - 1) % 2][0:H, k * P:(k + 1) * P],
                                             col["w_vec"][:], start=True, stop=True)
                        last.then_inc(gate_out, 1)
                        for m in range(K):
                            for k in range(K):
                                last = pe.matmul(tiles(b_sum)[m], tiles(same[(u - 1) % 2][k])[m],
                                                 tiles(msg[(u - 1) % 2])[k], start=k == 0, stop=k == K - 1)
                        last.then_inc(sum_out, 1)
                        pe.wait_ge(sum_out, t + 1)
                        pe.sem_inc(pe_step, 1)

                    steps_of(pe, body, STEPS)

        def pass_l3():
            new = Rings()
            xs, attr, d3, goes_on, d3_late, d3t, d3b, y4, y5, res = (new(4) for _ in range(10))
            xst, attrt, m1, total, degree, mean, h, n4 = (new(2) for _ in range(8))
            ones, scaled, count = (new(1)[0] for _ in range(3))
            b_xs, b_msg1, b_d3, b_msg, b_u, b_delta = bank[0], bank[1], bank[2], bank[3:5], bank[5], bank[6:8]
            every = engine_steps("l3")
            sp_step, pool_step, act_step, dve_step, pe_step = every
            xs_out, attr_out, attr_free, d3_out, m1_out, u_out = (
                sem(f"l3_{n}") for n in ("src_turned", "attr_turned", "attr_copied", "dst_turned", "msg1_done",
                                         "upd1_done"))
            shift_ready, root_ready, warm = sem("l3_shift"), sem("l3_root"), sem("l3_table_loaded")
            STEPS = GROUPS + 12
            RANGE = full_range(GROUPS, 12)
            with nc.Block() as block:
                @block.sync
                def _(sp):
                    sp_program(sp, every, "l3", GROUPS,
                               [(0, attr, load_edges(v["edge_attr_64"], H)), (3, goes_on, load_mask("goes_on")),
                                (6, d3_late, load_edges(dst3))],
                               [(0, d3, load_edges(dst3))], STEPS, *RANGE)

                @block.gpsimd
                def _(pool):
                    pool_program(pool, every, "l3", GROUPS, [(xs, tables[2], src_index), (d3, tables[2], dst_index)],
                                 (12, res, out), STEPS, *RANGE, put=put_at_last)

                @block.scalar
                def _(act):
                    act.sem_inc(act_step, 1)

                    def body(t, u):
                        await_step(act, t, every)
                        ln_root(act, 2 * K, u, root_ready)
                        act.wait_ge(xs_out, t + 1)
                        act.activation(xst[u % 2], b_xs[:], ACT.Copy)
                        act.wait_ge(attr_out, t + 1)
                        act.activation(attrt[u % 2][0:H, :], b_msg1[0:H, :], ACT.Copy).then_inc(attr_free, 1)
                        act.wait_ge(d3_out, t + 1)
                        act.activation(d3t[(u - 1) % 4], b_d3[:], ACT.Copy)
                        act.wait_ge(u_out, t + 1)
                        act.activation(h[u % 2], b_u[:], ACT.Relu, bias=col["upd_c_edge"][:])
                        act.wait_ge(m1_out, t + 1)
                        act.activation(m1[u % 2], b_msg1[:], ACT.Relu, bias=col["msg_c"][:])
                        act.wait_ge(shift_ready, t + 1)
                        ln_apply_act(act, n4[(u - 8) % 2], y4[(u - 8) % 4], 0, u)
                        ln_apply_act(act, res[(u - 11) % 4], y5[(u - 11) % 4], 1, u).then_inc(act_step, 1)

                    act.activation(root[:], var[0][:], ACT.Sqrt).then_inc(warm, 1)
                    act.wait_ge(warm, 1)
                    steps_of(act, body, STEPS)

                @block.vector
                def _(dve):
                    dve.memset(ones, 1.0).then_inc(dve_step, 1)

                    def body(t, u):
                        await_step(dve, t, every)
                        dve.tensor_tensor_scan(total[u % 2], goes_on[(u - 3) % 4], b_msg[(u - 1) % 2][:],
                                               total[(u - 1) % 2][:, G - 1:G], ALU.mult, ALU.add)
                        dve.tensor_tensor_scan(degree[u % 2], goes_on[(u - 3) % 4], ones,
                                               degree[(u - 1) % 2][:, G - 1:G], ALU.mult, ALU.add)
                        ln_shift(dve, 2 * K, u).then_inc(shift_ready, 1)
                        dve.tensor_tensor(y4[(u - 6) % 4], d3_late[(u - 6) % 4], b_delta[(u - 1) % 2][:], ALU.add)
                        dve.tensor_tensor(d3b[(u - 6) % 4], d3_late[(u - 6) % 4], wide["beta"][:], ALU.add)
                        ln_newton_1(dve, 2 * K, t, root_ready)
                        dve.drain()
                        dve.tensor_scalar(count, degree[u % 2], 1.0, None, ALU.max)
                        dve.tensor_tensor(scaled, n4[(u - 9) % 2], wide["gamma"][:], ALU.mult)
                        ln_newton_2(dve, 2 * K)
                        dve.drain()
                        dve.reciprocal(count, count)
                        ln_newton_3(dve, 2 * K, u)
                        dve.tensor_tensor(y5[(u - 9) % 4], scaled, d3b[(u - 9) % 4], ALU.add)
                        dve.drain()
                        ln_newton_4(dve, 2 * K)
                        dve.tensor_tensor(mean[u % 2], total[u % 2], count, ALU.mult)
                        dve.drain()
                        ln_newton_5(dve, 2 * K, u)
                        ln_stats(dve, y4[(u - 6) % 4], 0)
                        ln_stats(dve, y5[(u - 9) % 4], 1)
                        ln_variance(dve, 2 * K, u).then_inc(dve_step, 1)

                    steps_of(dve, body, STEPS)

                @block.tensor
                def _(pe):
                    pe.sem_inc(pe_step, 1)

                    def body(t, u):
                        await_step(pe, t, every)
                        turn(pe, b_xs, xs[u % 4]).then_inc(xs_out, 1)
                        turn(pe, b_msg1, attr[u % 4], H).then_inc(attr_out, 1)
                        turn(pe, b_d3, d3[(u - 1) % 4]).then_inc(d3_out, 1)
                        pe.matmul(b_u[:], w["upd1x"][:], d3t[(u - 4) % 4], start=True, stop=False)
                        pe.matmul(b_u[:], w["upd1a"][:], mean[(u - 1) % 2], start=False, stop=True).then_inc(u_out, 1)
                        pe.wait_ge(attr_free, t + 1)
                        pe.matmul(b_msg1[:], w["msg1x"][:], xst[(u - 1) % 2], start=True, stop=False)
                        pe.matmul(b_msg1[:], w["msg1e"][:], attrt[(u - 1) % 2][0:H, :], start=False,
                                  stop=True).then_inc(m1_out, 1)
                        pe.matmul(b_msg[u % 2][:], w["msg2"][:], m1[(u - 1) % 2], start=True, stop=True)
                        natural_product(pe, b_delta[u % 2], h[(u - 1) % 2], w["upd2"],
                                        row["upd_b2"]).then_inc(pe_step, 1)

                    steps_of(pe, body, STEPS)

        prepare()
        pass_nodes_a()
        pass_l0()
        pass_l1()
        pass_l2()
        pass_nodes_b()
        pass_l3()


_N, _D = 100000, 128
_OUTS = [((_N, _D), 'float32')]


def kernel(**inputs):
    import numpy as _np
    import concourse.bacc as _bacc
    from concourse import mybir as _mybir
    from concourse.bass_utils import run_bass_kernel_spmd as _run

    group = 512
    src, dst = _np.asarray(inputs["src"]), _np.asarray(inputs["dst"])
    edges = src.shape[0]
    groups = -(-edges // group)
    pad = groups * group - edges
    src_pad = _np.concatenate([src, _np.full(pad, _N + group, src.dtype)])
    dst_pad = _np.concatenate([_np.full(1, -1, dst.dtype), dst, _np.full(pad + 1, _N, dst.dtype)])
    laid = {
        "src_tiles": src_pad.reshape(-1, 128).T,
        "src_rows": src_pad.reshape(-1, group),
        "dst_tiles": dst_pad[1:-1].reshape(-1, 128).T,
        "dst_before_tiles": dst_pad[:-2].reshape(-1, 128).T,
        "dst_next_tiles": dst_pad[2:].reshape(-1, 128).T,
        "dst_windows": _np.lib.stride_tricks.sliding_window_view(dst_pad, group + 2)[::group],
    }
    for name, a in inputs.items():
        if name in ("src", "dst", "edge_attr_16"):
            continue
        a = _np.asarray(a)
        if name == "edge_attr_64":
            a = _np.concatenate([a, _np.zeros((pad, a.shape[1]), a.dtype)])
        laid[name] = a

    nc = _bacc.Bacc("TRN2", target_bir_lowering=False, num_devices=1)
    arrays, views = {}, {}
    for name, a in laid.items():
        a = _np.ascontiguousarray(a)
        arrays[f"in_{name}_dram"] = a
        views[name] = nc.dram_tensor(f"in_{name}_dram", a.shape, _mybir.dt.from_np(a.dtype), kind="ExternalInput").ap()
    outs = [nc.dram_tensor(f"out_{i}_dram", shape, _mybir.dt.from_np(_np.dtype(dtype)), kind="ExternalOutput").ap()
            for i, (shape, dtype) in enumerate(_OUTS)]
    build(nc, views, outs[0])
    r = _run(nc, [arrays], core_ids=[0])
    return r.results[0]["out_0_dram"]
```
